# Optimizing a Trainium2 kernel written in Bass

```python
import numpy as np
import jax
import jax.numpy as jnp

def _softmax(x, axis=-1):
    return jax.nn.softmax(x, axis=axis)

def _gelu(x):
    return jax.nn.gelu(x, approximate=True)

def _silu(x):
    return jax.nn.silu(x)

def _sigmoid(x):
    return jax.nn.sigmoid(x)

def _layernorm(x, axis=-1, eps=1e-05):
    m = jnp.mean(x, axis=axis, keepdims=True)
    v = jnp.var(x, axis=axis, keepdims=True)
    return (x - m) / jnp.sqrt(v + eps)

def _scatter_add(tgt, idx, src, axis=0):
    return tgt.at[idx].add(src)

def _segment_sum(src, seg, n):
    return jax.ops.segment_sum(src, seg, n)
kernel_name = 'mk_early_fusion_embed_d1_tok_img768_r4_d04811'

def setup_inputs(seed: int=0):
    np.random.seed(seed)
    _w = jnp.asarray

    def _rec_inputs():
        import jax
        import jax.numpy as jnp
        _rk = jax.random.key(seed)
        x = -0.000147625 + 0.999875 * jax.random.normal(jax.random.fold_in(_rk, 1), (32, 3, 224, 224), jnp.float32)
        x_txt = jax.random.randint(jax.random.fold_in(_rk, 51), (32, 128), 0, 50257, jnp.int32)
        itok_BS_0_4095 = jax.random.randint(jax.random.fold_in(_rk, 71), (32, 128), 0, 1024, jnp.int32)
        return (x, x_txt, itok_BS_0_4095)
    x, x_txt, itok_BS_0_4095 = _rec_inputs()

    def _L0_tok_setup():
        import jax, jax.numpy as jnp
        import numpy as np
        EPS = 1e-05
        P = 16

        def _layernorm(x, gamma, beta):
            mu = jnp.mean(x, axis=-1, keepdims=True)
            var = jnp.mean(jnp.square(x - mu), axis=-1, keepdims=True)
            return (x - mu) * jax.lax.rsqrt(var + EPS) * gamma + beta
        key = jax.random.key(seed)
        ks = jax.random.split(key, 9)
        B, C, H, W = (64, 3, 224, 224)
        dim = 192
        patch_dim = C * P * P
        num_patches = (H // P) ** 2
        img = jax.random.normal(ks[0], (B, C, H, W), dtype=jnp.float32)
        ln1_g = jnp.ones((patch_dim,), jnp.float32)
        ln1_b = jnp.zeros((patch_dim,), jnp.float32)
        W_proj = jax.random.normal(ks[1], (patch_dim, dim), jnp.float32) / np.sqrt(patch_dim)
        b_proj = jnp.zeros((dim,), jnp.float32)
        ln2_g = jnp.ones((dim,), jnp.float32)
        ln2_b = jnp.zeros((dim,), jnp.float32)
        pos_embedding = jax.random.normal(ks[2], (1, num_patches + 1, dim), jnp.float32)
        cls_token = jax.random.normal(ks[3], (1, 1, dim), jnp.float32)
        return {'img': img, 'ln1_g': ln1_g, 'ln1_b': ln1_b, 'W_proj': W_proj, 'b_proj': b_proj, 'ln2_g': ln2_g, 'ln2_b': ln2_b, 'pos_embedding': pos_embedding, 'cls_token': cls_token}
    _L0_tok_all = _L0_tok_setup()
    _L0_tok_in = {k: v for k, v in _L0_tok_all.items() if k in ('ln1_g', 'ln1_b', 'W_proj', 'b_proj', 'ln2_g', 'ln2_b', 'pos_embedding', 'cls_token')}
    del _L0_tok_all

    def _L0_txt_setup():
        import jax, jax.numpy as jnp
        import numpy as np
        V = 50257
        NV = 1024
        NF = 64
        NG = 64
        B, S = (8, 2048)
        H, D = (64, 192)
        SPECIAL = (0, 1, 2)
        IN_DIM = 5 + NF + 4 + 12

        def _forward(token_ids, var_ids, token_has_int, token_signed_norm, token_log_norm, token_is_zero, token_is_one, token_is_pow2, var_family_onehot, var_family_id, var_outer_norm, var_inner_norm, var_has_outer, var_has_inner, var_group_id, ln_g, ln_b, W1, b1, W2, b2, scale):
            bsz, seq_len = token_ids.shape
            dtype = token_log_norm.dtype
            denom = float(max(seq_len - 1, 1))
            has_int = token_has_int[token_ids]
            signed = token_signed_norm[token_ids]
            tlog = token_log_norm[token_ids]
            is_zero = token_is_zero[token_ids]
            is_one = token_is_one[token_ids]
            is_pow2 = token_is_pow2[token_ids]
            fam_oh = var_family_onehot[var_ids]
            fam_id = var_family_id[var_ids]
            outer = var_outer_norm[var_ids]
            inner = var_inner_norm[var_ids]
            has_o = var_has_outer[var_ids]
            has_i = var_has_inner[var_ids]
            gid = var_group_id[var_ids]
            valid = has_int > 0.0
            for sid in SPECIAL:
                valid = valid & (token_ids != sid)
            validf = valid.astype(dtype)
            pos_norm = jnp.broadcast_to(jnp.arange(seq_len, dtype=dtype) / denom, (bsz, seq_len))
            tlog_v = tlog * validf
            prev_count = jnp.cumsum(validf, axis=1) - validf
            prev_logsum = jnp.cumsum(tlog_v, axis=1) - tlog_v
            prev_count_n = prev_count / denom
            prev_logsum_n = prev_logsum / denom
            prev_tlog = jnp.pad(tlog[:, :-1], ((0, 0), (1, 0)))
            prev_signed = jnp.pad(signed[:, :-1], ((0, 0), (1, 0)))
            fam_v = fam_oh * validf[..., None]
            fam_lv = fam_oh * tlog_v[..., None]
            fam_pc = jnp.cumsum(fam_v, axis=1) - fam_v
            fam_pl = jnp.cumsum(fam_lv, axis=1) - fam_lv
            fidx = fam_id[..., None]
            psf_c = jnp.take_along_axis(fam_pc, fidx, axis=-1)[..., 0]
            psf_l = jnp.take_along_axis(fam_pl, fidx, axis=-1)[..., 0]
            psf_cn = psf_c / denom
            psf_ln = psf_l / denom
            psf_r = psf_c / jnp.maximum(prev_count, 1.0)
            g_oh = jax.nn.one_hot(jnp.maximum(gid, 0), NG, dtype=dtype)
            vg = (gid > 0).astype(dtype)
            g_v = g_oh * (validf * vg)[..., None]
            g_lv = g_oh * (tlog_v * vg)[..., None]
            g_pc = jnp.cumsum(g_v, axis=1) - g_v
            g_pl = jnp.cumsum(g_lv, axis=1) - g_lv
            gidx = gid[..., None]
            psg_c = jnp.take_along_axis(g_pc, gidx, axis=-1)[..., 0]
            psg_l = jnp.take_along_axis(g_pl, gidx, axis=-1)[..., 0]
            psg_c = jnp.where(gid > 0, psg_c, 0.0)
            psg_l = jnp.where(gid > 0, psg_l, 0.0)
            psg_cn = psg_c / denom
            psg_ln = psg_l / denom
            psg_r = psg_c / jnp.maximum(prev_count, 1.0)
            static_token = jnp.stack([has_int, signed, tlog, is_zero, is_pow2], axis=-1)
            static_var = jnp.concatenate([fam_oh, outer[..., None], inner[..., None], has_o[..., None], has_i[..., None]], axis=-1)
            dyn = jnp.stack([pos_norm, prev_count_n, prev_logsum_n, psf_cn, psf_ln, psf_r, psg_cn, psg_ln, psg_r, prev_tlog, prev_signed, is_one], axis=-1)
            feat = jnp.concatenate([static_token, static_var, dyn], axis=-1)
            mu = jnp.mean(feat, axis=-1, keepdims=True)
            var = jnp.var(feat, axis=-1, keepdims=True)
            x = (feat - mu) / jnp.sqrt(var + 1e-05) * ln_g + ln_b
            h = jax.nn.gelu(x @ W1 + b1, approximate=False)
            return scale * (h @ W2 + b2)
        key = jax.random.key(seed)
        ks = jax.random.split(key, 18)
        f32 = jnp.float32
        token_has_int = (jax.random.uniform(ks[0], (V,)) > 0.3).astype(f32)
        token_signed_norm = jax.random.uniform(ks[1], (V,), minval=-1.0, maxval=1.0).astype(f32)
        token_log_norm = jax.random.uniform(ks[2], (V,)).astype(f32)
        token_is_zero = (jax.random.uniform(ks[3], (V,)) > 0.95).astype(f32)
        token_is_one = (jax.random.uniform(ks[4], (V,)) > 0.95).astype(f32)
        token_is_pow2 = (jax.random.uniform(ks[5], (V,)) > 0.9).astype(f32)
        var_family_id = jax.random.randint(ks[6], (NV,), 0, NF)
        var_family_onehot = jax.nn.one_hot(var_family_id, NF, dtype=f32)
        var_outer_norm = jax.random.uniform(ks[7], (NV,)).astype(f32)
        var_inner_norm = jax.random.uniform(ks[8], (NV,)).astype(f32)
        var_has_outer = (jax.random.uniform(ks[9], (NV,)) > 0.5).astype(f32)
        var_has_inner = (jax.random.uniform(ks[10], (NV,)) > 0.5).astype(f32)
        var_group_id = jax.random.randint(ks[11], (NV,), 0, NG)
        ln_g = jnp.ones((IN_DIM,), f32)
        ln_b = jnp.zeros((IN_DIM,), f32)
        W1 = (jax.random.normal(ks[12], (IN_DIM, H)) * 0.05).astype(f32)
        b1 = jnp.zeros((H,), f32)
        W2 = (jax.random.normal(ks[13], (H, D)) * 0.05).astype(f32)
        b2 = jnp.zeros((D,), f32)
        scale = jnp.asarray(0.1, f32)
        token_ids = jax.random.randint(ks[14], (B, S), 0, V)
        var_ids = jax.random.randint(ks[15], (B, S), 0, NV)
        return dict(token_ids=token_ids, var_ids=var_ids, token_has_int=token_has_int, token_signed_norm=token_signed_norm, token_log_norm=token_log_norm, token_is_zero=token_is_zero, token_is_one=token_is_one, token_is_pow2=token_is_pow2, var_family_onehot=var_family_onehot, var_family_id=var_family_id, var_outer_norm=var_outer_norm, var_inner_norm=var_inner_norm, var_has_outer=var_has_outer, var_has_inner=var_has_inner, var_group_id=var_group_id, ln_g=ln_g, ln_b=ln_b, W1=W1, b1=b1, W2=W2, b2=b2, scale=scale)
    _L0_txt_all = _L0_txt_setup()
    _L0_txt_in = {k: v for k, v in _L0_txt_all.items() if k in ('token_has_int', 'token_signed_norm', 'token_log_norm', 'token_is_zero', 'token_is_one', 'token_is_pow2', 'var_family_onehot', 'var_family_id', 'var_outer_norm', 'var_inner_norm', 'var_has_outer', 'var_has_inner', 'var_group_id', 'ln_g', 'ln_b', 'W1', 'b1', 'W2', 'b2', 'scale')}
    del _L0_txt_all

    def _L0_attn_setup():
        import jax, jax.numpy as jnp
        import numpy as np
        DIM = 192
        D_STATE = 16
        D_CONV = 4
        EXPAND = 2
        E = DIM * EXPAND
        EPS = 1e-06
        key = jax.random.key(seed)
        ks = jax.random.split(key, 9)
        B, L = (2, 512)
        s = lambda *sh: 0.02
        return {'x': jax.random.normal(ks[0], (B, L, DIM), jnp.float32), 'gamma': jnp.ones((DIM,), jnp.float32), 'W_in': jax.random.normal(ks[1], (E, DIM), jnp.float32) * 0.02, 'b_in': jax.random.normal(ks[2], (E,), jnp.float32) * 0.02, 'conv_w': jax.random.normal(ks[3], (E, D_CONV), jnp.float32) * 0.1, 'A': jax.random.normal(ks[4], (E, D_STATE), jnp.float32) * 0.1, 'Bp': jax.random.normal(ks[5], (E, D_STATE), jnp.float32) * 0.1, 'C': jax.random.normal(ks[6], (E, D_STATE), jnp.float32) * 0.1, 'W_out': jax.random.normal(ks[7], (DIM, E), jnp.float32) * 0.02, 'b_out': jax.random.normal(ks[8], (DIM,), jnp.float32) * 0.02}
    _L0_attn_all = _L0_attn_setup()
    _L0_attn_in = {k: v for k, v in _L0_attn_all.items() if k in ('gamma', 'W_in', 'b_in', 'conv_w', 'A', 'Bp', 'C', 'W_out', 'b_out')}
    del _L0_attn_all

    def _L0_ffn_setup():
        import jax, jax.numpy as jnp
        import numpy as np
        B, S, D, F, E = (4, 512, 192, 768, 8)
        key = jax.random.key(seed)
        ks = jax.random.split(key, 5)
        return {'x': jax.random.normal(ks[0], (B, S, D), dtype=jnp.float32), 'Ws': jax.random.normal(ks[1], (D, E), dtype=jnp.float32) * 0.02, 'bs': jnp.zeros((E,), dtype=jnp.float32), 'W1': jax.random.normal(ks[2], (E, D, F), dtype=jnp.float32) * 0.02, 'b1': jnp.zeros((E, F), dtype=jnp.float32), 'W2': jax.random.normal(ks[3], (E, F, D), dtype=jnp.float32) * 0.02, 'b2': jnp.zeros((E, D), dtype=jnp.float32)}
    _L0_ffn_all = _L0_ffn_setup()
    _L0_ffn_in = {k: v for k, v in _L0_ffn_all.items() if k in ('Ws', 'bs', 'W1', 'b1', 'W2', 'b2')}
    del _L0_ffn_all
    return {'x': x, 'x_txt': x_txt, 'itok_BS_0_4095': itok_BS_0_4095, 'L0_tok_ln1_g': _L0_tok_in['ln1_g'], 'L0_tok_ln1_b': _L0_tok_in['ln1_b'], 'L0_tok_W_proj': _L0_tok_in['W_proj'], 'L0_tok_b_proj': _L0_tok_in['b_proj'], 'L0_tok_ln2_g': _L0_tok_in['ln2_g'], 'L0_tok_ln2_b': _L0_tok_in['ln2_b'], 'L0_tok_pos_embedding': _L0_tok_in['pos_embedding'], 'L0_tok_cls_token': _L0_tok_in['cls_token'], 'L0_txt_token_has_int': _L0_txt_in['token_has_int'], 'L0_txt_token_signed_norm': _L0_txt_in['token_signed_norm'], 'L0_txt_token_log_norm': _L0_txt_in['token_log_norm'], 'L0_txt_token_is_zero': _L0_txt_in['token_is_zero'], 'L0_txt_token_is_one': _L0_txt_in['token_is_one'], 'L0_txt_token_is_pow2': _L0_txt_in['token_is_pow2'], 'L0_txt_var_family_onehot': _L0_txt_in['var_family_onehot'], 'L0_txt_var_family_id': _L0_txt_in['var_family_id'], 'L0_txt_var_outer_norm': _L0_txt_in['var_outer_norm'], 'L0_txt_var_inner_norm': _L0_txt_in['var_inner_norm'], 'L0_txt_var_has_outer': _L0_txt_in['var_has_outer'], 'L0_txt_var_has_inner': _L0_txt_in['var_has_inner'], 'L0_txt_var_group_id': _L0_txt_in['var_group_id'], 'L0_txt_ln_g': _L0_txt_in['ln_g'], 'L0_txt_ln_b': _L0_txt_in['ln_b'], 'L0_txt_W1': _L0_txt_in['W1'], 'L0_txt_b1': _L0_txt_in['b1'], 'L0_txt_W2': _L0_txt_in['W2'], 'L0_txt_b2': _L0_txt_in['b2'], 'L0_txt_scale': _L0_txt_in['scale'], 'L0_attn_gamma': _L0_attn_in['gamma'], 'L0_attn_W_in': _L0_attn_in['W_in'], 'L0_attn_b_in': _L0_attn_in['b_in'], 'L0_attn_conv_w': _L0_attn_in['conv_w'], 'L0_attn_A': _L0_attn_in['A'], 'L0_attn_Bp': _L0_attn_in['Bp'], 'L0_attn_C': _L0_attn_in['C'], 'L0_attn_W_out': _L0_attn_in['W_out'], 'L0_attn_b_out': _L0_attn_in['b_out'], 'L0_ffn_Ws': _L0_ffn_in['Ws'], 'L0_ffn_bs': _L0_ffn_in['bs'], 'L0_ffn_W1': _L0_ffn_in['W1'], 'L0_ffn_b1': _L0_ffn_in['b1'], 'L0_ffn_W2': _L0_ffn_in['W2'], 'L0_ffn_b2': _L0_ffn_in['b2']}

def reference(x, x_txt, itok_BS_0_4095, L0_tok_ln1_g, L0_tok_ln1_b, L0_tok_W_proj, L0_tok_b_proj, L0_tok_ln2_g, L0_tok_ln2_b, L0_tok_pos_embedding, L0_tok_cls_token, L0_txt_token_has_int, L0_txt_token_signed_norm, L0_txt_token_log_norm, L0_txt_token_is_zero, L0_txt_token_is_one, L0_txt_token_is_pow2, L0_txt_var_family_onehot, L0_txt_var_family_id, L0_txt_var_outer_norm, L0_txt_var_inner_norm, L0_txt_var_has_outer, L0_txt_var_has_inner, L0_txt_var_group_id, L0_txt_ln_g, L0_txt_ln_b, L0_txt_W1, L0_txt_b1, L0_txt_W2, L0_txt_b2, L0_txt_scale, L0_attn_gamma, L0_attn_W_in, L0_attn_b_in, L0_attn_conv_w, L0_attn_A, L0_attn_Bp, L0_attn_C, L0_attn_W_out, L0_attn_b_out, L0_ffn_Ws, L0_ffn_bs, L0_ffn_W1, L0_ffn_b1, L0_ffn_W2, L0_ffn_b2):
    import jax
    import jax.numpy as jnp

    def _L0_tok_ref(img, ln1_g, ln1_b, W_proj, b_proj, ln2_g, ln2_b, pos_embedding, cls_token):
        import jax, jax.numpy as jnp
        import numpy as np
        EPS = 1e-05
        P = 16

        def _layernorm(x, gamma, beta):
            mu = jnp.mean(x, axis=-1, keepdims=True)
            var = jnp.mean(jnp.square(x - mu), axis=-1, keepdims=True)
            return (x - mu) * jax.lax.rsqrt(var + EPS) * gamma + beta
        B, C, H, Wd = img.shape
        h, w = (H // P, Wd // P)
        x = img.reshape(B, C, h, P, w, P)
        x = jnp.transpose(x, (0, 2, 4, 3, 5, 1)).reshape(B, h * w, P * P * C)
        x = _layernorm(x, ln1_g, ln1_b)
        x = jnp.einsum('bnp,pd->bnd', x, W_proj) + b_proj
        x = _layernorm(x, ln2_g, ln2_b)
        cls = jnp.broadcast_to(cls_token, (B, 1, cls_token.shape[-1]))
        x = jnp.concatenate([cls, x], axis=1)
        x = x + pos_embedding
        return x

    def _L0_txt_ref(token_ids, var_ids, token_has_int, token_signed_norm, token_log_norm, token_is_zero, token_is_one, token_is_pow2, var_family_onehot, var_family_id, var_outer_norm, var_inner_norm, var_has_outer, var_has_inner, var_group_id, ln_g, ln_b, W1, b1, W2, b2, scale):
        import jax, jax.numpy as jnp
        import numpy as np
        V = 50257
        NV = 1024
        NF = 64
        NG = 64
        B, S = (8, 2048)
        H, D = (64, 192)
        SPECIAL = (0, 1, 2)
        IN_DIM = 5 + NF + 4 + 12

        def _forward(token_ids, var_ids, token_has_int, token_signed_norm, token_log_norm, token_is_zero, token_is_one, token_is_pow2, var_family_onehot, var_family_id, var_outer_norm, var_inner_norm, var_has_outer, var_has_inner, var_group_id, ln_g, ln_b, W1, b1, W2, b2, scale):
            bsz, seq_len = token_ids.shape
            dtype = token_log_norm.dtype
            denom = float(max(seq_len - 1, 1))
            has_int = token_has_int[token_ids]
            signed = token_signed_norm[token_ids]
            tlog = token_log_norm[token_ids]
            is_zero = token_is_zero[token_ids]
            is_one = token_is_one[token_ids]
            is_pow2 = token_is_pow2[token_ids]
            fam_oh = var_family_onehot[var_ids]
            fam_id = var_family_id[var_ids]
            outer = var_outer_norm[var_ids]
            inner = var_inner_norm[var_ids]
            has_o = var_has_outer[var_ids]
            has_i = var_has_inner[var_ids]
            gid = var_group_id[var_ids]
            valid = has_int > 0.0
            for sid in SPECIAL:
                valid = valid & (token_ids != sid)
            validf = valid.astype(dtype)
            pos_norm = jnp.broadcast_to(jnp.arange(seq_len, dtype=dtype) / denom, (bsz, seq_len))
            tlog_v = tlog * validf
            prev_count = jnp.cumsum(validf, axis=1) - validf
            prev_logsum = jnp.cumsum(tlog_v, axis=1) - tlog_v
            prev_count_n = prev_count / denom
            prev_logsum_n = prev_logsum / denom
            prev_tlog = jnp.pad(tlog[:, :-1], ((0, 0), (1, 0)))
            prev_signed = jnp.pad(signed[:, :-1], ((0, 0), (1, 0)))
            fam_v = fam_oh * validf[..., None]
            fam_lv = fam_oh * tlog_v[..., None]
            fam_pc = jnp.cumsum(fam_v, axis=1) - fam_v
            fam_pl = jnp.cumsum(fam_lv, axis=1) - fam_lv
            fidx = fam_id[..., None]
            psf_c = jnp.take_along_axis(fam_pc, fidx, axis=-1)[..., 0]
            psf_l = jnp.take_along_axis(fam_pl, fidx, axis=-1)[..., 0]
            psf_cn = psf_c / denom
            psf_ln = psf_l / denom
            psf_r = psf_c / jnp.maximum(prev_count, 1.0)
            g_oh = jax.nn.one_hot(jnp.maximum(gid, 0), NG, dtype=dtype)
            vg = (gid > 0).astype(dtype)
            g_v = g_oh * (validf * vg)[..., None]
            g_lv = g_oh * (tlog_v * vg)[..., None]
            g_pc = jnp.cumsum(g_v, axis=1) - g_v
            g_pl = jnp.cumsum(g_lv, axis=1) - g_lv
            gidx = gid[..., None]
            psg_c = jnp.take_along_axis(g_pc, gidx, axis=-1)[..., 0]
            psg_l = jnp.take_along_axis(g_pl, gidx, axis=-1)[..., 0]
            psg_c = jnp.where(gid > 0, psg_c, 0.0)
            psg_l = jnp.where(gid > 0, psg_l, 0.0)
            psg_cn = psg_c / denom
            psg_ln = psg_l / denom
            psg_r = psg_c / jnp.maximum(prev_count, 1.0)
            static_token = jnp.stack([has_int, signed, tlog, is_zero, is_pow2], axis=-1)
            static_var = jnp.concatenate([fam_oh, outer[..., None], inner[..., None], has_o[..., None], has_i[..., None]], axis=-1)
            dyn = jnp.stack([pos_norm, prev_count_n, prev_logsum_n, psf_cn, psf_ln, psf_r, psg_cn, psg_ln, psg_r, prev_tlog, prev_signed, is_one], axis=-1)
            feat = jnp.concatenate([static_token, static_var, dyn], axis=-1)
            mu = jnp.mean(feat, axis=-1, keepdims=True)
            var = jnp.var(feat, axis=-1, keepdims=True)
            x = (feat - mu) / jnp.sqrt(var + 1e-05) * ln_g + ln_b
            h = jax.nn.gelu(x @ W1 + b1, approximate=False)
            return scale * (h @ W2 + b2)
        return _forward(token_ids, var_ids, token_has_int, token_signed_norm, token_log_norm, token_is_zero, token_is_one, token_is_pow2, var_family_onehot, var_family_id, var_outer_norm, var_inner_norm, var_has_outer, var_has_inner, var_group_id, ln_g, ln_b, W1, b1, W2, b2, scale)

    def _L0_attn_ref(x, gamma, W_in, b_in, conv_w, A, Bp, C, W_out, b_out):
        import jax, jax.numpy as jnp
        import numpy as np
        DIM = 192
        D_STATE = 16
        D_CONV = 4
        EXPAND = 2
        E = DIM * EXPAND
        EPS = 1e-06
        residual = x
        rms = jnp.linalg.norm(x, axis=-1, keepdims=True) * x.shape[-1] ** (-0.5)
        xn = gamma * (x / (rms + EPS))
        xp = xn @ W_in.T + b_in
        B_, L_, _ = xp.shape
        pad = D_CONV - 1
        xpad = jnp.pad(xp, ((0, 0), (pad, 0), (0, 0)))
        xc = jnp.zeros_like(xp)
        for k in range(D_CONV):
            xc = xc + xpad[:, k:k + L_, :] * conv_w[:, k]
        sigA = jax.nn.sigmoid(A)
        sigB = jax.nn.sigmoid(Bp)
        sigC = jax.nn.sigmoid(C)

        def step(h, xt):
            h = sigA * h + sigB * xt[:, :, None]
            y = jnp.einsum('ben,en->be', h, sigC)
            return (h, y)
        h0 = jnp.zeros((B_, E, D_STATE), xp.dtype)
        _, ys = jax.lax.scan(step, h0, jnp.swapaxes(xc, 0, 1))
        y = jnp.swapaxes(ys, 0, 1)
        out = y @ W_out.T + b_out
        return out + residual

    def _L0_ffn_ref(x, Ws, bs, W1, b1, W2, b2):
        import jax, jax.numpy as jnp
        import numpy as np
        B, S, D, F, E = (4, 512, 192, 768, 8)
        b, s, d = x.shape
        xt = x.reshape(-1, d)
        logits = xt @ Ws + bs
        probs = jax.nn.softmax(logits, axis=-1)
        routes = jnp.argmax(probs, axis=-1)
        prob_max = jnp.max(probs, axis=-1)
        h = jax.nn.gelu(jnp.einsum('td,edf->etf', xt, W1) + b1[:, None, :], approximate=False)
        y = jnp.einsum('etf,efd->etd', h, W2) + b2[:, None, :]
        out = jnp.take_along_axis(y, routes[None, :, None], axis=0)[0]
        out = out * prob_max[:, None]
        return out.reshape(b, s, d)
    h = _L0_tok_ref(x, L0_tok_ln1_g, L0_tok_ln1_b, L0_tok_W_proj, L0_tok_b_proj, L0_tok_ln2_g, L0_tok_ln2_b, L0_tok_pos_embedding, L0_tok_cls_token)
    h = jnp.concatenate([h, _L0_txt_ref(x_txt, itok_BS_0_4095, L0_txt_token_has_int, L0_txt_token_signed_norm, L0_txt_token_log_norm, L0_txt_token_is_zero, L0_txt_token_is_one, L0_txt_token_is_pow2, L0_txt_var_family_onehot, L0_txt_var_family_id, L0_txt_var_outer_norm, L0_txt_var_inner_norm, L0_txt_var_has_outer, L0_txt_var_has_inner, L0_txt_var_group_id, L0_txt_ln_g, L0_txt_ln_b, L0_txt_W1, L0_txt_b1, L0_txt_W2, L0_txt_b2, L0_txt_scale)], axis=1)
    h = h + _L0_attn_ref(_layernorm(h, axis=-1), L0_attn_gamma, L0_attn_W_in, L0_attn_b_in, L0_attn_conv_w, L0_attn_A, L0_attn_Bp, L0_attn_C, L0_attn_W_out, L0_attn_b_out)
    h = h + _L0_ffn_ref(_layernorm(h, axis=-1), L0_ffn_Ws, L0_ffn_bs, L0_ffn_W1, L0_ffn_b1, L0_ffn_W2, L0_ffn_b2)
    return h

_drawn_inputs = setup_inputs


def setup_inputs(seed=0):
    import zlib

    import numpy as np

    out = dict(_drawn_inputs(seed))
    spreads = {'L0_tok_ln1_g': (1.0, 0.2),
     'L0_tok_ln1_b': (0.0, 0.1),
     'L0_tok_b_proj': (0.0, 0.1),
     'L0_tok_ln2_g': (1.0, 0.2),
     'L0_tok_ln2_b': (0.0, 0.1),
     'L0_txt_ln_g': (1.0, 0.2),
     'L0_txt_ln_b': (0.0, 0.286),
     'L0_txt_b1': (0.0, 0.1),
     'L0_txt_b2': (0.0, 0.1),
     'L0_attn_gamma': (1.0, 0.6),
     'L0_ffn_bs': (0.0, 0.8),
     'L0_ffn_b1': (0.0, 0.8),
     'L0_ffn_b2': (0.0, 0.8)}
    factors = {'L0_txt_token_is_zero': 3.283,
     'L0_txt_token_is_one': 3.431,
     'L0_attn_b_in': 8.0,
     'L0_attn_A': 8.0,
     'L0_attn_Bp': 8.0,
     'L0_attn_C': 8.0,
     'L0_attn_b_out': 5.296,
     'L0_ffn_Ws': 4.921,
     'L0_ffn_W1': 7.775,
     'L0_ffn_W2': 7.296}
    for name, (base, spread) in spreads.items():
        noise = np.random.default_rng([zlib.crc32(name.encode()), seed]).standard_normal(out[name].shape)
        drawn = base * np.exp(spread * noise) if base else spread * noise
        out[name] = jnp.asarray(drawn.astype(out[name].dtype))
    for name, factor in factors.items():
        out[name] = (out[name] * factor).astype(out[name].dtype)
    return out
```

```python
from contextlib import ExitStack

import concourse.bass as bass
from concourse import mybir

F32 = mybir.dt.float32
I32 = mybir.dt.int32
ALU = mybir.AluOpType
ACT = mybir.ActivationFunctionType
AX = mybir.AxisListType

B = 32
D = 192
HD = D // 2
IMG, PATCH, CH = 224, 16, 3
GRID = IMG // PATCH
NIMG = GRID * GRID
TXT = 128
L = 1 + NIMG + TXT
NCHUNK, Q = 4, 82
LP = NCHUNK * Q
CB = B * NCHUNK
E = 384
NS = 16
TAPS = 4
HALO = TAPS - 1
W = Q + HALO
EB = 96
NBLK = E // EB
GE = 8
NG = EB // GE
GPW = Q + NS
KREV = 180
NEX, FF = 8, 768
FC = FF // 128
V = 50257
NVAR = 1024
NF = 64
FEAT = 85
NTILE = (B * L + NEX * 127) // 128
SLOTS = NTILE * 128
ROW = D + 4
FAR = 1 << 20
EPS = 1e-5

GB = 8
GP_ROWS = GB * GRID
NGRP = B // GB
PD = PATCH * PATCH * CH
KC = PD // 128



def bank(nc, ctx, name, shape):
    t = ctx.enter_context(nc.psum_tensor(name, [128, 512], F32))
    n = 1
    for s in shape[1:]:
        n *= s
    v = t[0:shape[0], 0:n]
    if len(shape) == 3:
        v = v.rearrange("p (a b) -> p a b", a=shape[1])
    return v


def embed_images(nc, io, dr, keep):
    with ExitStack() as ctx:
        def sb(name, shape, dt=F32):
            return ctx.enter_context(nc.sbuf_tensor(name, shape, dt))

        def sem(name):
            return ctx.enter_context(nc.semaphore(name))

        R = GP_ROWS
        xg = [sb(f"xg{j}", [R, CH * PATCH, IMG]) for j in range(2)]
        xc = [sb(f"xc{j}", [R, CH * PATCH, PATCH]) for j in range(2)]
        xt = [sb(f"xt{j}", [128, KC, R]) for j in range(2)]
        wp = sb("wp", [128, KC, D])
        g1 = sb("g1", [128, KC])
        b1 = sb("b1", [128, KC])
        b1w = sb("b1w", [128, KC, R])
        wg = sb("wg", [128, KC, D])
        bias1 = sb("bias1", [R, D])
        g2 = sb("g2", [R, D])
        b2 = sb("b2", [R, D])
        pos = sb("pos", [R, GRID, D])
        yg = [sb(f"yg{j}", [R, GRID, D]) for j in range(2)]
        st = sb("st1", [R, GRID, 2, 6])
        mv = [sb(f"mv1{j}", [R, GRID, 2]) for j in range(2)]
        ve = [sb(f"ve1{j}", [R, GRID]) for j in range(2)]
        rs = [sb(f"rs1{j}", [R, GRID]) for j in range(2)]
        nb = [sb(f"nb1{j}", [R, GRID]) for j in range(2)]
        sty = sb("sty", [R, GRID, 6])
        mvy = sb("mvy", [R, GRID, 2])
        vey = sb("vey", [R, GRID])
        rsy = sb("rsy", [R, GRID])
        cls = sb("cls", [B, 2, D])
        zrow = sb("zrow", [128, HALO * D])
        xs0 = sb("xs0", [128, ROW])

        ps_t = [[bank(nc, ctx, f"ps_t{j}{k}", [128, 3, R]) for k in range(2)]
                for j in range(2)]
        ps_y = [bank(nc, ctx, f"ps_y{j}", [R, D]) for j in range(2)]
        ps_b = bank(nc, ctx, "ps_b", [R, D])

        x_in = [sem("x_in0"), sem("x_in1")]
        w_in = sem("w_in")
        w_ready = sem("w_ready")
        x_std = sem("x_std")
        x_sqrt = sem("x_sqrt")
        x_rstd = sem("x_rstd")
        x_normed = sem("x_normed")
        turned = sem("turned")
        turned_out = sem("turned_out")
        projected = sem("projected")
        y_taken = sem("y_taken")
        bias_mm = sem("bias_mm")
        y_var = sem("y_var")
        y_sqrt = sem("y_sqrt")
        y_normed = sem("y_normed")
        y_scaled = sem("y_scaled")
        y_out = [sem("y_out0"), sem("y_out1")]
        step = sem("step1")
        pstep = sem("pstep1")
        const = sem("const1")
        ids_in = sem("ids_in")
        gath = sem("gath")
        tab = sem("tab")
        misc = sem("misc")
        block = ctx.enter_context(nc.Block())

        xv = io["x"].rearrange("b c (h p) w -> b h c (p w)", p=PATCH)
        wv = io["L0_tok_W_proj"].rearrange("(f c) d -> c f d", c=CH)
        gv = io["L0_tok_ln1_g"].rearrange("(f c) -> c f", c=CH)
        bv = io["L0_tok_ln1_b"].rearrange("(f c) -> c f", c=CH)
        posv = io["L0_tok_pos_embedding"]
        h0 = dr["h0"]

        @block.sync
        def _(sp):
            for g in range(NGRP):
                if g >= 2:
                    sp.wait_ge(x_normed, GRID * (g - 1))
                for b in range(GB):
                    sp.dma_start(xg[g % 2][b * GRID:(b + 1) * GRID, :, :].rearrange("r (c p) w -> r c (p w)", c=CH),
                                 xv[g * GB + b]).then_inc(x_in[g % 2], 16)
            for g in range(NGRP):
                sp.wait_ge(y_scaled, 2 * (g + 1))
                for b in range(GB):
                    row = (g * GB + b) * LP + 1
                    sp.dma_start(h0[row:row + NIMG, :].rearrange("(h w) d -> h (w d)", w=GRID),
                                 yg[g % 2][b * GRID:(b + 1) * GRID, :, :].rearrange("r w d -> r (w d)")
                                 ).then_inc(y_out[g % 2], 16)
            for j in range(2):
                sp.wait_ge(y_out[j], 16 * GB * NGRP // 2)

        @block.gpsimd
        def _(pool):
            pool.memset(keep["ident"][:], 0.0).then_inc(const, 1)
            pool.memset(keep["before"][:], 1.0).then_inc(const, 1)
            pool.memset(keep["shift"][:], 0.0).then_inc(const, 1)
            pool.memset(keep["ones"][:], 1.0).then_inc(const, 1)
            pool.wait_ge(const, 4)
            pool.affine_select(out=keep["ident"][:], in_=keep["ident"][:], compare_op=ALU.not_equal, fill=1.0,
                               base=0, pattern=[[-1, 128]], channel_multiplier=1).then_inc(const, 1)
            pool.affine_select(out=keep["before"][:], in_=keep["before"][:], compare_op=ALU.is_gt, fill=0.0,
                               base=0, pattern=[[1, 128]], channel_multiplier=-1).then_inc(const, 1)
            pool.affine_select(out=keep["shift"][:], in_=keep["shift"][:], compare_op=ALU.not_equal, fill=1.0,
                               base=-1, pattern=[[1, 128]], channel_multiplier=-1).then_inc(const, 1)
            pool.memset(xs0[:], 0.0).then_inc(pstep, 1)
            pool.memset(zrow[:], 0.0).then_inc(pstep, 1)
            pool.wait_ge(pstep, 2)
            pool.memset(xs0[:, ROW - 1:ROW].bitcast(I32), FAR).then_inc(misc, 1)
            pool.wait_ge(ids_in, 32)
            for b in range(B):
                pool.indirect_dma_start(keep["tk"][:, b * 6:(b + 1) * 6], None, io["tok_tab"],
                                        bass.IndirectOffsetOnAxis(ap=keep["tid"][:, b:b + 1], axis=0)
                                        ).then_inc(gath, 16)
            pool.wait_ge(tab, 16 * 7)
            for b in range(B):
                pool.indirect_dma_start(keep["vr"][:, b * 70:(b + 1) * 70], None, dr["var_tab"],
                                        bass.IndirectOffsetOnAxis(ap=keep["vid"][:, b:b + 1], axis=0)
                                        ).then_inc(gath, 16)
            for g in range(NGRP):
                y = yg[g % 2][:, :, :]
                pool.wait_ge(y_normed, GRID * (g + 1))
                pool.tensor_tensor(y, y, g2[:, :].unsqueeze(1).to_broadcast([R, GRID, D]), ALU.mult
                                   ).then_inc(y_scaled, 1)
                pool.wait_ge(y_scaled, 2 * g + 1)
                pool.tensor_tensor(y, y, pos[:, :, :], ALU.add).then_inc(y_scaled, 1)
            pool.wait_ge(gath, 16 * 2 * B)

        @block.scalar
        def _(act):
            for k in range(KC):
                c, p0 = k // 2, (k % 2) * 128
                act.dma_start(wp[:, k, :], wv[c, p0:p0 + 128, :]).then_inc(w_in, 16)
            with nc.allow_non_contiguous_dma(reason="per-feature vectors of a few values"):
                for k in range(KC):
                    c, p0 = k // 2, (k % 2) * 128
                    act.dma_start(g1[:, k:k + 1], gv[c, p0:p0 + 128].unsqueeze(1)).then_inc(w_in, 16)
                    act.dma_start(b1[:, k:k + 1], bv[c, p0:p0 + 128].unsqueeze(1)).then_inc(w_in, 16)
                act.dma_start(keep["tid"][:], io["x_txt"].rearrange("b s -> s b")).then_inc(ids_in, 16)
                act.dma_start(keep["vid"][:], io["itok_BS_0_4095"].rearrange("b s -> s b")).then_inc(ids_in, 16)
                vt = dr["var_tab"]
                act.dma_start(vt[:, 0:NF], io["L0_txt_var_family_onehot"]).then_inc(tab, 16)
                for n, name in enumerate(["var_outer_norm", "var_inner_norm", "var_has_outer", "var_has_inner"]):
                    act.dma_start(vt[:, NF + n:NF + n + 1], io["L0_txt_" + name].unsqueeze(1)).then_inc(tab, 16)
                for n, name in enumerate(["var_family_id", "var_group_id"]):
                    act.dma_start(vt[:, NF + 4 + n:NF + 5 + n].bitcast(I32), io["L0_txt_" + name].unsqueeze(1)
                                  ).then_inc(tab, 16)
            for tile, name in ((bias1, "L0_tok_b_proj"), (g2, "L0_tok_ln2_g"), (b2, "L0_tok_ln2_b")):
                act.dma_start(tile[:], io[name].partition_broadcast(R)).then_inc(w_in, 16)
            for b in range(GB):
                act.dma_start(pos[b * GRID:(b + 1) * GRID, :, :].rearrange("r w d -> r (w d)"),
                              posv[0, 1:1 + NIMG, :].rearrange("(h w) d -> h (w d)", w=GRID)).then_inc(w_in, 16)
            act.dma_start(cls[:, 0, :], posv[0, 0, :].partition_broadcast(B)).then_inc(w_in, 16)
            act.dma_start(cls[:, 1, :], io["L0_tok_cls_token"][0, 0, :].partition_broadcast(B)).then_inc(w_in, 16)
            act.wait_ge(misc, 1)
            act.dma_start(dr["xs"].rearrange("(p n) d -> p n d", p=128),
                          xs0[:, :].unsqueeze(1).to_broadcast([128, NTILE, ROW])).then_inc(misc, 16)
            act.dma_start(h0.rearrange("(b t) d -> b t d", t=LP)[:, L:LP, :].rearrange("b t d -> b (t d)"),
                          zrow[0:B, :]).then_inc(misc, 16)

            def root(g):
                act.wait_ge(x_std, g + 1)
                act.activation(rs[g % 2][:], ve[g % 2][:], ACT.Sqrt).then_inc(x_sqrt, 1)

            def normalise(g, w, j):
                act.activation(xc[j][:], xg[g % 2][:, :, bass.ds(w * PATCH, PATCH)], ACT.Identity,
                               bias=nb[g % 2][:, bass.ds(w, 1)], scale=rs[g % 2][:, bass.ds(w, 1)]
                               ).then_inc(x_normed, 1)

            def take(i, j):
                act.wait_ge(turned, i + 1)
                act.wait_ge(projected, i + 1)
                act.copy(xt[j][:, 0:3, :], ps_t[j][0][:])
                act.copy(xt[j][:, 3:6, :], ps_t[j][1][:]).then_inc(turned_out, 1)

            act.sem_inc(projected, 2)
            def root_y(g):
                act.wait_ge(y_var, g + 1)
                act.activation(rsy[:], vey[:], ACT.Sqrt).then_inc(y_sqrt, 1)

            root(0)
            for g in range(NGRP):
                act.wait_ge(x_rstd, g + 1)
                if g:
                    act.wait_ge(turned, GRID * g)
                normalise(g, 0, 0)
                normalise(g, 1, 1)
                if g:
                    root_y(g - 1)
                if g + 1 < NGRP:
                    root(g + 1)
                with act.Fori(0, GRID // 2 - 1) as p:
                    for j in range(2):
                        take(g * GRID + 2 * p + j, j)
                        normalise(g, 2 * p + 2 + j, j)
                for j in range(2):
                    take(g * GRID + GRID - 2 + j, j)
            root_y(NGRP - 1)
            act.wait_ge(misc, 1 + 32)
            act.wait_ge(step, CLS_STEP)
            act.dma_start(h0.rearrange("(b t) d -> b t d", t=LP)[:, 0, :], cls[:, 0, :]).then_inc(misc, 16)
            act.wait_ge(misc, 1 + 48)

        @block.tensor
        def _(pe):
            def turn(i, j):
                pe.wait_ge(x_normed, i + 1)
                pe.wait_ge(turned_out, i + 1)
                flat = xc[j][:, :, :].rearrange("r a q -> r (a q)")
                for k in range(KC):
                    t = pe.transpose(ps_t[j][k // 3][:, k % 3, :], flat[:, k * 128:(k + 1) * 128],
                                     keep["ident"][0:R, 0:R])
                t.then_inc(turned, 1)

            def project(i, j):
                pe.wait_ge(turned_out, i + 3)
                pe.wait_ge(y_taken, i + 1)
                for k in range(KC):
                    m = pe.matmul(ps_y[j][:], xt[j][:, k, :], wg[:, k, :], start=(k == 0), stop=(k == KC - 1))
                m.then_inc(projected, 1)

            pe.sem_inc(turned_out, 2)
            pe.sem_inc(y_taken, 2)
            pe.wait_ge(const, 7)
            pe.wait_ge(w_ready, 1)
            for k in range(KC):
                m = pe.matmul(ps_b[:], b1w[:, k, :], wp[:, k, :], start=(k == 0), stop=(k == KC - 1))
            m.then_inc(bias_mm, 1)
            n = NGRP * GRID
            turn(0, 0)
            with pe.Fori(0, n // 2 - 1) as p:
                for j in range(2):
                    turn(2 * p + 1 + j, 1 - j)
                    project(2 * p + j, j)
            turn(n - 1, 1)
            project(n - 2, 0)
            project(n - 1, 1)

        @block.vector
        def _(dve):
            done = [0]

            def link(ins):
                done[0] += 1
                ins.then_inc(step, 1)
                dve.wait_ge(step, done[0])

            def x_stats(g):
                dve.wait_ge(x_in[g % 2], 16 * GB * (g // 2 + 1))
                if g >= 2:
                    dve.wait_ge(x_normed, GRID * (g - 1))
                x = xg[g % 2]
                half = CH * PATCH // 2
                with dve.Fori(0, GRID) as w:
                    for k in range(2):
                        dve.bn_stats(st[:, bass.ds(w, 1), k, :].rearrange("r a b -> r (a b)"),
                                     x[:, k * half:(k + 1) * half, bass.ds(w * PATCH, PATCH)])
                link(dve.memset(ve[g % 2][:], 0.0))
                for w in range(GRID):
                    dve.bn_aggr(mv[g % 2][:, w, :], st[:, w, :, :].rearrange("r k s -> r (k s)"))
                link(dve.memset(nb[g % 2][:], 0.0))
                dve.tensor_scalar(ve[g % 2][:], mv[g % 2][:, :, 1], EPS, None, ALU.add).then_inc(x_std, 1)
                dve.wait_ge(x_sqrt, g + 1)
                link(dve.reciprocal(rs[g % 2][:], rs[g % 2][:]))
                dve.scalar_tensor_tensor(out=nb[g % 2][:], in0=mv[g % 2][:, :, 0], scalar=-1.0, in1=rs[g % 2][:],
                                         op0=ALU.mult, op1=ALU.mult).then_inc(x_rstd, 1)

            dve.wait_ge(w_in, 16 * (3 * KC + 3 + GB + 2))
            for k in range(KC):
                dve.tensor_scalar(wg[:, k, :], wp[:, k, :], g1[:, k:k + 1], None, ALU.mult)
                dve.tensor_copy(b1w[:, k, :], b1[:, k:k + 1].to_broadcast([128, R]))
            link(dve.memset(mvy[:], 0.0))
            dve.sem_inc(w_ready, 1)
            dve.wait_ge(bias_mm, 1)
            link(dve.tensor_tensor(bias1[:], bias1[:], ps_b[:], ALU.add))
            link(dve.tensor_tensor(pos[:, :, :], pos[:, :, :], b2[:, :].unsqueeze(1).to_broadcast([R, GRID, D]),
                                   ALU.add))
            link(dve.tensor_tensor(cls[:, 0, :], cls[:, 0, :], cls[:, 1, :], ALU.add))
            assert done[0] == CLS_STEP
            x_stats(0)
            for g in range(NGRP):
                y = yg[g % 2]
                if g + 1 < NGRP:
                    x_stats(g + 1)
                if g >= 2:
                    dve.wait_ge(y_out[g % 2], 16 * GB * (g // 2))
                with dve.Fori(0, GRID // 2) as p:
                    for j in range(2):
                        i = g * GRID + 2 * p + j
                        dve.wait_ge(projected, i + 3)
                        dve.tensor_tensor(y[:, bass.ds(2 * p + j, 1), :].rearrange("r a d -> r (a d)"), ps_y[j][:],
                                          bias1[:], ALU.add).then_inc(y_taken, 1)
                dve.wait_ge(y_taken, 2 + GRID * (g + 1))
                with dve.Fori(0, GRID) as w:
                    dve.bn_stats(sty[:, bass.ds(w, 1), :].rearrange("r a s -> r (a s)"),
                                 y[:, bass.ds(w, 1), :].rearrange("r a d -> r (a d)"))
                link(dve.memset(vey[:], 0.0))
                for w in range(GRID):
                    dve.bn_aggr(mvy[:, w, :], sty[:, w, :])
                link(dve.memset(rsy[:], 0.0))
                dve.tensor_scalar(vey[:], mvy[:, :, 1], EPS, None, ALU.add).then_inc(y_var, 1)
                dve.wait_ge(y_sqrt, g + 1)
                link(dve.reciprocal(rsy[:], rsy[:]))
                with dve.Fori(0, GRID) as w:
                    row = y[:, bass.ds(w, 1), :].rearrange("r a d -> r (a d)")
                    dve.tensor_scalar(row, row, mvy[:, bass.ds(w, 1), 0], rsy[:, bass.ds(w, 1)],
                                      ALU.subtract, ALU.mult).then_inc(y_normed, 1)
                if g + 1 < NGRP:
                    dve.wait_ge(y_normed, GRID * (g + 1))


CLS_STEP = 4


def embed_text(nc, io, dr, keep):
    with ExitStack() as ctx:
        def sb(name, shape, dt=F32):
            return ctx.enter_context(nc.sbuf_tensor(name, shape, dt))

        def sem(name):
            return ctx.enter_context(nc.semaphore(name))

        tk = keep["tk"][:, :].rearrange("p (b f) -> p b f", f=6)
        vr = keep["vr"][:, :].rearrange("p (b f) -> p b f", f=70)
        vri = keep["vr"][:, :].bitcast(I32).rearrange("p (b f) -> p b f", f=70)
        ft = sb("ft", [128, B, FEAT])
        mo = sb("mo", [128, B, 4 * NF + 2])
        sel = sb("sel", [128, B, 2, NF])
        pk = sb("pk", [128, B, 4 * NF])
        ps4 = sb("ps4", [128, B, 4])
        pc = sb("pc", [128, B, 2])
        io64 = sb("io64", [128, NF])
        tf = sb("tf", [128, B])
        ff = sb("ff", [128, B, 2])
        va = sb("va", [128, B])
        vg = sb("vg", [128, B])
        va2 = sb("va2", [128, B])
        tlv = sb("tlv", [128, B])
        shi = sb("shi", [128, 2, B])
        rc = sb("rc", [128, B])
        posn = sb("posn", [128, 1])
        st = sb("stt", [128, B, 6])
        mv = sb("mvt", [128, B, 2])
        ve = sb("vet", [128, B])
        xt = [sb(f"xtt{j}", [FEAT, 4, 128]) for j in range(2)]
        ht = [sb(f"htt{j}", [NF + 1, 4, 128]) for j in range(2)]
        ot = [sb(f"ott{j}", [128, 4, D]) for j in range(2)]
        w1 = sb("w1t", [FEAT, NF])
        w2 = sb("w2t", [NF + 1, D])
        sc = sb("sct", [NF + 1, 1])
        lg = sb("lgt", [FEAT, 1])
        lb = sb("lbt", [FEAT, 1])
        bb = sb("bbt", [NF, 1])
        pp = [bank(nc, ctx, f"pp{j}", [128, 512]) for j in range(2)]
        pt = [bank(nc, ctx, f"pt{j}", [FEAT, 4, 128]) for j in range(2)]
        ph = bank(nc, ctx, "ph", [NF, 512])
        po = [bank(nc, ctx, f"po{j}", [128, 2, 256]) for j in range(2)]

        w_in = sem("tw_in")
        iot = sem("iot")
        step = sem("step2")
        mo_ready = sem("mo_ready")
        summed = sem("summed")
        sum_taken = sem("sum_taken")
        ft_std = sem("ft_std")
        ft_sqrt = sem("ft_sqrt")
        ft_ready = sem("ft_ready")
        turned = sem("t_turned")
        xt_ready = sem("t_xt")
        hid = sem("t_hid")
        ht_ready = sem("t_ht")
        outp = sem("t_outp")
        taken = sem("t_taken")
        stored = [sem("t_st0"), sem("t_st1")]
        block = ctx.enter_context(nc.Block())
        T = "L0_txt_"
        NG4 = B // 4

        @block.sync
        def _(sp):
            sp.dma_start(w1[:], io[T + "W1"]).then_inc(w_in, 16)
            sp.dma_start(w2[0:NF, :], io[T + "W2"]).then_inc(w_in, 16)
            sp.dma_start(w2[NF:NF + 1, :], io[T + "b2"].unsqueeze(0)).then_inc(w_in, 16)
            sp.dma_start(sc[:], io[T + "scale"].partition_broadcast(NF + 1)).then_inc(w_in, 16)
            with nc.allow_non_contiguous_dma(reason="one value per partition"):
                sp.dma_start(lg[:], io[T + "ln_g"].unsqueeze(1)).then_inc(w_in, 16)
                sp.dma_start(lb[:], io[T + "ln_b"].unsqueeze(1)).then_inc(w_in, 16)
                sp.dma_start(bb[:], io[T + "b1"].unsqueeze(1)).then_inc(w_in, 16)
            hv = dr["h0"].rearrange("(b t) d -> t b d", t=LP)
            for n in range(NG4):
                sp.wait_ge(taken, 2 * (n + 1))
                sp.dma_start(hv[1 + NIMG:L, 4 * n:4 * n + 4, :], ot[n % 2][:]).then_inc(stored[n % 2], 16)
            for j in range(2):
                sp.wait_ge(stored[j], 16 * (NG4 // 2))

        @block.gpsimd
        def _(pool):
            pool.iota(io64[:], pattern=[[1, NF]], base=0, channel_multiplier=0,
                      allow_small_or_imprecise_dtypes=True).then_inc(iot, 1)
            pool.iota(posn[:], pattern=[[0, 1]], base=0, channel_multiplier=1,
                      allow_small_or_imprecise_dtypes=True).then_inc(iot, 1)
            pool.wait_ge(iot, 2)
            for j in range(2):
                pool.memset(ht[j][NF:NF + 1, :, :], 1.0).then_inc(iot, 1)

        @block.vector
        def _(dve):
            done = [0]

            def link(ins):
                done[0] += 1
                ins.then_inc(step, 1)
                dve.wait_ge(step, done[0])

            def bc(ap, n=NF):
                return ap.unsqueeze(2).to_broadcast([128, B, n])

            tt, ts = dve.tensor_tensor, dve.tensor_scalar
            dve.wait_ge(iot, 4)
            tt(sel[:, :, 0, :], vri[:, :, 68:69].to_broadcast([128, B, NF]),
               io64[:, :].unsqueeze(1).to_broadcast([128, B, NF]), ALU.is_equal)
            ts(ff[:, :, :], vri[:, :, 68:70], 0.0, None, ALU.max)
            ts(va2[:, :], vri[:, :, 69], 0.0, None, ALU.is_gt)
            ts(tf[:, :], keep["tid"][:, :], 2.5, None, ALU.is_gt)
            link(ts(va[:, :], tk[:, :, 0], 0.0, None, ALU.is_gt))
            tt(sel[:, :, 1, :], bc(ff[:, :, 1]), io64[:, :].unsqueeze(1).to_broadcast([128, B, NF]), ALU.is_equal)
            link(tt(va[:, :], va[:, :], tf[:, :], ALU.mult))
            tt(sel[:, :, 1, :], sel[:, :, 1, :], bc(va2[:, :]), ALU.mult)
            link(tt(tlv[:, :], tk[:, :, 2], va[:, :], ALU.mult))
            tt(mo[:, :, 0:NF], vr[:, :, 0:NF], bc(va[:, :]), ALU.mult)
            tt(mo[:, :, NF:2 * NF], vr[:, :, 0:NF], bc(tlv[:, :]), ALU.mult)
            tt(mo[:, :, 2 * NF:3 * NF], sel[:, :, 1, :], bc(va[:, :]), ALU.mult)
            tt(mo[:, :, 3 * NF:4 * NF], sel[:, :, 1, :], bc(tlv[:, :]), ALU.mult)
            dve.tensor_copy(mo[:, :, 4 * NF], va[:, :])
            dve.tensor_copy(mo[:, :, 4 * NF + 1], tlv[:, :])
            dve.tensor_copy(shi[:, 0, :], tk[:, :, 2])
            dve.tensor_copy(shi[:, 1, :], tk[:, :, 1]).then_inc(mo_ready, 1)
            dve.tensor_copy(ft[:, :, 0:5], tk[:, :, 0:5])
            dve.tensor_copy(ft[:, :, 5:5 + NF + 4], vr[:, :, 0:NF + 4])
            ts(ft[:, :, 73], posn[:, :].to_broadcast([128, B]), 1.0 / (TXT - 1), None, ALU.mult)
            dve.tensor_copy(ft[:, :, 84], tk[:, :, 5])
            for b in range(B):
                dve.wait_ge(summed, b + 1)
                p = pp[b % 2]
                tt(pk[:, b, :].rearrange("p (g c f) -> p g c f", g=2, c=2),
                   p[:, 0:4 * NF].rearrange("p (g c f) -> p g c f", g=2, c=2),
                   sel[:, b, :, :].unsqueeze(2).to_broadcast([128, 2, 2, NF]), ALU.mult)
                dve.tensor_copy(pc[:, b, :], p[:, 4 * NF:4 * NF + 2]).then_inc(sum_taken, 1)
            dve.wait_ge(summed, B + 1)
            dve.wait_ge(sum_taken, B)
            dve.tensor_copy(ft[:, :, 82:84].rearrange("p b c -> p c b"),
                            pp[0][:, 0:2 * B].rearrange("p (c b) -> p c b", c=2))
            link(dve.tensor_reduce(ps4[:, :, :], pk[:, :, :].rearrange("p b (k f) -> p b k f", f=NF), AX.X, ALU.add))
            link(ts(rc[:, :], pc[:, :, 0], 1.0, None, ALU.max))
            link(dve.reciprocal(rc[:, :], rc[:, :]))
            inv = 1.0 / (TXT - 1)
            ts(ft[:, :, 74:76], pc[:, :, :], inv, None, ALU.mult)
            ts(ft[:, :, 76:78], ps4[:, :, 0:2], inv, None, ALU.mult)
            tt(ft[:, :, 78], ps4[:, :, 0], rc[:, :], ALU.mult)
            ts(ft[:, :, 79:81], ps4[:, :, 2:4], inv, None, ALU.mult)
            link(tt(ft[:, :, 81], ps4[:, :, 2], rc[:, :], ALU.mult))
            for b in range(B):
                s = dve.bn_stats(st[:, b, :], ft[:, b, :])
            link(s)
            for b in range(B):
                s = dve.bn_aggr(mv[:, b, :], st[:, b, :])
            link(s)
            ts(ve[:, :], mv[:, :, 1], EPS, None, ALU.add).then_inc(ft_std, 1)
            tt(ft[:, :, :], ft[:, :, :], bc(mv[:, :, 0], FEAT), ALU.subtract)
            dve.wait_ge(ft_sqrt, 1)
            link(dve.reciprocal(ve[:, :], ve[:, :]))
            tt(ft[:, :, :], ft[:, :, :], bc(ve[:, :], FEAT), ALU.mult).then_inc(ft_ready, 1)
            dve.wait_ge(w_in, 16 * 7)
            ts(w2[:, :], w2[:, :], sc[:, 0:1], None, ALU.mult).then_inc(ft_ready, 1)
            for n in range(NG4):
                if n >= 2:
                    dve.wait_ge(stored[n % 2], 16 * (n // 2))
                for k in range(2):
                    dve.wait_ge(outp, 2 * n + k + 1)
                    dve.tensor_copy(ot[n % 2][:, 2 * k:2 * k + 2, :], po[k][:, :, 0:D]).then_inc(taken, 1)

        @block.scalar
        def _(act):
            act.wait_ge(ft_std, 1)
            act.activation(ve[:, :], ve[:, :], ACT.Sqrt).then_inc(ft_sqrt, 1)
            act.wait_ge(w_in, 16 * 7)
            act.wait_ge(iot, 4)
            for n in range(NG4):
                act.wait_ge(turned, n + 1)
                if n >= 2:
                    act.wait_ge(hid, n - 1)
                act.activation(xt[n % 2][:, :, :], pt[n % 2][:], ACT.Identity, bias=lb[:, 0:1], scale=lg[:, 0:1]
                               ).then_inc(xt_ready, 1)
                act.wait_ge(hid, n + 1)
                if n >= 2:
                    act.wait_ge(outp, 2 * (n - 1))
                act.activation(ht[n % 2][0:NF, :, :].rearrange("p a b -> p (a b)"), ph[:, :], ACT.Gelu,
                               bias=bb[:, 0:1]).then_inc(ht_ready, 1)

        @block.tensor
        def _(pe):
            pe.wait_ge(mo_ready, 1)
            for b in range(B):
                if b >= 2:
                    pe.wait_ge(sum_taken, b - 1)
                pe.matmul(pp[b % 2][:, 0:4 * NF + 2], keep["before"][:], mo[:, b, :], start=True, stop=True
                          ).then_inc(summed, 1)
            pe.wait_ge(sum_taken, B - 1)
            pe.matmul(pp[0][:, 0:2 * B], keep["shift"][:], shi[:, :, :].rearrange("p c b -> p (c b)"),
                      start=True, stop=True).then_inc(summed, 1)
            pe.wait_ge(w_in, 16 * 7)
            pe.wait_ge(ft_ready, 2)

            def turn(n):
                if n >= 2:
                    pe.wait_ge(xt_ready, n - 1)
                for k in range(4):
                    t = pe.transpose(pt[n % 2][:, k, :], ft[:, 4 * n + k, :], keep["ident"][:])
                t.then_inc(turned, 1)

            turn(0)
            for n in range(NG4):
                if n + 1 < NG4:
                    turn(n + 1)
                pe.wait_ge(xt_ready, n + 1)
                if n:
                    pe.wait_ge(ht_ready, n)
                pe.matmul(ph[:, :], w1[:], xt[n % 2][:, :, :].rearrange("p a b -> p (a b)"), start=True, stop=True
                          ).then_inc(hid, 1)
                pe.wait_ge(ht_ready, n + 1)
                for k in range(2):
                    if n:
                        pe.wait_ge(taken, 2 * (n - 1) + k + 1)
                    for q in range(2):
                        m = pe.matmul(po[k][:, q, 0:D], ht[n % 2][:, 2 * k + q, :], w2[:], start=True, stop=True)
                    m.then_inc(outp, 1)


def mixer_tables(nc, io, dr, keep):
    with ExitStack() as ctx:
        def sb(name, shape, dt=F32):
            return ctx.enter_context(nc.sbuf_tensor(name, shape, dt))

        def sem(name):
            return ctx.enter_context(nc.semaphore(name))

        abc = sb("abc", [EB, 3, NBLK, NS])
        cw = sb("cw", [EB, NBLK, TAPS])
        lam = sb("lam", [EB, NBLK, NS])
        cc = sb("cc", [EB, NBLK, NS])
        c2 = sb("c2", [EB, NBLK, NS])
        t1 = sb("t1", [EB, NBLK, NS])
        t2 = sb("t2", [EB, NBLK, NS])
        k3 = sb("k3", [EB, 3, NBLK])
        u3 = sb("u3", [EB, NBLK])
        ex = sb("ex", [EB, NS, Q])
        mex = sb("mex", [EB, Q])
        kr = sb("kr", [EB, NBLK, KREV])
        in_ = sem("m_in")
        sg = sem("m_sg")
        iot = sem("m_iot")
        step = sem("m_step")
        argd = sem("m_arg")
        expd = sem("m_exp")
        done_k = sem("m_done")
        out = sem("m_out")
        block = ctx.enter_context(nc.Block())

        @block.sync
        def _(sp):
            for n, name in enumerate(["A", "Bp", "C"]):
                sp.dma_start(abc[:, n, :, :], io["L0_attn_" + name].rearrange("(k p) n -> p k n", p=EB)).then_inc(in_, 16)
            sp.dma_start(cw[:, :, :], io["L0_attn_conv_w"].rearrange("(k p) n -> p k n", p=EB)).then_inc(in_, 16)
            sp.wait_ge(done_k, 1)
            sp.dma_start(dr["kd"].rearrange("(k p) n -> p k n", p=EB), kr[:]).then_inc(out, 16)
            sp.dma_start(dr["lamd"].rearrange("(k p n) -> p k n", p=EB, n=NS), lam[:]).then_inc(out, 16)
            sp.dma_start(dr["c2d"].rearrange("(k p n) -> p k n", p=EB, n=NS), c2[:]).then_inc(out, 16)
            sp.wait_ge(out, 48)
            with nc.allow_non_contiguous_dma(reason="one value per partition"):
                sp.dma_start(keep["lamc"][:], dr["lamd"].rearrange("(g p) -> p g", p=128)).then_inc(out, 16)
                sp.dma_start(keep["c2c"][:], dr["c2d"].rearrange("(g p) -> p g", p=128)).then_inc(out, 16)
            sp.wait_ge(out, 80)

        @block.gpsimd
        def _(pool):
            pool.iota(mex[:], pattern=[[-1, Q]], base=Q - 1, channel_multiplier=0,
                      allow_small_or_imprecise_dtypes=True).then_inc(iot, 1)
            pool.iota(keep["texp"][:], pattern=[[-1, Q]], base=Q, channel_multiplier=0,
                      allow_small_or_imprecise_dtypes=True).then_inc(iot, 1)
            pool.iota(keep["sexp"][:, 0:1], pattern=[[0, 1]], base=Q - 1, channel_multiplier=-1,
                      allow_small_or_imprecise_dtypes=True).then_inc(iot, 1)
            pool.memset(keep["sexp"][:, 1:2], 0.0).then_inc(iot, 1)
            pool.wait_ge(iot, 4)
            pool.affine_select(out=keep["sexp"][:, 0:1], in_=keep["sexp"][:, 0:1], compare_op=ALU.is_ge, fill=0.0,
                               base=Q - 1, pattern=[[0, 1]], channel_multiplier=-1).then_inc(iot, 1)
            pool.affine_select(out=keep["sexp"][:, 1:2], in_=keep["sexp"][:, 1:2], compare_op=ALU.is_ge, fill=-1e4,
                               base=Q - 1, pattern=[[0, 1]], channel_multiplier=-1).then_inc(iot, 1)
            own = keep["own"]
            pool.memset(own[:], 1.0).then_inc(iot, 1)
            pool.wait_ge(iot, 7)
            pool.affine_select(out=own[:], in_=own[:], compare_op=ALU.is_ge, fill=0.0, base=0,
                               pattern=[[-NS, GE]], channel_multiplier=1).then_inc(iot, 1)
            pool.wait_ge(iot, 8)
            pool.affine_select(out=own[:], in_=own[:], compare_op=ALU.is_ge, fill=0.0, base=NS - 1,
                               pattern=[[NS, GE]], channel_multiplier=-1).then_inc(iot, 1)

        @block.scalar
        def _(act):
            act.wait_ge(in_, 64)
            act.activation(abc[:], abc[:], ACT.Sigmoid).then_inc(sg, 1)
            act.wait_ge(sg, 1)
            act.activation(lam[:], abc[:, 0, :, :], ACT.Ln).then_inc(sg, 1)
            for k in range(NBLK):
                act.wait_ge(argd, k + 1)
                act.activation(ex[:], ex[:], ACT.Exp).then_inc(expd, 1)

        @block.vector
        def _(dve):
            done = [0]

            def link(ins):
                done[0] += 1
                ins.then_inc(step, 1)
                dve.wait_ge(step, done[0])

            def tap(j):
                return cw[:, :, j:j + 1].to_broadcast([EB, NBLK, NS])

            tt = dve.tensor_tensor
            dve.wait_ge(in_, 64)
            dve.wait_ge(sg, 1)
            a = abc[:, 0, :, :]
            dve.memset(kr[:], 0.0)
            tt(t1[:], a, tap(3), ALU.mult)
            link(tt(cc[:], abc[:, 1, :, :], abc[:, 2, :, :], ALU.mult))
            link(tt(t1[:], t1[:], tap(2), ALU.add))
            link(tt(t1[:], t1[:], a, ALU.mult))
            link(tt(t1[:], t1[:], tap(1), ALU.add))
            link(tt(t1[:], t1[:], a, ALU.mult))
            link(tt(t1[:], t1[:], tap(0), ALU.add))
            dve.tensor_reduce(k3[:, 0, :], cc[:], AX.X, ALU.add)
            link(tt(c2[:], t1[:], cc[:], ALU.mult))
            link(tt(t2[:], cc[:], a, ALU.mult))
            dve.tensor_reduce(k3[:, 1, :], t2[:], AX.X, ALU.add)
            link(tt(t1[:], t2[:], a, ALU.mult))
            link(dve.tensor_reduce(k3[:, 2, :], t1[:], AX.X, ALU.add))
            for lag in range(3):
                col = kr[:, :, HALO + Q - 1 - lag]
                link(tt(col, k3[:, lag, :], cw[:, :, 3], ALU.mult))
                for j in range(1, lag + 1):
                    link(tt(u3[:], k3[:, lag - j, :], cw[:, :, 3 - j], ALU.mult))
                    link(tt(col, col, u3[:], ALU.add))
            dve.wait_ge(sg, 2)
            dve.wait_ge(iot, 9)
            for k in range(NBLK):
                tt(ex[:], lam[:, k, :].unsqueeze(2).to_broadcast([EB, NS, Q]),
                   mex[:, :].unsqueeze(1).to_broadcast([EB, NS, Q]), ALU.mult).then_inc(argd, 1)
                dve.wait_ge(expd, k + 1)
                link(tt(ex[:], ex[:], c2[:, k, :].unsqueeze(2).to_broadcast([EB, NS, Q]), ALU.mult))
                link(dve.tensor_reduce(kr[:, k, 0:Q], ex[:].rearrange("p n q -> p q n"), AX.X, ALU.add))
            dve.sem_inc(done_k, 1)


def hold(eng, tick):
    eng.sem_inc(tick, 1)


def normalise_in(nc, io, dr, keep, xn):
    with ExitStack() as ctx:
        def sb(name, shape, dt=F32):
            return ctx.enter_context(nc.sbuf_tensor(name, shape, dt))

        def sem(name):
            return ctx.enter_context(nc.semaphore(name))

        h = sb("h4", [CB, Q, D])
        st = sb("st4", [CB, Q, 6])
        mv = sb("mv4", [CB, Q, 2])
        rms = sb("rms4", [CB, Q])
        zs = sb("zs4", [CB, Q])
        nz = sb("nz4", [CB, Q])
        z = [sb(f"z4{j}", [CB, D]) for j in range(2)]
        wi = keep["wi"]
        gam = sb("gam4", [HD, 2])
        win_row = sb("win_row", [128, E // 128, D])
        wout_row = sb("wout_row", [HD, 2, E])
        pz = [bank(nc, ctx, f"pz{j}", [HD, 2, CB]) for j in range(2)]
        h_in = sem("h_in")
        w_in = sem("w4_in")
        step = sem("s4")
        var_ok = sem("var4")
        root = sem("root4")
        zs_ok = sem("zs4s")
        ready = [sem("z_ready0"), sem("z_ready1")]
        turned = [sem("z_turned0"), sem("z_turned1")]
        taken = [sem("z_taken0"), sem("z_taken1")]
        ones = sem("ones4")
        tick = sem("tick4")
        block = ctx.enter_context(nc.Block())
        mu, rs = keep["mu"], keep["rs"]
        NQ = 2

        def scatter_cols(t):
            full = xn[0:HD, :, :, :]
            return full[:, :, :, HALO:HALO + LP].rearrange("p k b (c t) -> p k b c t", c=NCHUNK)[:, :, :, :, bass.ds(t, 1)]

        @block.sync
        def _(sp):
            hv = dr["h0"].rearrange("(p t) d -> p t d", t=Q)
            for n in range(NQ):
                k = Q // NQ
                sp.dma_start(h[:, n * k:(n + 1) * k, :], hv[:, n * k:(n + 1) * k, :]).then_inc(h_in, 16)
            with nc.allow_non_contiguous_dma(reason="weights, transposed once"):
                sp.dma_start(gam[:], io["L0_attn_gamma"].rearrange("(k p) -> p k", p=HD)).then_inc(w_in, 16)
            sp.dma_start(win_row[:, :, :], io["L0_attn_W_in"].rearrange("(k p) d -> p k d", p=128)).then_inc(w_in, 16)
            sp.dma_start(wi[HD:HD + 1, 1, :], io["L0_attn_b_in"].unsqueeze(0)).then_inc(w_in, 16)
            for n in range(2):
                sp.dma_start(wout_row[:, n, :], io["L0_attn_W_out"][n * HD:(n + 1) * HD, :]).then_inc(w_in, 16)
            sp.dma_start(keep["wo"][EB:EB + 1, NBLK - 1, :], io["L0_attn_b_out"].unsqueeze(0)).then_inc(w_in, 16)
            sp.wait_ge(w_in, 96)

        @block.gpsimd
        def _(pool):
            pool.memset(xn[0:HD, :, :, 0:HALO], 0.0).then_inc(ones, 1)
            pool.wait_ge(ones, 1)
            pool.memset(xn[HD:HD + 1, 1, :, HALO:], 1.0).then_inc(ones, 1)
            pool.memset(xn[HD:HD + 1, 1, :, 0:HALO], 0.0).then_inc(ones, 1)

        @block.vector
        def _(dve):
            done = [0]

            def link(ins):
                done[0] += 1
                ins.then_inc(step, 1)
                dve.wait_ge(step, done[0])

            tt = dve.tensor_tensor
            for n in range(NQ):
                k = Q // NQ
                dve.wait_ge(h_in, 16 * NQ)
                with dve.Fori(n * k, (n + 1) * k) as t:
                    dve.bn_stats(st[:, bass.ds(t, 1), :].rearrange("p a s -> p (a s)"),
                                 h[:, bass.ds(t, 1), :].rearrange("p a d -> p (a d)"))
            link(dve.memset(zs[:], 0.0))
            for t in range(Q):
                dve.bn_aggr(mv[:, t, :], st[:, t, :])
            link(dve.memset(nz[:], 0.0))
            dve.tensor_copy(mu[:], mv[:, :, 0])
            dve.tensor_copy(rms[:], mv[:, :, 1])
            dve.tensor_scalar(rs[:], mv[:, :, 1], EPS, None, ALU.add).then_inc(var_ok, 1)
            dve.wait_ge(root, 2)
            link(dve.reciprocal(rs[:], rs[:]))
            link(tt(rms[:], rms[:], rs[:], ALU.mult))
            link(dve.tensor_scalar(rms[:], rms[:], 1e-6, None, ALU.add))
            link(dve.reciprocal(rms[:], rms[:]))
            link(tt(zs[:], rms[:], rs[:], ALU.mult))
            dve.scalar_tensor_tensor(out=nz[:], in0=mu[:], scalar=-1.0, in1=zs[:], op0=ALU.mult, op1=ALU.mult
                                     ).then_inc(zs_ok, 1)
            dve.wait_ge(zs_ok, 1)

            def make(t):
                dve.tensor_scalar(z[1][:], h[:, bass.ds(t, 1), :].rearrange("p a d -> p (a d)"),
                                  zs[:, bass.ds(t, 1)], nz[:, bass.ds(t, 1)], ALU.mult, ALU.add).then_inc(ready[1], 1)

            make(1)
            with dve.Fori(0, Q // 2 - 1) as p:
                dve.wait_ge(turned[1], p + 1)
                make(2 * p + 3)
                dve.tensor_copy(scatter_cols(2 * p + 1), pz[1][:].rearrange("p k (b c) -> p k b c", c=NCHUNK).unsqueeze(4)
                                ).then_inc(taken[1], 1)
            dve.wait_ge(turned[1], Q // 2)
            dve.tensor_copy(scatter_cols(Q - 1), pz[1][:].rearrange("p k (b c) -> p k b c", c=NCHUNK).unsqueeze(4)
                            ).then_inc(taken[1], 1)
            dve.wait_ge(taken[1], Q // 2)

        @block.scalar
        def _(act):
            act.wait_ge(var_ok, 1)
            act.activation(rs[:], rs[:], ACT.Sqrt).then_inc(root, 1)
            act.activation(rms[:], rms[:], ACT.Sqrt).then_inc(root, 1)
            act.wait_ge(zs_ok, 1)

            def make(t):
                act.activation(z[0][:], h[:, bass.ds(t, 1), :].rearrange("p a d -> p (a d)"), ACT.Identity,
                               scale=zs[:, bass.ds(t, 1)], bias=nz[:, bass.ds(t, 1)]).then_inc(ready[0], 1)

            make(0)
            with act.Fori(0, Q // 2 - 1) as p:
                act.wait_ge(turned[0], p + 1)
                hold(act, tick)
                make(2 * p + 2)
                act.activation(scatter_cols(2 * p), pz[0][:].rearrange("p k (b c) -> p k b c", c=NCHUNK).unsqueeze(4),
                               ACT.Copy).then_inc(taken[0], 1)
            act.wait_ge(turned[0], Q // 2)
            act.activation(scatter_cols(Q - 2), pz[0][:].rearrange("p k (b c) -> p k b c", c=NCHUNK).unsqueeze(4),
                           ACT.Copy).then_inc(taken[0], 1)
            act.wait_ge(w_in, 96)
            for n in range(6):
                act.wait_ge(turned[0], Q // 2 + n + 1)
                src, k, m = pz[0][:, 0, :], n // 3, n % 3
                act.activation(wi[0:HD, k, m * 128:(m + 1) * 128], src, ACT.Identity, scale=gam[:, k:k + 1]
                               ).then_inc(taken[0], 1)
            for n in range(2 * NBLK):
                act.wait_ge(turned[0], Q // 2 + 6 + n + 1)
                k, m = n // 2, n % 2
                act.activation(keep["wo"][0:EB, k, m * HD:(m + 1) * HD], pz[0][:, 0, 0:HD], ACT.Copy
                               ).then_inc(taken[0], 1)

        @block.tensor
        def _(pe):
            for j in range(2):
                pe.sem_inc(taken[j], 1)
            with pe.Fori(0, Q // 2) as p:
                for j in range(2):
                    pe.wait_ge(ready[j], p + 1)
                    pe.wait_ge(taken[j], p + 1)
                    for k in range(2):
                        t = pe.transpose(pz[j][:, k, :], z[j][:, k * HD:(k + 1) * HD], keep["ident"][:])
                    t.then_inc(turned[j], 1)
            pe.wait_ge(w_in, 96)
            for n in range(6):
                k, m = n // 3, n % 3
                pe.wait_ge(taken[0], Q // 2 + n + 1)
                pe.transpose(pz[0][:, 0, :], win_row[:, m, k * HD:(k + 1) * HD], keep["ident"][:]
                             ).then_inc(turned[0], 1)
            for n in range(2 * NBLK):
                k, m = n // 2, n % 2
                pe.wait_ge(taken[0], Q // 2 + 6 + n + 1)
                pe.transpose(pz[0][0:EB, 0, 0:HD], wout_row[:, m, k * EB:(k + 1) * EB],
                             keep["ident"][0:HD, 0:HD]).then_inc(turned[0], 1)


XU = CB // 4
IU = EB // 4
TU = [4] * 10 + [3] * 14
UNITS = XU + IU + len(TU)
PARTS = IU


def mix(nc, io, dr, keep, xn):
    with ExitStack() as ctx:
        def sb(name, shape, dt=F32):
            return ctx.enter_context(nc.sbuf_tensor(name, shape, dt))

        def sem(name):
            return ctx.enter_context(nc.semaphore(name))

        x = sb("x5", [W, CB, EB])
        y = sb("y5", [CB, EB, Q])
        gp = [sb(f"gp{j}", [96, GE * GPW + 32]) for j in range(2)]
        lg = [sb(f"lg{j}", [96, GE * NS]) for j in range(2)]
        sm = [sb(f"sm{j}", [CB, GE * NS]) for j in range(2)]
        ht = [sb(f"hs{j}", [128, B, NCHUNK]) for j in range(2)]
        rr = [sb(f"rr{j}", [128, Q]) for j in range(2)]
        bd = [sb(f"bd{j}", [128, GE, Q]) for j in range(2)]
        mc = sb("mc5", [128, NBLK * NG, GE])
        aq = sb("aq5", [128, NBLK * NG])
        yt = [sb(f"yt{j}", [EB, 4, CB]) for j in range(4)]
        pa = [bank(nc, ctx, f"pa{j}", [128, 4, 128]) for j in range(4)]
        pst = bank(nc, ctx, "pst", [128, B, NCHUNK])
        pb = [bank(nc, ctx, f"pb{j}", [128, 4, Q]) for j in range(2)]

        setup = sem("set5")
        aq_ok = sem("aq_ok")
        g_in = [sem("g_in0"), sem("g_in1")]
        p_ok = sem("p_ok")
        unit = sem("unit")
        free = [sem("free_act"), sem("free_dve")]
        s_ok = [sem("s_ok_act"), sem("s_ok_dve")]
        st_ok = sem("st_ok")
        h_ok = sem("h_ok")
        r_ok = sem("r_ok")
        bd_ok = sem("bd_ok")
        inter = sem("inter")
        added = sem("added")
        step = sem("s5")
        stored = [sem(f"yst{j}") for j in range(4)]
        tick = sem("tick5")
        tick_p = sem("tick5p")
        tick_s = sem("tick5s")
        block = ctx.enter_context(nc.Block())
        own, lamc, c2c, texp, sexp = (keep[k] for k in ("own", "lamc", "c2c", "texp", "sexp"))

        def cols(j, e):
            return gp[j][0:W, e * GPW:e * GPW + 128]

        @block.sync
        def _(sp):
            def load(k, g):
                j = g % 2
                last = XU + 2 * (g - 1) + UNITS if g >= 2 else XU + 2 * (NG + g - 1)
                sp.wait_ge(unit, k * UNITS + last)
                hold(sp, tick_s)
                first = k * EB + g * GE
                src = bass.AP(tensor=dr["kd"].tensor, offset=first * KREV, ap=[[1, 96], [KREV, GE], [1, Q]])
                sp.dma_start(gp[j][:, 0:GE * GPW].rearrange("r (e q) -> r e q", q=GPW)[:, :, 0:Q], src
                             ).then_inc(g_in[j], 16)
                lamsrc = bass.AP(tensor=dr["lamd"].tensor, offset=first * NS, ap=[[0, 96], [1, GE * NS]])
                sp.dma_start(lg[j][:], lamsrc).then_inc(g_in[j], 16)

            def store(k, n):
                t0 = sum(TU[:n])
                sp.wait_ge(free[n % 2], (k + 1) * (UNITS // 2) - len(TU) // 2 + n // 2 + 3)
                hold(sp, tick_s)
                sp.dma_start(dr["yd"][bass.ds(k * EB, EB), t0 * CB:(t0 + TU[n]) * CB],
                             yt[n % 4][:, 0:TU[n], :].rearrange("e t c -> e (t c)")).then_inc(stored[n % 4], 16)

            with sp.Fori(0, NBLK) as k:
                for g in range(NG):
                    load(k, g)
                for n in range(len(TU)):
                    store(k, n)
            for j in range(4):
                sp.wait_ge(stored[j], 16 * (NBLK * len(TU) // 4 + 1))

        @block.gpsimd
        def _(pool):
            for j in range(2):
                pool.memset(gp[j][:, GE * GPW:], 0.0).then_inc(setup, 1)
                pool.memset(ht[j][:, :, 0], 0.0).then_inc(setup, 1)
            pool.tensor_tensor(mc[:], own[:, :].unsqueeze(1).to_broadcast([128, NBLK * NG, GE]),
                               c2c[:, :].unsqueeze(2).to_broadcast([128, NBLK * NG, GE]), ALU.mult).then_inc(setup, 1)
            pool.wait_ge(setup, 5)
            pool.sem_inc(inter, 4)
            with pool.Fori(0, NBLK) as k:
                for g in range(NG):
                    n = k * NG + g
                    pool.wait_ge(r_ok, n + 1)
                    hold(pool, tick_p)
                    pool.wait_ge(inter, 2 * n + 2)
                    hold(pool, tick_p)
                    pool.tensor_tensor(bd[g % 2][:], rr[g % 2][:, :].unsqueeze(1).to_broadcast([128, GE, Q]),
                                       mc[:, bass.ds(n, 1), :].rearrange("p a e -> p (a e)").unsqueeze(2)
                                       .to_broadcast([128, GE, Q]), ALU.mult).then_inc(bd_ok, 1)

        def read_unit(eng, copy, k, m, who):
            eng.wait_ge(unit, (k + 1) * UNITS + m + 1)
            hold(eng, tick)
            p = pa[m % 4]
            if m < XU:
                copy(x[:, 4 * m:4 * m + 4, :].rearrange("w c e -> w (c e)"),
                     p[0:W, :, :].rearrange("w a b -> w (a b)")[:, 0:4 * EB]).then_inc(free[who], 1)
            elif m < XU + IU:
                n = m - XU
                g = n // 2
                eng.wait_ge(st_ok, k * NG + g + 1)
                copy(sm[g % 2][:, (n % 2) * 64:(n % 2) * 64 + 64].rearrange("c (e n) -> c e n", n=NS),
                     p[:, :, Q:GPW]).then_inc(s_ok[who], 1)
                copy(y[:, 4 * n:4 * n + 4, :], p[:, :, 0:Q]).then_inc(free[who], 1)
            else:
                n = m - XU - IU
                q = n % 4
                eng.wait_ge(stored[q], 16 * (k * (len(TU) // 4) + n // 4 + 1))
                copy(yt[q][:, 0:TU[n], :], p[0:EB, 0:TU[n], :]).then_inc(free[who], 1)

        @block.scalar
        def _(act):
            def copy(out, in_):
                return act.activation(out, in_, ACT.Copy)

            def tables(k, g):
                n = k * NG + g
                j = g % 2
                act.wait_ge(g_in[j], 32 * (k * (NG // 2) + g // 2 + 1))
                hold(act, tick)
                act.activation(gp[j][:, 0:GE * GPW].rearrange("r (e q) -> r e q", q=GPW)[:, :, Q:GPW],
                               lg[j][:, :].rearrange("r (e n) -> r e n", n=NS), ACT.Exp,
                               scale=sexp[:, 0:1], bias=sexp[:, 1:2]).then_inc(p_ok, 1)
                act.wait_ge(bd_ok, n + 1)
                hold(act, tick)
                act.activation(rr[j][:], texp[:, :], ACT.Exp, scale=lamc[:, bass.ds(n, 1)]).then_inc(r_ok, 1)

            act.activation(aq[:], lamc[:], ACT.Exp, scale=float(Q)).then_inc(aq_ok, 1)
            act.sem_inc(bd_ok, 2)
            act.sem_inc(st_ok, 2)
            act.sem_inc(stored[0], 16)
            act.sem_inc(stored[2], 16)
            with act.Fori(0, NBLK) as k:
                for m in range(0, XU, 2):
                    read_unit(act, copy, k, m, 0)
                tables(k, 0)
                tables(k, 1)
                for g in range(NG):
                    read_unit(act, copy, k, XU + 2 * g, 0)
                    if g + 2 < NG:
                        tables(k, g + 2)
                for m in range(XU + IU, UNITS, 2):
                    read_unit(act, copy, k, m, 0)

        @block.vector
        def _(dve):
            def carry(k, g):
                n = k * NG + g
                j = g % 2
                dve.wait_ge(st_ok, n + 3)
                dve.wait_ge(inter, 2 * n + 2)
                hold(dve, tick)
                dve.tensor_copy(ht[j][:, :, 1], pst[:, :, 0]).then_inc(step, 1)
                for c in range(2, NCHUNK):
                    dve.wait_ge(step, 3 * n + c - 1)
                    ins = dve.scalar_tensor_tensor(out=ht[j][:, :, c], in0=ht[j][:, :, c - 1],
                                                   scalar=aq[:, bass.ds(n, 1)], in1=pst[:, :, c - 1],
                                                   op0=ALU.mult, op1=ALU.add)
                    ins.then_inc(step, 1)
                dve.wait_ge(step, 3 * n + 3)
                hold(dve, h_ok)

            def add(k, g):
                n = k * NG + g
                for q in range(2):
                    dve.wait_ge(inter, 2 * n + q + 5)
                    dve.wait_ge(free[q], k * (UNITS // 2) + XU // 2 + g + 3)
                    hold(dve, tick)
                    e0 = g * GE + 4 * q
                    dve.tensor_tensor(y[:, e0:e0 + 4, :], y[:, e0:e0 + 4, :], pb[q][:], ALU.add).then_inc(added, 1)

            dve.sem_inc(stored[1], 16)
            dve.sem_inc(stored[3], 16)
            dve.wait_ge(setup, 5)
            dve.wait_ge(aq_ok, 1)
            with dve.Fori(0, NBLK) as k:
                for m in range(1, XU, 2):
                    read_unit(dve, dve.tensor_copy, k, m, 1)
                for g in range(NG):
                    read_unit(dve, dve.tensor_copy, k, XU + 2 * g + 1, 1)
                    if g >= 1:
                        carry(k, g - 1)
                    if g >= 2:
                        add(k, g - 2)
                carry(k, NG - 1)
                add(k, NG - 2)
                add(k, NG - 1)
                for m in range(XU + IU + 1, UNITS, 2):
                    read_unit(dve, dve.tensor_copy, k, m, 1)

        @block.tensor
        def _(pe):
            ident = keep["ident"]

            def bank(k, m):
                pe.wait_ge(free[m % 2], k * (UNITS // 2) + m // 2 + 1)
                return pa[m % 4]

            def turn_states(k, g):
                n = k * NG + g
                for who in range(2):
                    pe.wait_ge(s_ok[who], n + 1)
                pe.wait_ge(h_ok, n + 1)
                pe.transpose(pst[:, :, :].rearrange("s b c -> s (b c)"), sm[g % 2][:], ident[:]).then_inc(st_ok, 1)

            def reach(k, g):
                n = k * NG + g
                pe.wait_ge(h_ok, n + 2)
                pe.wait_ge(bd_ok, n + 3)
                for q in range(2):
                    pe.wait_ge(added, 2 * n + q + 1)
                    pe.matmul(pb[q][:].rearrange("c e t -> c (e t)"), ht[g % 2][:].rearrange("s b c -> s (b c)"),
                              bd[g % 2][:, 4 * q:4 * q + 4, :].rearrange("s e t -> s (e t)"),
                              start=True, stop=True).then_inc(inter, 1)

            pe.sem_inc(unit, UNITS)
            pe.sem_inc(free[0], 2)
            pe.sem_inc(free[1], 2)
            pe.sem_inc(h_ok, 1)
            pe.sem_inc(added, 2)
            pe.wait_ge(setup, 5)
            with pe.Fori(0, NBLK) as k:
                for m in range(XU):
                    p = bank(k, m)[0:W, :, :].rearrange("w a b -> w (a b)")
                    for i in range(4):
                        b, c = divmod(4 * m + i, NCHUNK)
                        for f in range(2):
                            rows = HD + f
                            mm = pe.matmul(p[:, i * EB:(i + 1) * EB], xn[0:rows, f, b, c * Q:c * Q + W],
                                           keep["wi"][0:rows, f, bass.ds(k * EB, EB)],
                                           start=(f == 0), stop=(f == 1))
                    mm.then_inc(unit, 1)
                for who in range(2):
                    pe.wait_ge(free[who], k * (UNITS // 2) + XU // 2 + 2)
                for g in range(NG):
                    pe.wait_ge(p_ok, k * NG + g + 1)
                    for q in range(2):
                        p = bank(k, XU + 2 * g + q)
                        for i in range(4):
                            e = 4 * q + i
                            mm = pe.matmul(p[:, i, :], x[:, :, g * GE + e], cols(g % 2, e), start=True, stop=True)
                        mm.then_inc(unit, 1)
                    if g >= 1:
                        turn_states(k, g - 1)
                    if g >= 2:
                        reach(k, g - 2)
                turn_states(k, NG - 1)
                reach(k, NG - 2)
                reach(k, NG - 1)
                pe.wait_ge(added, 2 * (k * NG + NG) + 2)
                t0 = 0
                for n, size in enumerate(TU):
                    p = bank(k, XU + IU + n)
                    for i in range(size):
                        tr = pe.transpose(p[0:EB, i, :], y[:, :, t0 + i], ident[:])
                    tr.then_inc(unit, 1)
                    t0 += size


def project_route(nc, io, dr, keep, late):
    with ExitStack() as ctx:
        def sb(name, shape, dt=F32):
            return ctx.enter_context(nc.sbuf_tensor(name, shape, dt))

        def sem(name):
            return ctx.enter_context(nc.semaphore(name))

        h1 = sb("h1", [CB, Q, ROW])
        hb = [sb(f"hb{j}", [CB, 2, D]) for j in range(2)]
        yt = [sb(f"y6{j}", [EB + 1, NBLK, 2, CB]) for j in range(2)]
        s1 = sb("s1", [CB, Q])
        s2 = sb("s2", [CB, Q])
        st = sb("st6", [CB, Q, 6])
        mv = sb("mv6", [CB, Q, 2])
        rs2 = sb("rs2", [CB, Q])
        nm2 = sb("nm2", [CB, Q])
        z = [sb(f"z6{j}", [CB, D]) for j in range(2)]
        zt = [sb(f"zt{j}", [HD + 1, 2, CB]) for j in range(2)]
        ws = sb("ws", [HD + 1, 2, NEX])
        lgt = sb("lgt6", [CB, Q, NEX])
        mx = sb("mx", [CB, Q])
        ex = sb("ex6", [CB, Q, NEX])
        oh = sb("oh", [CB, NEX, Q])
        inc = sb("inc", [CB, NEX, Q])
        one = sb("one6", [CB, Q])
        rank = sb("rank", [CB, NEX])
        tot = sb("tot", [CB, NEX])
        sbase = sb("sbase", [CB, NEX])
        tiles = sb("tiles", [CB, NEX])
        tint = sb("tint", [CB, NEX], I32)
        tend = sb("tend", [CB, NEX])
        slot = sb("slot", [CB, Q])
        sloti = sb("sloti", [CB, Q], I32)
        pid = sb("pid", [CB, 1], I32)
        pcol = sb("pcol", [CB, 4], F32)
        pint = sb("pint", [CB, 2], I32)
        tio = sb("tio", [CB, Q])
        cmp_ = sb("cmp", [1, NTILE, NEX])
        tie = sb("tie", [1, NTILE])
        po = [bank(nc, ctx, f"p6{j}", [CB, 2, 256]) for j in range(2)]
        pz = [bank(nc, ctx, f"pz6{j}", [HD, 2, CB]) for j in range(2)]
        T0 = 64
        pl = [bank(nc, ctx, f"pl{j}", [CB, T0, NEX]) for j in range(2)]
        pc = bank(nc, ctx, "pc6", [CB, 2, NEX])

        y_in = [sem("y_in0"), sem("y_in1")]
        w_in = sem("w6_in")
        iot = sem("iot6")
        sc_ok = sem("sc_ok")
        hb_ok = sem("hb_ok")
        out_ok = sem("out_ok")
        h_done = sem("h_done")
        step = sem("s6")
        var_ok = sem("var6")
        root = sem("root6")
        rs_ok = sem("rs6")
        ready = [sem("r_z0"), sem("r_z1")]
        turned = [sem("t_z0"), sem("t_z1")]
        taken = [sem("k_z0"), sem("k_z1")]
        routed = [sem("q_z0"), sem("q_z1")]
        lmx = sem("lmx")
        lex = sem("lex")
        tot_ok = sem("tot_ok")
        cnt_ok = sem("cnt_ok")
        rows_ok = sem("rows_ok")
        sent = sem("sent")
        wl = keep["wl"]
        tick = sem("tick6")
        tick_s = sem("tick6s")
        block = ctx.enter_context(nc.Block())
        mu, rs = keep["mu"], keep["rs"]
        NP = Q // 2
        w1, w2, b2 = late["w1"], late["w2"], late["b2"]

        def pairs(eng, body):
            with eng.Fori(0, NP // 2) as i:
                for j in range(2):
                    body(2 * i + j, j)
            body(NP - 1, 0)

        @block.sync
        def _(sp):
            ydv = dr["yd"].rearrange("(k p) (t c) -> p k t c", p=EB, c=CB)
            hv = dr["h0"].rearrange("(p t) d -> p t d", t=Q)

            def load(p, j):
                sp.wait_ge(h_done, p + 1)
                hold(sp, tick_s)
                for k in range(NBLK):
                    sp.dma_start(yt[j][0:EB, k, :, :], ydv[:, k, bass.ds(Q - 2 - 2 * p, 2), :]).then_inc(y_in[j], 16)
                sp.dma_start(hb[j][:], hv[:, bass.ds(2 * p, 2), :]).then_inc(y_in[j], 16)

            sp.sem_inc(h_done, 2)
            pairs(sp, load)

        @block.gpsimd
        def _(pool):
            for j in range(2):
                pool.memset(yt[j][EB:EB + 1, :, :, :], 1.0).then_inc(iot, 1)
                pool.memset(zt[j][HD:HD + 1, :, :], 1.0).then_inc(iot, 1)
            pool.wait_ge(iot, 4)
            pool.memset(one[:], 1.0).then_inc(iot, 1)
            pool.iota(pid[:], pattern=[[0, 1]], base=0, channel_multiplier=1).then_inc(iot, 1)
            pool.iota(tio[:], pattern=[[1, Q]], base=0, channel_multiplier=0,
                      allow_small_or_imprecise_dtypes=True).then_inc(iot, 1)
            pool.iota(tie[:], pattern=[[1, NTILE]], base=0, channel_multiplier=0,
                      allow_small_or_imprecise_dtypes=True).then_inc(iot, 1)
            bound = pool.to_reg(SLOTS - 1)
            pool.wait_ge(rows_ok, 1)
            for t in range(Q):
                pool.indirect_dma_start(dr["xs"], bass.IndirectOffsetOnAxis(ap=sloti[:, t:t + 1], axis=0),
                                        h1[:, t, :], None, bounds_check=bound, oob_is_err=False).then_inc(sent, 16)
            pool.wait_ge(sent, 16 * Q)

        @block.scalar
        def _(act):
            act.dma_start(ws[0:HD, 0, :], io["L0_ffn_Ws"][0:HD, :]).then_inc(w_in, 16)
            act.dma_start(ws[0:HD, 1, :], io["L0_ffn_Ws"][HD:D, :]).then_inc(w_in, 16)
            act.dma_start(ws[HD:HD + 1, 1, :], io["L0_ffn_bs"].unsqueeze(0)).then_inc(w_in, 16)
            for k in range(2):
                act.dma_start(w1[0:HD, k, :].rearrange("p (e f) -> p e f", e=NEX),
                              io["L0_ffn_W1"][:, k * HD:(k + 1) * HD, :].rearrange("e p f -> p e f")).then_inc(wl, 16)
            act.dma_start(w1[HD:HD + 1, 1, :], io["L0_ffn_b1"].rearrange("e f -> (e f)").unsqueeze(0)).then_inc(wl, 16)
            for k in range(FC):
                act.dma_start(w2[:, k, :].rearrange("p (e d) -> p e d", e=NEX),
                              io["L0_ffn_W2"][:, k * 128:(k + 1) * 128, :].rearrange("e p d -> p e d")).then_inc(wl, 16)
            act.dma_start(b2[:, :], io["L0_ffn_b2"].rearrange("e d -> (e d)").partition_broadcast(128)).then_inc(wl, 16)

            def residual(t, j):
                for k in range(2):
                    a = act.activation(hb[j][:, k, :], hb[j][:, k, :], ACT.Identity,
                                       scale=s1[:, bass.ds(t + k, 1)], bias=s2[:, bass.ds(t + k, 1)])
                a.then_inc(hb_ok, 1)

            act.wait_ge(sc_ok, 1)
            with act.Fori(0, NP // 2) as i:
                for j in range(2):
                    act.wait_ge(y_in[j], 16 * (NBLK + 1) * (i + 1))
                    hold(act, tick)
                    residual(4 * i + 2 * j, j)
            act.wait_ge(y_in[0], 16 * (NBLK + 1) * (NP // 2 + 1))
            residual(Q - 2, 0)
            act.wait_ge(var_ok, 1)
            act.activation(rs2[:], rs2[:], ACT.Sqrt).then_inc(root, 1)
            act.wait_ge(rs_ok, 1)

            def make(t):
                act.activation(z[0][:], h1[:, bass.ds(t, 1), 0:D].rearrange("p a d -> p (a d)"), ACT.Identity,
                               scale=rs2[:, bass.ds(t, 1)], bias=nm2[:, bass.ds(t, 1)]).then_inc(ready[0], 1)

            make(0)
            with act.Fori(0, NP - 1) as p:
                act.wait_ge(turned[0], p + 1)
                hold(act, tick)
                make(2 * p + 2)
                act.wait_ge(routed[0], p + 1)
                hold(act, tick)
                act.activation(zt[0][0:HD, :, :], pz[0][:], ACT.Copy).then_inc(taken[0], 1)
            act.wait_ge(turned[0], NP)
            act.wait_ge(routed[0], NP)
            act.activation(zt[0][0:HD, :, :], pz[0][:], ACT.Copy).then_inc(taken[0], 1)
            act.wait_ge(lmx, 1)
            act.activation(ex[:], ex[:], ACT.Exp).then_inc(lex, 1)

        @block.tensor
        def _(pe):
            def project(p, j, use):
                pe.wait_ge(y_in[j], 16 * (NBLK + 1) * (use + 1))
                pe.wait_ge(h_done, p + 1)
                for i in range(2):
                    for k in range(NBLK):
                        rows = EB + (k == NBLK - 1)
                        m = pe.matmul(po[j][:, i, 0:D], yt[j][0:rows, k, 1 - i, :], keep["wo"][0:rows, k, :],
                                      start=(k == 0), stop=(k == NBLK - 1))
                m.then_inc(out_ok, 1)

            pe.wait_ge(iot, 8)
            with pe.Fori(0, NP // 2) as i:
                for j in range(2):
                    project(2 * i + j, j, i)
            project(NP - 1, 0, NP // 2)
            for j in range(2):
                pe.sem_inc(taken[j], 1)
                pe.sem_inc(routed[j], 1)
            pe.wait_ge(w_in, 48)

            def turn(p, j):
                pe.wait_ge(ready[j], p + 1)
                pe.wait_ge(taken[j], p + 1)
                for k in range(2):
                    t = pe.transpose(pz[j][:, k, :], z[j][:, k * HD:(k + 1) * HD], keep["ident"][:])
                t.then_inc(turned[j], 1)

            def logits(p, j, bank, t0):
                pe.wait_ge(taken[j], p + 2)
                for k in range(2):
                    m = pe.matmul(pl[bank][:, bass.ds(2 * p + j - t0, 1), :].rearrange("c a e -> c (a e)"),
                                  zt[j][0:HD + k, k, :], ws[0:HD + k, k, :], start=(k == 0), stop=(k == 1))
                m.then_inc(routed[j], 1)

            turn(0, 0)
            turn(0, 1)
            for bank, lo, hi in ((0, 0, T0 // 2), (1, T0 // 2, NP - 1)):
                with pe.Fori(lo, hi) as p:
                    for j in range(2):
                        logits(p, j, bank, bank * T0)
                        turn(p + 1, j)
            for j in range(2):
                logits(NP - 1, j, 1, T0)
            pe.wait_ge(tot_ok, 1)
            pe.matmul(pc[:, 0, :], keep["before"][:], tot[:], start=True, stop=True)
            pe.matmul(pc[:, 1, :], keep["ones"][:], tot[:], start=True, stop=True).then_inc(cnt_ok, 1)

        @block.vector
        def _(dve):
            done = [0]

            def link(ins):
                done[0] += 1
                ins.then_inc(step, 1)
                dve.wait_ge(step, done[0])

            tt, ts = dve.tensor_tensor, dve.tensor_scalar
            ts(s1[:], rs[:], 1.0, None, ALU.add)
            dve.scalar_tensor_tensor(out=s2[:], in0=mu[:], scalar=-1.0, in1=rs[:], op0=ALU.mult, op1=ALU.mult
                                     ).then_inc(sc_ok, 1)

            def finish(p, j):
                dve.wait_ge(hb_ok, p + 1)
                dve.wait_ge(out_ok, p + 1)
                tt(h1[:, bass.ds(2 * p, 2), 0:D], hb[j][:], po[j][:, :, 0:D], ALU.add).then_inc(h_done, 1)

            pairs(dve, finish)
            dve.wait_ge(h_done, NP + 2)
            with dve.Fori(0, Q) as t:
                dve.bn_stats(st[:, bass.ds(t, 1), :].rearrange("p a s -> p (a s)"),
                             h1[:, bass.ds(t, 1), 0:D].rearrange("p a d -> p (a d)"))
            link(dve.memset(nm2[:], 0.0))
            for t in range(Q):
                dve.bn_aggr(mv[:, t, :], st[:, t, :])
            link(dve.memset(mx[:], 0.0))
            ts(rs2[:], mv[:, :, 1], EPS, None, ALU.add).then_inc(var_ok, 1)
            dve.wait_ge(root, 1)
            link(dve.reciprocal(rs2[:], rs2[:]))
            dve.scalar_tensor_tensor(out=nm2[:], in0=mv[:, :, 0], scalar=-1.0, in1=rs2[:], op0=ALU.mult, op1=ALU.mult
                                     ).then_inc(rs_ok, 1)
            dve.wait_ge(rs_ok, 1)
            dve.tensor_copy(h1[:, :, D], mv[:, :, 0])
            dve.tensor_copy(h1[:, :, D + 1], rs2[:])

            def make(t):
                ts(z[1][:], h1[:, bass.ds(t, 1), 0:D].rearrange("p a d -> p (a d)"), rs2[:, bass.ds(t, 1)],
                   nm2[:, bass.ds(t, 1)], ALU.mult, ALU.add).then_inc(ready[1], 1)

            make(1)
            with dve.Fori(0, NP - 1) as p:
                dve.wait_ge(turned[1], p + 1)
                make(2 * p + 3)
                dve.wait_ge(routed[1], p + 1)
                dve.tensor_copy(zt[1][0:HD, :, :], pz[1][:]).then_inc(taken[1], 1)
            dve.wait_ge(turned[1], NP)
            dve.wait_ge(routed[1], NP)
            dve.tensor_copy(zt[1][0:HD, :, :], pz[1][:]).then_inc(taken[1], 1)
            for j in range(2):
                dve.wait_ge(routed[j], NP + 1)
            dve.tensor_copy(lgt[:, 0:T0, :], pl[0][:])
            link(dve.tensor_copy(lgt[:, T0:Q, :], pl[1][:, 0:Q - T0, :]))
            link(dve.tensor_reduce(mx[:], lgt[:], AX.X, ALU.max))
            link(tt(lgt[:], lgt[:], mx[:, :].unsqueeze(2).to_broadcast([CB, Q, NEX]), ALU.subtract))
            dve.tensor_copy(ex[:], lgt[:]).then_inc(lmx, 1)
            link(ts(lgt[:], lgt[:], 0.0, None, ALU.is_ge))
            seen = mx
            lv = lgt[:].rearrange("c q e -> c e q")
            dve.memset(seen[:], 1.0)
            dve.memset(one[:], 1.0)
            link(dve.memset(tot[:], 0.0))
            for e in range(NEX):
                link(tt(oh[:, e, :], lv[:, e, :], seen[:], ALU.mult))
                link(tt(seen[:], seen[:], oh[:, e, :], ALU.subtract))
            dve.wait_ge(iot, 8)
            link(ts(pint[:, 0:1], pid[:], NCHUNK - 1, None, ALU.bitwise_and))
            link(ts(pint[:, 1:2], pid[:], 2, None, ALU.arith_shift_right))
            link(ts(pcol[:, 0:1], pint[:, 0:1], float(NCHUNK - 1), None, ALU.is_equal))
            link(ts(pcol[:, 1:2], pcol[:, 0:1], -1.0, 1.0, ALU.mult, ALU.add))
            link(ts(pcol[:, 2:3], pint[:, 1:2], float(L - LP), None, ALU.mult))
            dve.tensor_copy(pcol[:, 3:4], pid[:])
            link(ts(oh[:, :, Q - HALO:Q], oh[:, :, Q - HALO:Q], pcol[:, 1:2], None, ALU.mult))
            for e in range(NEX):
                s = dve.tensor_tensor_scan(inc[:, e, :], one[:], oh[:, e, :], 0.0, ALU.mult, ALU.add)
            link(s)
            dve.tensor_copy(tot[:], inc[:, :, Q - 1]).then_inc(tot_ok, 1)
            dve.wait_ge(cnt_ok, 1)
            link(ts(tint[:], pc[:, 1, :], 127.0, None, ALU.add))
            link(ts(tint[:], tint[:], 7, None, ALU.arith_shift_right))
            link(dve.tensor_copy(tiles[:], tint[:]))
            link(dve.tensor_tensor_scan(tend[:], one[:, 0:NEX], tiles[:], 0.0, ALU.mult, ALU.add))
            link(tt(tiles[:], tend[:], tiles[:], ALU.subtract))
            link(dve.scalar_tensor_tensor(out=sbase[:], in0=tiles[:], scalar=128.0, in1=pc[:, 0, :],
                                          op0=ALU.mult, op1=ALU.add))
            link(ts(sbase[:], sbase[:], -1.0, None, ALU.add))
            link(tt(inc[:], inc[:], sbase[:, :].unsqueeze(2).to_broadcast([CB, NEX, Q]), ALU.add))
            link(tt(inc[:], inc[:], oh[:], ALU.mult))
            link(dve.tensor_reduce(slot[:], inc[:].rearrange("c e q -> c q e"), AX.X, ALU.add))
            link(dve.scalar_tensor_tensor(out=slot[:, Q - HALO:Q], in0=pcol[:, 0:1].to_broadcast([CB, HALO]),
                                          scalar=float(FAR), in1=slot[:, Q - HALO:Q], op0=ALU.mult, op1=ALU.add))
            link(dve.tensor_copy(sloti[:], slot[:]))
            link(tt(cmp_[:], tie[:, :].unsqueeze(2).to_broadcast([1, NTILE, NEX]),
                    tend[0:1, :].unsqueeze(1).to_broadcast([1, NTILE, NEX]), ALU.is_ge))
            link(dve.tensor_reduce(tie[:], cmp_[:], AX.X, ALU.add))
            link(ts(late["te"][:], tie[:], float(NEX - 1), None, ALU.min))
            link(ts(pcol[:, 3:4], pcol[:, 3:4], float(Q), None, ALU.mult))
            link(tt(pcol[:, 3:4], pcol[:, 3:4], pcol[:, 2:3], ALU.add))
            link(ts(slot[:], tio[:], pcol[:, 3:4], None, ALU.add))
            dve.tensor_copy(h1[:, :, D + 3].bitcast(I32), slot[:])
            dve.wait_ge(lex, 1)
            link(dve.tensor_reduce(seen[:], ex[:], AX.X, ALU.add))
            link(dve.reciprocal(seen[:], seen[:]))
            dve.tensor_copy(h1[:, :, D + 2], seen[:]).then_inc(rows_ok, 1)


def experts(nc, io, dr, keep, late, out):
    with ExitStack() as ctx:
        def sb(name, shape, dt=F32):
            return ctx.enter_context(nc.sbuf_tensor(name, shape, dt))

        def sem(name):
            return ctx.enter_context(nc.semaphore(name))

        w1, w2, b2, te = late["w1"], late["w2"], late["b2"], late["te"]
        NB = 3
        xr = [sb(f"xr{j}", [128, ROW]) for j in range(NB)]
        z = [sb(f"z7{j}", [128, D]) for j in range(NB)]
        zt = [sb(f"zt7{j}", [HD + 1, 2, 128]) for j in range(NB)]
        hh = [sb(f"hh{j}", [128, FF]) for j in range(NB)]
        ht = [sb(f"ht7{j}", [128, FC, 128]) for j in range(NB)]
        ob = [sb(f"ob{j}", [128, D]) for j in range(NB)]
        yb = [sb(f"yb{j}", [128, D]) for j in range(NB)]
        oi = [sb(f"oi{j}", [128, 1], I32) for j in range(NB)]
        pz = bank(nc, ctx, "pz7", [HD, 2, 128])
        ph = [bank(nc, ctx, f"ph7{k}", [128, 512]) for k in range(2)]
        pt = [bank(nc, ctx, f"pt7{k}", [128, 3, 128]) for k in range(2)]
        py = bank(nc, ctx, "py7", [128, D])
        x_in = [sem(f"x7_in{j}") for j in range(NB)]
        z_ok = sem("z7_ok")
        turned = sem("t7")
        zt_ok = sem("zt7_ok")
        hid = sem("hid7")
        act_ok = sem("act7")
        ht_turned = sem("htt7")
        ht_ok = sem("ht7_ok")
        y_ok = sem("y7_ok")
        y_b = sem("y7_b")
        o_ok = sem("o7_ok")
        sent = [sem(f"sent7_{j}") for j in range(NB)]
        iot = sem("iot7")
        tick = sem("tick7")
        tickp = sem("tick7p")
        tick_s = sem("tick7s")
        block = ctx.enter_context(nc.Block())
        N = NTILE
        HEAD = NB + 1
        assert (N - HEAD - 1) % NB == 0
        half = FF // 2

        def steps(eng, body):
            for i in range(HEAD):
                body(i, i % NB, i // NB)
            with eng.Fori(0, (N - HEAD - 1) // NB) as p:
                for j in range(HEAD, HEAD + NB):
                    body(NB * p + j, j % NB, p + j // NB)
            body(N - 1, (N - 1) % NB, (N - 1) // NB)

        @block.sync
        def _(sp):
            def load(i, j, use):
                sp.wait_ge(o_ok, i + 1)
                hold(sp, tick_s)
                sp.dma_start(xr[j][:], dr["xs"][bass.ds(i * 128, 128), :]).then_inc(x_in[j], 16)

            sp.sem_inc(o_ok, 3)
            steps(sp, load)

        @block.gpsimd
        def _(pool):
            for j in range(NB):
                pool.memset(zt[j][HD:HD + 1, :, :], 1.0).then_inc(iot, 1)
            bound = pool.to_reg(B * L - 1)

            def send(i, j, use):
                pool.wait_ge(o_ok, i + 4)
                hold(pool, tickp)
                pool.indirect_dma_start(out, bass.IndirectOffsetOnAxis(ap=oi[j][:, 0:1], axis=0), ob[j][:], None,
                                        bounds_check=bound, oob_is_err=False).then_inc(sent[j], 16)

            steps(pool, send)
            for j in range(NB):
                pool.wait_ge(sent[j], 16 * len(range(j, N, NB)))

        @block.scalar
        def _(act):
            def take(i, j):
                act.wait_ge(turned, i + 3)
                act.wait_ge(hid, 2 * i + 2)
                act.activation(zt[j][0:HD, :, :], pz[:], ACT.Copy).then_inc(zt_ok, 1)

            def body(i, j, use):
                act.wait_ge(ht_turned, i + 1)
                for k in range(2):
                    act.wait_ge(hid, 2 * i + k + 5)
                    act.activation(hh[j][:, k * half:(k + 1) * half], ph[k][:, 0:half], ACT.Gelu).then_inc(act_ok, 1)
                if not isinstance(i, int) or i < N - 1:
                    take(i + 1, (j + 1) % NB)

            act.wait_ge(iot, 3)
            act.activation(hh[0][:, 0:1], keep["ident"][:, 0:1], ACT.Gelu)
            act.sem_inc(ht_turned, 2)
            act.sem_inc(hid, 4)
            take(0, 0)
            steps(act, body)

        @block.vector
        def _(dve):
            def normal(i, j, use):
                dve.wait_ge(x_in[j], 16 * (use + 1))
                dve.wait_ge(turned, i + 1)
                dve.tensor_scalar(z[j][:], xr[j][:, 0:D], xr[j][:, D:D + 1], xr[j][:, D + 1:D + 2],
                                  ALU.subtract, ALU.mult).then_inc(z_ok, 1)

            def finish(i, j, use):
                ex = dve.value_load(te[0:1, bass.ds(i, 1)], min_val=0, max_val=NEX - 1)
                dve.wait_ge(y_ok, i + 3)
                dve.tensor_tensor(yb[j][:], py[:], b2[:, bass.ds(ex * D, D)], ALU.add).then_inc(y_b, 1)
                if not isinstance(use, int) or use > 0:
                    dve.wait_ge(sent[j], 16 * use)
                dve.tensor_copy(oi[j][:], xr[j][:, ROW - 1:ROW].bitcast(I32))
                dve.wait_ge(y_b, i + 2)
                dve.scalar_tensor_tensor(out=ob[j][:], in0=yb[j][:], scalar=xr[j][:, D + 2:D + 3], in1=xr[j][:, 0:D],
                                         op0=ALU.mult, op1=ALU.add).then_inc(o_ok, 1)

            def body(i, j, use):
                if not isinstance(i, int) or i < N - 1:
                    normal(i + 1, (j + 1) % NB, use + (j + 1) // NB)
                if not isinstance(i, int) or i > 0:
                    finish(i - 1, (j - 1) % NB, use - (1 if j == 0 else 0))
                dve.wait_ge(y_ok, i + 1)
                dve.wait_ge(ht_turned, i + 3)
                dve.tensor_copy(ht[j][:, 0:3, :], pt[0][:])
                dve.tensor_copy(ht[j][:, 3:6, :], pt[1][:]).then_inc(ht_ok, 1)

            dve.sem_inc(y_ok, 2)
            dve.sem_inc(y_b, 1)
            dve.wait_ge(keep["wl"], WLOADS)
            normal(0, 0, 0)
            steps(dve, body)
            finish(N - 1, (N - 1) % NB, (N - 1) // NB)

        @block.tensor
        def _(pe):
            ident = keep["ident"]

            def turn(i, j):
                pe.wait_ge(z_ok, i + 1)
                pe.wait_ge(zt_ok, i + 1)
                for k in range(2):
                    t = pe.transpose(pz[:, k, :], z[j][:, k * HD:(k + 1) * HD], ident[:])
                t.then_inc(turned, 1)

            def second(i, j):
                ex = pe.value_load(te[0:1, bass.ds(i, 1)], min_val=0, max_val=NEX - 1)
                pe.wait_ge(ht_ok, i + 2)
                pe.wait_ge(y_b, i + 1)
                for k in range(FC):
                    m = pe.matmul(py[:], ht[j][:, k, :], w2[:, k, bass.ds(ex * D, D)], start=(k == 0),
                                  stop=(k == FC - 1))
                m.then_inc(y_ok, 1)

            def body(i, j, use):
                ex = pe.value_load(te[0:1, bass.ds(i, 1)], min_val=0, max_val=NEX - 1)
                pe.wait_ge(zt_ok, i + 2)
                for k in range(2):
                    pe.wait_ge(act_ok, 2 * i + k + 1)
                    for f in range(2):
                        m = pe.matmul(ph[k][:, 0:half], zt[j][0:HD + f, f, :],
                                      w1[0:HD + f, f, bass.ds(ex * FF + k * half, half)], start=(f == 0), stop=(f == 1))
                    m.then_inc(hid, 1)
                if not isinstance(i, int) or i > 0:
                    second(i - 1, (j - 1) % NB)
                if not isinstance(i, int) or i < N - 1:
                    turn(i + 1, (j + 1) % NB)
                pe.wait_ge(act_ok, 2 * i + 4)
                pe.wait_ge(ht_ok, i + 1)
                for k in range(FC):
                    t = pe.transpose(pt[k // 3][:, k % 3, :], hh[j][:, k * 128:(k + 1) * 128], ident[:])
                t.then_inc(ht_turned, 1)

            pe.sem_inc(zt_ok, 1)
            pe.sem_inc(ht_ok, 1)
            pe.sem_inc(turned, 2)
            pe.sem_inc(act_ok, 2)
            pe.wait_ge(keep["wl"], WLOADS)
            turn(0, 0)
            steps(pe, body)
            second(N - 1, (N - 1) % NB)


WLOADS = 16 * (2 + 1 + FC + 1)


def build(nc, io, out):
    def dram(name, shape):
        return nc.dram_tensor(name, shape, F32).ap()

    dr = {"h0": dram("h0", (B * LP, D)), "xs": dram("xs", (SLOTS, ROW)), "var_tab": dram("var_tab", (NVAR, 70)),
          "kd": dram("kd", (E, KREV)), "lamd": dram("lamd", (E * NS,)), "c2d": dram("c2d", (E * NS,)),
          "yd": dram("yd", (E, Q * CB))}
    with ExitStack() as ctx:
        def sb(name, shape, dt=F32):
            return ctx.enter_context(nc.sbuf_tensor(name, shape, dt))

        keep = {"ident": sb("ident", [128, 128]), "before": sb("before", [128, 128]), "ones": sb("ones", [128, 128]),
                "wi": sb("wi", [HD + 1, 2, E]), "wo": sb("wo", [EB + 1, NBLK, D]),
                "mu": sb("mu", [CB, Q]), "rs": sb("rs", [CB, Q]),
                "lamc": sb("lamc", [128, NBLK * NG]), "c2c": sb("c2c", [128, NBLK * NG]),
                "texp": sb("texp", [128, Q]), "sexp": sb("sexp", [96, 2]), "own": sb("own", [128, GE]),
                "wl": ctx.enter_context(nc.semaphore("expert_weights_in"))}
        with ExitStack() as early:
            def esb(name, shape, dt=F32):
                return early.enter_context(nc.sbuf_tensor(name, shape, dt))

            keep |= {"shift": esb("shift", [128, 128]), "tk": esb("tk", [128, B * 6]), "vr": esb("vr", [128, B * 70]),
                     "tid": esb("tid", [128, B], I32), "vid": esb("vid", [128, B], I32)}
            embed_images(nc, io, dr, keep)
            embed_text(nc, io, dr, keep)
        mixer_tables(nc, io, dr, keep)
        with nc.sbuf_tensor("xn", [HD + 1, 2, B, HALO + LP], F32) as xn:
            normalise_in(nc, io, dr, keep, xn)
            mix(nc, io, dr, keep, xn)
        late = {"w1": sb("w1e", [HD + 1, 2, NEX * FF]), "w2": sb("w2e", [128, FC, NEX * D]),
                "b2": sb("b2e", [128, NEX * D]), "te": sb("te", [1, NTILE], I32)}
        project_route(nc, io, dr, keep, late)
        experts(nc, io, dr, keep, late, out)


_TOK = ["token_has_int", "token_signed_norm", "token_log_norm", "token_is_zero", "token_is_pow2", "token_is_one"]


def kernel(**inputs):
    import numpy as _np
    import concourse.bacc as _bacc
    from concourse import mybir as _mybir
    from concourse.bass_utils import run_bass_kernel_spmd as _run

    nc = _bacc.Bacc("TRN2", target_bir_lowering=False, num_devices=1)
    named = {k: _np.asarray(v) for k, v in inputs.items() if k[7:] not in _TOK}
    named["tok_tab"] = _np.stack([_np.asarray(inputs["L0_txt_" + k]) for k in _TOK], axis=1)
    arrays, io = {}, {}
    for name, a in named.items():
        a = _np.ascontiguousarray(a).reshape(a.shape or (1,))
        arrays[f"in_{name}"] = a
        io[name] = nc.dram_tensor(f"in_{name}", a.shape, _mybir.dt.from_np(a.dtype), kind="ExternalInput").ap()
    out = nc.dram_tensor("out_dram", (B * L, D), F32, kind="ExternalOutput").ap()
    build(nc, io, out)
    r = _run(nc, [arrays], core_ids=[0])
    return r.results[0]["out_dram"].reshape(B, L, D)
```

```python
from contextlib import ExitStack

import concourse.bass as bass
from concourse import mybir

F32 = mybir.dt.float32
I32 = mybir.dt.int32
ALU = mybir.AluOpType
ACT = mybir.ActivationFunctionType
AX = mybir.AxisListType

B = 32
D = 192
HD = D // 2
IMG, PATCH, CH = 224, 16, 3
GRID = IMG // PATCH
NIMG = GRID * GRID
TXT = 128
L = 1 + NIMG + TXT
NCHUNK, Q = 4, 82
LP = NCHUNK * Q
CB = B * NCHUNK
E = 384
NS = 16
TAPS = 4
HALO = TAPS - 1
W = Q + HALO
EB = 96
NBLK = E // EB
GE = 8
NG = EB // GE
GPW = Q + NS
KREV = 180
NEX, FF = 8, 768
FC = FF // 128
V = 50257
NVAR = 1024
NF = 64
FEAT = 85
NTILE = (B * L + NEX * 127) // 128
CAP = (B * L + 128 + 127) // 128 * 128
SPARE = NTILE - (B * L + 127) // 128
XROWS = NEX * CAP + SPARE * 128
ROW = D + 4
FAR = 1 << 20
EPS = 1e-5
NB = 3

GB = 8
GP_ROWS = GB * GRID
NGRP = B // GB
PD = PATCH * PATCH * CH
KC = PD // 128



def bank(nc, ctx, name, shape):
    t = ctx.enter_context(nc.psum_tensor(name, [128, 512], F32))
    n = 1
    for s in shape[1:]:
        n *= s
    v = t[0:shape[0], 0:n]
    if len(shape) == 3:
        v = v.rearrange("p (a b) -> p a b", a=shape[1])
    return v


def embed_images(nc, io, dr, keep):
    with ExitStack() as ctx:
        def sb(name, shape, dt=F32):
            return ctx.enter_context(nc.sbuf_tensor(name, shape, dt))

        def sem(name):
            return ctx.enter_context(nc.semaphore(name))

        R = GP_ROWS
        xg = [sb(f"xg{j}", [R, CH * PATCH, IMG]) for j in range(2)]
        xc = [sb(f"xc{j}", [R, CH * PATCH, PATCH]) for j in range(2)]
        xt = [sb(f"xt{j}", [128, KC, R]) for j in range(2)]
        wp = sb("wp", [128, KC, D])
        g1 = sb("g1", [128, KC])
        b1 = sb("b1", [128, KC])
        b1w = sb("b1w", [128, KC, R])
        wg = sb("wg", [128, KC, D])
        bias1 = sb("bias1", [R, D])
        g2 = sb("g2", [R, D])
        b2 = sb("b2", [R, D])
        pos = sb("pos", [R, GRID, D])
        NY = 3
        yg = [sb(f"yg{j}", [R, GRID, D]) for j in range(NY)]
        st = sb("st1", [R, GRID, 2, 6])
        mx = [sb(f"mx1{j}", [R, GRID]) for j in range(2)]
        ve = [sb(f"ve1{j}", [R, GRID]) for j in range(2)]
        dev = sb("dev1", [R, GRID, 4])
        d2 = sb("d21", [R, GRID])
        m2 = sb("m21", [R, GRID])
        rs = [sb(f"rs1{j}", [R, GRID]) for j in range(2)]
        nb = [sb(f"nb1{j}", [R, GRID]) for j in range(2)]
        sty = sb("sty", [R, GRID, 6])
        muy = sb("muy", [R, GRID])
        dfy = sb("dfy", [R, GRID])
        vey = sb("vey", [R, GRID])
        rsy = sb("rsy", [R, GRID])
        cls = sb("cls", [B, 2, D])
        zrow = sb("zrow", [128, HALO * D])

        ps_t = [[bank(nc, ctx, f"ps_t{j}{k}", [128, 3, R]) for k in range(2)]
                for j in range(2)]
        ps_y = [bank(nc, ctx, f"ps_y{j}", [R, D]) for j in range(2)]
        ps_b = bank(nc, ctx, "ps_b", [R, D])

        x_in = [[sem(f"x_in{g}{n}") for n in range(1 if g < 2 else 2)] for g in range(NGRP)]
        w_in = sem("w_in")
        w_ready = sem("w_ready")
        x_std = sem("x_std")
        x_sqrt = sem("x_sqrt")
        x_rstd = sem("x_rstd")
        x_normed = sem("x_normed")
        turned = sem("turned")
        turned_out = sem("turned_out")
        projected = sem("projected")
        y_taken = sem("y_taken")
        bias_mm = sem("bias_mm")
        y_var = sem("y_var")
        y_sqrt = sem("y_sqrt")
        y_mid = sem("y_mid")
        y_scaled = sem("y_scaled")
        tick = keep["tick"]
        y_out = [sem(f"y_out{g}") for g in range(NGRP)]
        pos_in = sem("pos_in")
        cls_ok = sem("cls_ok")
        step = sem("step1")
        const = sem("const1")
        ids_in = sem("ids_in")
        gath = keep["gathered"]
        tab = sem("tab")
        misc = sem("misc")
        block = ctx.enter_context(nc.Block())

        xv = io["x"].rearrange("b c (h p) w -> b h c p w", p=PATCH)
        wv = io["L0_tok_W_proj"].rearrange("(f c) d -> c f d", c=CH)
        gv = io["L0_tok_ln1_g"].rearrange("(f c) -> c f", c=CH)
        bv = io["L0_tok_ln1_b"].rearrange("(f c) -> c f", c=CH)
        posv = io["L0_tok_pos_embedding"]
        h0 = dr["h0"]
        PIECES = ((0, 8), (8, GRID))
        W_LOADS = 3 * KC + 3

        @block.sync
        def _(sp):
            for g in range(2):
                if g:
                    sp.wait_ge(x_in[0][0], 16 * GB)
                    sp.wait_ge(w_in, 16 * W_LOADS)
                for b in range(GB):
                    sp.dma_start(xg[g][b * GRID:(b + 1) * GRID, :, :].rearrange("r (c p) w -> r c (p w)", c=CH),
                                 xv[g * GB + b].rearrange("h c p w -> h c (p w)")).then_inc(x_in[g][0], 16)
            for g in range(2, NGRP):
                for n, (lo, hi) in enumerate(PIECES):
                    sp.wait_ge(x_normed, GRID * (g - 2) + hi)
                    for b in range(GB):
                        for c in range(CH):
                            sp.dma_start(xg[g % 2][b * GRID:(b + 1) * GRID, c * PATCH:(c + 1) * PATCH,
                                                   lo * PATCH:hi * PATCH],
                                         xv[g * GB + b][:, c, :, lo * PATCH:hi * PATCH]).then_inc(x_in[g][n], 16)
            for g in range(NGRP):
                sp.wait_ge(y_scaled, GRID * (g + 1))
                for b in range(GB):
                    row = (g * GB + b) * LP + 1
                    sp.dma_start(h0[row:row + NIMG, :].rearrange("(h w) d -> h (w d)", w=GRID),
                                 yg[g % NY][b * GRID:(b + 1) * GRID, :, :].rearrange("r w d -> r (w d)")
                                 ).then_inc(y_out[g], 16)
            for g in range(NGRP):
                sp.wait_ge(y_out[g], 16 * GB)

        @block.gpsimd
        def _(pool):
            pool.memset(keep["ident"][:], 0.0).then_inc(const, 1)
            pool.memset(keep["before"][:], 1.0).then_inc(const, 1)
            pool.memset(keep["shift"][:], 0.0).then_inc(const, 1)
            pool.memset(keep["ones"][:], 1.0).then_inc(const, 1)
            pool.wait_ge(const, 4)
            pool.affine_select(out=keep["ident"][:], in_=keep["ident"][:], compare_op=ALU.not_equal, fill=1.0,
                               base=0, pattern=[[-1, 128]], channel_multiplier=1).then_inc(const, 1)
            pool.affine_select(out=keep["before"][:], in_=keep["before"][:], compare_op=ALU.is_gt, fill=0.0,
                               base=0, pattern=[[1, 128]], channel_multiplier=-1).then_inc(const, 1)
            pool.affine_select(out=keep["shift"][:], in_=keep["shift"][:], compare_op=ALU.not_equal, fill=1.0,
                               base=-1, pattern=[[1, 128]], channel_multiplier=-1).then_inc(const, 1)
            pool.memset(zrow[:], 0.0).then_inc(misc, 1)
            pool.wait_ge(ids_in, 32)
            for b in range(B):
                pool.indirect_dma_start(keep["tk"][:, b * 6:(b + 1) * 6], None, io["tok_tab"],
                                        bass.IndirectOffsetOnAxis(ap=keep["tid"][:, b:b + 1], axis=0)
                                        ).then_inc(gath, 16)
            pool.wait_ge(tab, 16 * 7)
            for b in range(B):
                pool.indirect_dma_start(keep["vr"][:, b * 70:(b + 1) * 70], None, dr["var_tab"],
                                        bass.IndirectOffsetOnAxis(ap=keep["vid"][:, b:b + 1], axis=0)
                                        ).then_inc(gath, 16)
            pool.wait_ge(gath, 16 * 2 * B)

        @block.scalar
        def _(act):
            for k in range(KC):
                c, p0 = k // 2, (k % 2) * 128
                act.dma_start(wp[:, k, :], wv[c, p0:p0 + 128, :]).then_inc(w_in, 16)
            for tile, name in ((bias1, "L0_tok_b_proj"), (g2, "L0_tok_ln2_g"), (b2, "L0_tok_ln2_b")):
                act.dma_start(tile[:], io[name].partition_broadcast(R)).then_inc(w_in, 16)
            with nc.allow_non_contiguous_dma(reason="per-feature vectors of a few values"):
                for k in range(KC):
                    c, p0 = k // 2, (k % 2) * 128
                    act.dma_start(g1[:, k:k + 1], gv[c, p0:p0 + 128].unsqueeze(1)).then_inc(w_in, 16)
                    act.dma_start(b1[:, k:k + 1], bv[c, p0:p0 + 128].unsqueeze(1)).then_inc(w_in, 16)
                act.dma_start(keep["tid"][:], io["x_txt"].rearrange("b s -> s b")).then_inc(ids_in, 16)
                act.dma_start(keep["vid"][:], io["itok_BS_0_4095"].rearrange("b s -> s b")).then_inc(ids_in, 16)
                vt = dr["var_tab"]
                act.dma_start(vt[:, 0:NF], io["L0_txt_var_family_onehot"]).then_inc(tab, 16)
                for n, name in enumerate(["var_outer_norm", "var_inner_norm", "var_has_outer", "var_has_inner"]):
                    act.dma_start(vt[:, NF + n:NF + n + 1], io["L0_txt_" + name].unsqueeze(1)).then_inc(tab, 16)
                for n, name in enumerate(["var_family_id", "var_group_id"]):
                    act.dma_start(vt[:, NF + 4 + n:NF + 5 + n].bitcast(I32), io["L0_txt_" + name].unsqueeze(1)
                                  ).then_inc(tab, 16)
            act.wait_ge(misc, 1)
            act.dma_start(h0.rearrange("(b t) d -> b t d", t=LP)[:, L:LP, :].rearrange("b t d -> b (t d)"),
                          zrow[0:B, :]).then_inc(misc, 16)

            def root(g):
                act.wait_ge(x_std, g + 1)
                act.activation(rs[g % 2][:], ve[g % 2][:], ACT.Sqrt).then_inc(x_sqrt, 1)

            def normalise(g, w, j):
                act.activation(xc[j][:], xg[g % 2][:, :, bass.ds(w * PATCH, PATCH)], ACT.Identity,
                               bias=nb[g % 2][:, bass.ds(w, 1)], scale=rs[g % 2][:, bass.ds(w, 1)]
                               ).then_inc(x_normed, 1)

            def take(i, j):
                act.wait_ge(turned, i + 1)
                act.wait_ge(projected, i + 1)
                act.copy(xt[j][:, 0:3, :], ps_t[j][0][:])
                act.copy(xt[j][:, 3:6, :], ps_t[j][1][:]).then_inc(turned_out, 1)

            act.sem_inc(projected, 2)
            def root_y(g):
                act.wait_ge(y_var, g + 1)
                act.activation(rsy[:], vey[:], ACT.Sqrt).then_inc(y_sqrt, 1)

            def steps(g, lo, hi):
                with act.Fori(lo, hi) as p:
                    for j in range(2):
                        take(g * GRID + 2 * p + j, j)
                        normalise(g, 2 * p + 2 + j, j)

            root(0)
            act.wait_ge(x_rstd, 1)
            normalise(0, 0, 0)
            normalise(0, 1, 1)
            for b in range(GB):
                act.dma_start(pos[b * GRID:(b + 1) * GRID, :, :].rearrange("r w d -> r (w d)"),
                              posv[0, 1:1 + NIMG, :].rearrange("(h w) d -> h (w d)", w=GRID)).then_inc(pos_in, 16)
            act.dma_start(cls[:, 0, :], posv[0, 0, :].partition_broadcast(B)).then_inc(pos_in, 16)
            act.dma_start(cls[:, 1, :], io["L0_tok_cls_token"][0, 0, :].partition_broadcast(B)).then_inc(pos_in, 16)
            for g in range(NGRP):
                steps(g, 0, EARLY)
                if g:
                    root_y(g - 1)
                steps(g, EARLY, LATE)
                if g + 1 < NGRP:
                    root(g + 1)
                steps(g, LATE, GRID // 2 - 1)
                if g + 1 < NGRP:
                    act.wait_ge(x_rstd, g + 2)
                for j in range(2):
                    take(g * GRID + GRID - 2 + j, j)
                    if g + 1 < NGRP:
                        normalise(g + 1, j, j)
            root_y(NGRP - 1)
            act.wait_ge(misc, 1 + 16)
            act.wait_ge(cls_ok, 1)
            act.dma_start(h0.rearrange("(b t) d -> b t d", t=LP)[:, 0, :], cls[:, 0, :]).then_inc(misc, 16)
            act.wait_ge(misc, 1 + 32)

        @block.tensor
        def _(pe):
            def turn(i, j):
                pe.wait_ge(x_normed, i + 1)
                pe.wait_ge(turned_out, i + 1)
                flat = xc[j][:, :, :].rearrange("r a q -> r (a q)")
                for k in range(KC):
                    t = pe.transpose(ps_t[j][k // 3][:, k % 3, :], flat[:, k * 128:(k + 1) * 128],
                                     keep["ident"][0:R, 0:R])
                t.then_inc(turned, 1)

            def project(i, j):
                pe.wait_ge(turned_out, i + 3)
                pe.wait_ge(y_taken, i + 1)
                for k in range(KC):
                    m = pe.matmul(ps_y[j][:], xt[j][:, k, :], wg[:, k, :], start=(k == 0), stop=(k == KC - 1))
                m.then_inc(projected, 1)

            pe.sem_inc(turned_out, 2)
            pe.sem_inc(y_taken, 2)
            pe.wait_ge(const, 7)
            pe.wait_ge(w_ready, 1)
            for k in range(KC):
                m = pe.matmul(ps_b[:], b1w[:, k, :], wp[:, k, :], start=(k == 0), stop=(k == KC - 1))
            m.then_inc(bias_mm, 1)
            n = NGRP * GRID
            turn(0, 0)
            with pe.Fori(0, n // 2 - 1) as p:
                for j in range(2):
                    turn(2 * p + 1 + j, 1 - j)
                    project(2 * p + j, j)
            turn(n - 1, 1)
            project(n - 2, 0)
            project(n - 1, 1)

        @block.vector
        def _(dve):
            done = [0]

            def link(ins):
                done[0] += 1
                ins.then_inc(step, 1)
                dve.wait_ge(step, done[0])

            def x_arrived(g, n):
                dve.wait_ge(x_in[g][n], 16 * GB * (1 if g < 2 else CH))

            def x_stats(g, w):
                half = CH * PATCH // 2
                for k in range(2):
                    dve.bn_stats(st[:, bass.ds(w, 1), k, :].rearrange("r a b -> r (a b)"),
                                 xg[g % 2][:, k * half:(k + 1) * half, bass.ds(w * PATCH, PATCH)])

            def x_moments(g):
                q = st[:, :, :, :].rearrange("r w k (h s) -> r w (k h) s", h=2)
                if g >= 2:
                    dve.wait_ge(x_normed, GRID * (g - 1))
                link(dve.memset(d2[:], 0.0))
                dve.tensor_reduce(m2[:], q[:, :, :, 2], AX.X, ALU.add)
                link(dve.tensor_reduce(mx[g % 2][:], q[:, :, :, 1], AX.X, ALU.add))
                link(dve.tensor_scalar(mx[g % 2][:], mx[g % 2][:], 0.25, None, ALU.mult))
                link(dve.tensor_tensor(dev[:], q[:, :, :, 1], mx[g % 2][:, :].unsqueeze(2).to_broadcast([R, GRID, 4]),
                                       ALU.subtract))
                link(dve.tensor_tensor(dev[:], dev[:], dev[:], ALU.mult))
                dve.tensor_scalar(m2[:], m2[:], 1.0 / PD, EPS, ALU.mult, ALU.add)
                link(dve.tensor_reduce(d2[:], dev[:], AX.X, ALU.add))
                dve.scalar_tensor_tensor(out=ve[g % 2][:], in0=d2[:], scalar=0.25, in1=m2[:], op0=ALU.mult,
                                         op1=ALU.add).then_inc(x_std, 1)

            def x_scales(g):
                dve.wait_ge(x_sqrt, g + 1)
                link(dve.reciprocal(rs[g % 2][:], rs[g % 2][:]))
                dve.scalar_tensor_tensor(out=nb[g % 2][:], in0=mx[g % 2][:], scalar=-1.0, in1=rs[g % 2][:],
                                         op0=ALU.mult, op1=ALU.mult).then_inc(x_rstd, 1)

            def y_moments(g):
                link(dve.memset(dfy[:], 0.0))
                dve.tensor_tensor(muy[:], sty[:, :, 1], sty[:, :, 4], ALU.add)
                dve.tensor_tensor(vey[:], sty[:, :, 2], sty[:, :, 5], ALU.add)
                link(dve.tensor_tensor(dfy[:], sty[:, :, 1], sty[:, :, 4], ALU.subtract))
                dve.tensor_scalar(muy[:], muy[:], 0.5, None, ALU.mult)
                dve.tensor_scalar(vey[:], vey[:], 1.0 / D, EPS, ALU.mult, ALU.add)
                link(dve.tensor_tensor(dfy[:], dfy[:], dfy[:], ALU.mult))
                dve.scalar_tensor_tensor(out=vey[:], in0=dfy[:], scalar=0.25, in1=vey[:], op0=ALU.mult, op1=ALU.add
                                         ).then_inc(y_var, 1)

            def col(t, w):
                return t[:, bass.ds(w, 1), :].rearrange("r a d -> r (a d)")

            def y_take(g, w, j):
                i = g * GRID + w
                dve.wait_ge(projected, i + 3)
                dve.tensor_tensor(col(yg[g % NY], w), ps_y[j][:], bias1[:], ALU.add).then_inc(y_taken, 1)

            def y_stat(g, w):
                dve.wait_ge(y_taken, g * GRID + w + 3)
                hold(dve, tick)
                dve.bn_stats(col(sty, w), col(yg[g % NY], w))

            def y_scale(g, w, n):
                for a in range(n):
                    r = col(yg[g % NY], w + a)
                    dve.scalar_tensor_tensor(out=r, in0=r, scalar=muy[:, bass.ds(w + a, 1)], in1=g2[:],
                                             op0=ALU.subtract, op1=ALU.mult).then_inc(y_mid, 1)
                for a in range(n):
                    dve.wait_ge(y_mid, g * GRID + w + a + 1)
                    r = col(yg[g % NY], w + a)
                    dve.scalar_tensor_tensor(out=r, in0=r, scalar=rsy[:, bass.ds(w + a, 1)], in1=col(pos, w + a),
                                             op0=ALU.mult, op1=ALU.add).then_inc(y_scaled, 1)

            def steps(g, lo, hi, more=False, scale=0, w0=0):
                with dve.Fori(lo, hi) as p:
                    for j in range(2):
                        y_take(g, 2 * p + j, j)
                        if more:
                            x_stats(g + 1, 2 * p + GRID - 2 * LATE + j)
                        y_stat(g, 2 * p + j)
                    if scale:
                        y_scale(g - 1, scale * p + (w0 - scale * lo), scale)

            x_arrived(0, 0)
            with dve.Fori(0, GRID // 7) as i:
                for a in range(7):
                    x_stats(0, 7 * i + a)
            dve.wait_ge(w_in, 16 * W_LOADS)
            for k in range(KC):
                dve.tensor_scalar(wg[:, k, :], wp[:, k, :], g1[:, k:k + 1], None, ALU.mult)
                dve.tensor_copy(b1w[:, k, :], b1[:, k:k + 1].to_broadcast([128, R]))
            link(dve.memset(muy[:], 0.0))
            dve.sem_inc(w_ready, 1)
            x_moments(0)
            x_scales(0)
            dve.wait_ge(bias_mm, 1)
            link(dve.tensor_tensor(bias1[:], bias1[:], ps_b[:], ALU.add))
            for g in range(NGRP):
                more = g + 1 < NGRP
                if more and g:
                    x_arrived(g + 1, 0)
                    for w in range(GRID - 2 * LATE):
                        x_stats(g + 1, w)
                if g >= NY:
                    dve.wait_ge(y_out[g - NY], 16 * GB)
                steps(g, 0, EARLY, more and g)
                if more and g:
                    x_arrived(g + 1, 1)
                if not g:
                    dve.wait_ge(pos_in, 16 * (GB + 2))
                    link(dve.tensor_tensor(pos[:, :, :], pos[:, :, :], b2[:, :].unsqueeze(1).to_broadcast([R, GRID, D]),
                                           ALU.add))
                    link(dve.tensor_tensor(cls[:, 0, :], cls[:, 0, :], cls[:, 1, :], ALU.add))
                    dve.sem_inc(cls_ok, 1)
                    x_arrived(1, 0)
                    with dve.Fori(0, (GRID - 2 * (LATE - EARLY)) // 4) as i:
                        for a in range(4):
                            x_stats(1, 4 * i + a)
                if g:
                    dve.wait_ge(y_sqrt, g)
                    link(dve.reciprocal(rsy[:], rsy[:]))
                steps(g, EARLY, LATE, more, 2 if g else 0)
                if more:
                    x_moments(g + 1)
                    x_scales(g + 1)
                steps(g, LATE, GRID // 2, False, 4 if g else 0, 2 * (LATE - EARLY))
                y_moments(g)
            dve.wait_ge(y_sqrt, NGRP)
            link(dve.reciprocal(rsy[:], rsy[:]))
            with dve.Fori(0, GRID // 2) as p:
                y_scale(NGRP - 1, 2 * p, 2)


EARLY, LATE = 2, 5


def embed_text(nc, io, dr, keep):
    with ExitStack() as ctx:
        def sb(name, shape, dt=F32):
            return ctx.enter_context(nc.sbuf_tensor(name, shape, dt))

        def sem(name):
            return ctx.enter_context(nc.semaphore(name))

        tk = keep["tk"][:, :].rearrange("p (b f) -> p b f", f=6)
        vr = keep["vr"][:, :].rearrange("p (b f) -> p b f", f=70)
        vri = keep["vr"][:, :].bitcast(I32).rearrange("p (b f) -> p b f", f=70)
        HB = B // 2
        NG4 = B // 4
        HN = NG4 // 2
        ft = sb("ft", [128, B, FEAT])
        mo = sb("mo", [128, B, 4 * NF + 2])
        sel = sb("sel", [128, B, 2, NF])
        pk = sb("pk", [128, HB, 4 * NF])
        ps4 = sb("ps4", [128, B, 4])
        pc = sb("pc", [128, B, 2])
        io64 = sb("io64", [128, NF])
        tf = sb("tf", [128, B])
        ff = sb("ff", [128, B, 2])
        va = sb("va", [128, B])
        va2 = sb("va2", [128, B])
        tlv = sb("tlv", [128, B])
        shi = sb("shi", [128, 2, B])
        rc = sb("rc", [128, B])
        posn = sb("posn", [128, 1])
        st = sb("stt", [128, B, 6])
        ve = sb("vet", [128, B])
        mu = sb("mut", [128, B])
        df = sb("dft", [128, B])
        nz = sb("nzt", [128, B])
        xt = [sb(f"xtt{j}", [FEAT, 4, 128]) for j in range(2)]
        ht = [sb(f"htt{j}", [NF + 1, 4, 128]) for j in range(2)]
        ot = [sb(f"ott{j}", [128, 4, D]) for j in range(2)]
        w1 = sb("w1t", [FEAT, NF])
        w2 = sb("w2t", [NF + 1, D])
        sc = sb("sct", [NF + 1, 1])
        lg = sb("lgt", [FEAT, 1])
        lb = sb("lbt", [FEAT, 1])
        bb = sb("bbt", [NF, 1])
        gam = sb("gam4", [HD, 2])
        win_row = sb("win_row", [128, E // 128, D])
        wout_row = sb("wout_row", [HD, 2, E])
        pp = [bank(nc, ctx, f"pp{j}", [128, 512]) for j in range(2)]
        pt = [bank(nc, ctx, f"pt{j}", [FEAT, 4, 128]) for j in range(2)]
        po = [bank(nc, ctx, f"po{j}", [128, 2, 256]) for j in range(2)]
        ph = [bank(nc, ctx, f"ph{j}", [128, 512]) for j in range(2)]

        w_in = sem("tw_in")
        iot = sem("iot")
        step = sem("step2")
        mo_ready = sem("mo_ready")
        summed = sem("summed")
        sum_taken = sem("sum_taken")
        ft_copied = sem("ft_copied")
        ft_std = sem("ft_std")
        ft_sqrt = sem("ft_sqrt")
        ft_scale = sem("ft_scale")
        ft_ready = sem("ft_ready")
        w2_ready = sem("w2_ready")
        turned = sem("t_turned")
        xt_ready = sem("t_xt")
        hid = sem("t_hid")
        ht_ready = sem("t_ht")
        outp = sem("t_outp")
        taken = sem("t_taken")
        stored = [sem("t_st0"), sem("t_st1")]
        p_in = sem("p_in")
        p_turned = sem("p_turned")
        p_taken = sem("p_taken")
        tables = MixerTables(nc, io, dr, keep, sb, sem)
        block = ctx.enter_context(nc.Block())
        T = "L0_txt_"
        wi, wo = keep["wi"], keep["wo"]

        @block.sync
        def _(sp):
            tables.load(sp)
            sp.dma_start(w1[:], io[T + "W1"]).then_inc(w_in, 16)
            sp.dma_start(w2[0:NF, :], io[T + "W2"]).then_inc(w_in, 16)
            sp.dma_start(w2[NF:NF + 1, :], io[T + "b2"].unsqueeze(0)).then_inc(w_in, 16)
            sp.dma_start(sc[:], io[T + "scale"].partition_broadcast(NF + 1)).then_inc(w_in, 16)
            with nc.allow_non_contiguous_dma(reason="one value per partition"):
                sp.dma_start(lg[:], io[T + "ln_g"].unsqueeze(1)).then_inc(w_in, 16)
                sp.dma_start(lb[:], io[T + "ln_b"].unsqueeze(1)).then_inc(w_in, 16)
                sp.dma_start(bb[:], io[T + "b1"].unsqueeze(1)).then_inc(w_in, 16)
                sp.dma_start(gam[:], io["L0_attn_gamma"].rearrange("(k p) -> p k", p=HD)).then_inc(p_in, 16)
            sp.dma_start(win_row[:, :, :], io["L0_attn_W_in"].rearrange("(k p) d -> p k d", p=128)).then_inc(p_in, 16)
            sp.dma_start(wi[HD:HD + 1, 1, :], io["L0_attn_b_in"].unsqueeze(0)).then_inc(p_in, 16)
            for n in range(2):
                sp.dma_start(wout_row[:, n, :], io["L0_attn_W_out"][n * HD:(n + 1) * HD, :]).then_inc(p_in, 16)
            sp.dma_start(wo[EB:EB + 1, NBLK - 1, :], io["L0_attn_b_out"].unsqueeze(0)).then_inc(p_in, 16)
            tables.store(sp)
            hv = dr["h0"].rearrange("(b t) d -> t b d", t=LP)
            for n in range(NG4):
                sp.wait_ge(taken, 2 * (n + 1))
                sp.dma_start(hv[1 + NIMG:L, 4 * n:4 * n + 4, :], ot[n % 2][:]).then_inc(stored[n % 2], 16)
            for j in range(2):
                sp.wait_ge(stored[j], 16 * (NG4 // 2))

        @block.gpsimd
        def _(pool):
            pool.iota(io64[:], pattern=[[1, NF]], base=0, channel_multiplier=0,
                      allow_small_or_imprecise_dtypes=True).then_inc(iot, 1)
            pool.iota(posn[:], pattern=[[0, 1]], base=0, channel_multiplier=1,
                      allow_small_or_imprecise_dtypes=True).then_inc(iot, 1)
            pool.wait_ge(iot, 2)
            for j in range(2):
                pool.memset(ht[j][NF:NF + 1, :, :], 1.0).then_inc(iot, 1)
            pool.wait_ge(iot, 4)
            tables.constants(pool)
            tables.work(pool)

        @block.vector
        def _(dve):
            done = [0]

            def link(ins):
                done[0] += 1
                ins.then_inc(step, 1)
                dve.wait_ge(step, done[0])

            tt, ts = dve.tensor_tensor, dve.tensor_scalar
            dve.wait_ge(iot, 4)
            dve.tensor_copy(shi[:, 0, :], tk[:, :, 2])
            dve.tensor_copy(shi[:, 1, :], tk[:, :, 1]).then_inc(mo_ready, 1)
            ts(ff[:, :, :], vri[:, :, 68:70], 0.0, None, ALU.max)
            ts(va2[:, :], vri[:, :, 69], 0.0, None, ALU.is_gt)
            ts(tf[:, :], keep["tid"][:, :], 2.5, None, ALU.is_gt)
            link(ts(va[:, :], tk[:, :, 0], 0.0, None, ALU.is_gt))
            link(tt(va[:, :], va[:, :], tf[:, :], ALU.mult))
            link(tt(tlv[:, :], tk[:, :, 2], va[:, :], ALU.mult))

            def inputs(u):
                s = slice(u * HB, (u + 1) * HB)

                def bc(ap):
                    return ap.unsqueeze(2).to_broadcast([128, HB, NF])

                cols = io64[:, :].unsqueeze(1).to_broadcast([128, HB, NF])
                tt(sel[:, s, 0, :], vri[:, s, 68:69].to_broadcast([128, HB, NF]), cols, ALU.is_equal)
                link(tt(sel[:, s, 1, :], bc(ff[:, s, 1]), cols, ALU.is_equal))
                tt(mo[:, s, 0:NF], vr[:, s, 0:NF], bc(va[:, s]), ALU.mult)
                link(tt(sel[:, s, 1, :], sel[:, s, 1, :], bc(va2[:, s]), ALU.mult))
                tt(mo[:, s, NF:2 * NF], vr[:, s, 0:NF], bc(tlv[:, s]), ALU.mult)
                tt(mo[:, s, 2 * NF:3 * NF], sel[:, s, 1, :], bc(va[:, s]), ALU.mult)
                tt(mo[:, s, 3 * NF:4 * NF], sel[:, s, 1, :], bc(tlv[:, s]), ALU.mult)
                dve.tensor_copy(mo[:, s, 4 * NF], va[:, s])
                dve.tensor_copy(mo[:, s, 4 * NF + 1], tlv[:, s]).then_inc(mo_ready, 1)

            def sums(u):
                for b in range(u * HB, (u + 1) * HB):
                    dve.wait_ge(summed, b + 2)
                    p = pp[b % 2]
                    tt(pk[:, b % HB, :].rearrange("p (g c f) -> p g c f", g=2, c=2),
                       p[:, 0:4 * NF].rearrange("p (g c f) -> p g c f", g=2, c=2),
                       sel[:, b, :, :].unsqueeze(2).to_broadcast([128, 2, 2, NF]), ALU.mult)
                    dve.tensor_copy(pc[:, b, :], p[:, 4 * NF:4 * NF + 2]).then_inc(sum_taken, 1)
                dve.wait_ge(sum_taken, (u + 1) * HB + 1)

            def features(u):
                s = slice(u * HB, (u + 1) * HB)
                link(dve.tensor_reduce(ps4[:, s, :], pk[:, :, :].rearrange("p b (k f) -> p b k f", f=NF), AX.X,
                                       ALU.add))
                link(ts(rc[:, s], pc[:, s, 0], 1.0, None, ALU.max))
                link(dve.reciprocal(rc[:, s], rc[:, s]))
                inv = 1.0 / (TXT - 1)
                ts(ft[:, s, 74:76], pc[:, s, :], inv, None, ALU.mult)
                ts(ft[:, s, 76:78], ps4[:, s, 0:2], inv, None, ALU.mult)
                tt(ft[:, s, 78], ps4[:, s, 0], rc[:, s], ALU.mult)
                ts(ft[:, s, 79:81], ps4[:, s, 2:4], inv, None, ALU.mult)
                link(tt(ft[:, s, 81], ps4[:, s, 2], rc[:, s], ALU.mult))
                dve.wait_ge(ft_copied, u + 1)
                for b in range(u * HB, (u + 1) * HB):
                    a = dve.bn_stats(st[:, b, :], ft[:, b, :])
                link(a)
                ev, od = (FEAT + 1) // 2, FEAT // 2
                ts(mu[:, s], st[:, s, 1], ev / FEAT, None, ALU.mult)
                tt(ve[:, s], st[:, s, 2], st[:, s, 5], ALU.add)
                link(tt(df[:, s], st[:, s, 1], st[:, s, 4], ALU.subtract))
                dve.scalar_tensor_tensor(out=mu[:, s], in0=st[:, s, 4], scalar=od / FEAT, in1=mu[:, s],
                                         op0=ALU.mult, op1=ALU.add)
                ts(ve[:, s], ve[:, s], 1.0 / FEAT, EPS, ALU.mult, ALU.add)
                link(tt(df[:, s], df[:, s], df[:, s], ALU.mult))
                dve.scalar_tensor_tensor(out=ve[:, s], in0=df[:, s], scalar=ev * od / FEAT ** 2, in1=ve[:, s],
                                         op0=ALU.mult, op1=ALU.add).then_inc(ft_std, 1)

            def scales(u):
                s = slice(u * HB, (u + 1) * HB)
                dve.wait_ge(ft_sqrt, u + 1)
                link(dve.reciprocal(ve[:, s], ve[:, s]))
                dve.scalar_tensor_tensor(out=nz[:, s], in0=mu[:, s], scalar=-1.0, in1=ve[:, s], op0=ALU.mult,
                                         op1=ALU.mult).then_inc(ft_scale, 1)

            inputs(0)
            dve.tensor_copy(ft[:, :, 0:5], tk[:, :, 0:5])
            ts(ft[:, :, 73], posn[:, :].to_broadcast([128, B]), 1.0 / (TXT - 1), None, ALU.mult)
            dve.tensor_copy(ft[:, :, 84], tk[:, :, 5])
            dve.wait_ge(summed, 1)
            dve.tensor_copy(ft[:, :, 82:84].rearrange("p b c -> p c b"),
                            pp[1][:, 0:2 * B].rearrange("p (c b) -> p c b", c=2)).then_inc(sum_taken, 1)
            inputs(1)
            sums(0)
            features(0)
            scales(0)
            dve.wait_ge(w_in, 16 * 7)
            ts(w2[:, :], w2[:, :], sc[:, 0:1], None, ALU.mult).then_inc(w2_ready, 1)
            sums(1)
            features(1)
            scales(1)

        @block.scalar
        def _(act):
            for u in range(2):
                s = slice(u * HB, (u + 1) * HB)
                act.activation(ft[:, s, 5:5 + NF + 4], vr[:, s, 0:NF + 4], ACT.Copy).then_inc(ft_copied, 1)
            tables.functions(act)
            act.wait_ge(p_in, 96)
            for k in range(2):
                act.wait_ge(p_turned, k + 1)
                act.activation(wi[0:HD, k, :], ph[k][0:HD, 0:E], ACT.Identity, scale=gam[:, k:k + 1]).then_inc(p_taken, 1)
            for k in range(2):
                act.wait_ge(p_turned, 2 + k + 1)
                act.activation(wo[0:EB, 2 * k:2 * k + 2, :].rearrange("p a d -> p (a d)"), ph[k][0:EB, 0:2 * D], ACT.Copy
                               ).then_inc(p_taken, 1)

            def root(u):
                act.wait_ge(ft_std, u + 1)
                act.activation(ve[:, u * HB:(u + 1) * HB], ve[:, u * HB:(u + 1) * HB], ACT.Sqrt).then_inc(ft_sqrt, 1)
                act.wait_ge(ft_scale, u + 1)

            def normalise(n):
                for b in range(4 * n, 4 * n + 4):
                    a = act.activation(ft[:, b, :], ft[:, b, :], ACT.Identity, scale=ve[:, b:b + 1], bias=nz[:, b:b + 1])
                a.then_inc(ft_ready, 1)

            act.wait_ge(w_in, 16 * 7)
            act.wait_ge(iot, 4)
            root(0)
            normalise(0)
            for m in range(NG4 + 2):
                if m < NG4:
                    act.wait_ge(turned, m + 1)
                    if m >= 2:
                        act.wait_ge(hid, m - 1)
                    act.activation(xt[m % 2][:, :, :], pt[m % 2][:], ACT.Identity, bias=lb[:, 0:1], scale=lg[:, 0:1]
                                   ).then_inc(xt_ready, 1)
                if 1 <= m <= NG4:
                    n = m - 1
                    act.wait_ge(hid, n + 1)
                    if n >= 2:
                        act.wait_ge(outp, 2 * (n - 1))
                    act.activation(ht[n % 2][0:NF, :, :].rearrange("p a b -> p (a b)"), ph[n % 2][0:NF, :], ACT.Gelu,
                                   bias=bb[:, 0:1]).then_inc(ht_ready, 1)
                if m + 1 < NG4:
                    if m + 1 == HN:
                        root(1)
                    normalise(m + 1)
                if m >= 2:
                    n = m - 2
                    if n >= 2:
                        act.wait_ge(stored[n % 2], 16 * (n // 2))
                    for k in range(2):
                        act.wait_ge(outp, 2 * n + k + 1)
                        act.activation(ot[n % 2][:, 2 * k:2 * k + 2, :], po[k][:, :, 0:D], ACT.Copy).then_inc(taken, 1)

        @block.tensor
        def _(pe):
            ident = keep["ident"]
            pe.wait_ge(mo_ready, 1)
            pe.matmul(pp[1][:, 0:2 * B], keep["shift"][:], shi[:, :, :].rearrange("p c b -> p (c b)"),
                      start=True, stop=True).then_inc(summed, 1)

            def sums(lo, hi):
                for b in range(lo, hi):
                    pe.wait_ge(sum_taken, b if b else 1)
                    pe.matmul(pp[b % 2][:, 0:4 * NF + 2], keep["before"][:], mo[:, b, :], start=True, stop=True
                              ).then_inc(summed, 1)

            def turn(n):
                pe.wait_ge(ft_ready, n + 1)
                if n >= 2:
                    pe.wait_ge(xt_ready, n - 1)
                for k in range(4):
                    t = pe.transpose(pt[n % 2][:, k, :], ft[:, 4 * n + k, :], ident[:])
                t.then_inc(turned, 1)

            pe.wait_ge(mo_ready, 2)
            sums(0, HB)
            pe.wait_ge(p_in, 96)
            for k in range(2):
                for m in range(3):
                    t = pe.transpose(ph[k][0:HD, m * 128:(m + 1) * 128], win_row[:, m, k * HD:(k + 1) * HD], ident[:])
                t.then_inc(p_turned, 1)
            for k in range(2):
                pe.wait_ge(p_taken, k + 1)
                for n in range(4):
                    t = pe.transpose(ph[k][0:EB, n * HD:(n + 1) * HD],
                                     wout_row[:, n % 2, (2 * k + n // 2) * EB:(2 * k + n // 2 + 1) * EB],
                                     ident[0:HD, 0:HD])
                t.then_inc(p_turned, 1)
            pe.wait_ge(w_in, 16 * 7)
            pe.wait_ge(mo_ready, 3)
            sums(HB, HB + 1)
            for m in range(NG4 + 2):
                if m < NG4:
                    turn(m)
                if 1 <= m <= NG4:
                    n = m - 1
                    pe.wait_ge(xt_ready, n + 1)
                    if n < 2:
                        pe.wait_ge(p_taken, 2 + n + 1)
                    else:
                        pe.wait_ge(ht_ready, n - 1)
                    pe.matmul(ph[n % 2][0:NF, :], w1[:], xt[n % 2][:, :, :].rearrange("p a b -> p (a b)"), start=True,
                              stop=True).then_inc(hid, 1)
                if m < HN - 1:
                    sums(HB + 1 + m * (HB - 1) // (HN - 1), HB + 1 + (m + 1) * (HB - 1) // (HN - 1))
                if m >= 2:
                    n = m - 2
                    pe.wait_ge(ht_ready, n + 1)
                    pe.wait_ge(w2_ready, 1)
                    for k in range(2):
                        if n:
                            pe.wait_ge(taken, 2 * (n - 1) + k + 1)
                        for q in range(2):
                            a = pe.matmul(po[k][:, q, 0:D], ht[n % 2][:, 2 * k + q, :], w2[:], start=True, stop=True)
                        a.then_inc(outp, 1)


class MixerTables:

    def __init__(self, nc, io, dr, keep, sb, sem):
        self.nc, self.io, self.dr, self.keep = nc, io, dr, keep
        self.abc = sb("abc", [EB, 3, NBLK, NS])
        self.cw = sb("cw", [EB, NBLK, TAPS])
        self.lam = sb("lam", [EB, NBLK, NS])
        self.c2 = sb("c2", [EB, NBLK, NS])
        self.t1 = sb("t1", [EB, NBLK, NS])
        self.lags = sb("lags", [EB, 3, NBLK, NS])
        self.u3 = sb("u3", [EB, NBLK])
        self.ex = sb("ex", [EB, NBLK, NS, Q])
        self.mex = sb("mex", [EB, Q])
        self.kr = sb("kr", [EB, NBLK, KREV])
        self.arrived = sem("m_in")
        self.sigmoids = sem("m_sg")
        self.consts = sem("m_iot")
        self.step = sem("m_step")
        self.argument = sem("m_arg")
        self.powers = sem("m_exp")
        self.done_k = sem("m_done")
        self.out = sem("m_out")

    def load(self, sp):
        io = self.io
        for n, name in enumerate(["A", "Bp", "C"]):
            sp.dma_start(self.abc[:, n, :, :], io["L0_attn_" + name].rearrange("(k p) n -> p k n", p=EB)
                         ).then_inc(self.arrived, 16)
        sp.dma_start(self.cw[:, :, :], io["L0_attn_conv_w"].rearrange("(k p) n -> p k n", p=EB)).then_inc(self.arrived, 16)

    def store(self, sp):
        dr, keep, out = self.dr, self.keep, self.out
        sp.wait_ge(self.done_k, 1)
        sp.dma_start(dr["kd"].rearrange("(k p) n -> p k n", p=EB), self.kr[:]).then_inc(out, 16)
        sp.dma_start(dr["lamd"].rearrange("(k p n) -> p k n", p=EB, n=NS), self.lam[:]).then_inc(out, 16)
        sp.dma_start(dr["c2d"].rearrange("(k p n) -> p k n", p=EB, n=NS), self.c2[:]).then_inc(out, 16)
        sp.wait_ge(out, 48)
        with self.nc.allow_non_contiguous_dma(reason="one value per partition"):
            sp.dma_start(keep["lamc"][:], dr["lamd"].rearrange("(g p) -> p g", p=128)).then_inc(out, 16)
            sp.dma_start(keep["c2c"][:], dr["c2d"].rearrange("(g p) -> p g", p=128)).then_inc(out, 16)
        sp.wait_ge(out, 80)

    def constants(self, pool):
        keep, iot, mex = self.keep, self.consts, self.mex
        pool.iota(mex[:], pattern=[[-1, Q]], base=Q - 1, channel_multiplier=0,
                  allow_small_or_imprecise_dtypes=True).then_inc(iot, 1)
        pool.iota(keep["texp"][:], pattern=[[-1, Q]], base=Q, channel_multiplier=0,
                  allow_small_or_imprecise_dtypes=True).then_inc(iot, 1)
        pool.iota(keep["sexp"][:, 0:1], pattern=[[0, 1]], base=Q - 1, channel_multiplier=-1,
                  allow_small_or_imprecise_dtypes=True).then_inc(iot, 1)
        pool.memset(keep["sexp"][:, 1:2], 0.0).then_inc(iot, 1)
        pool.wait_ge(iot, 4)
        pool.affine_select(out=keep["sexp"][:, 0:1], in_=keep["sexp"][:, 0:1], compare_op=ALU.is_ge, fill=0.0,
                           base=Q - 1, pattern=[[0, 1]], channel_multiplier=-1).then_inc(iot, 1)
        pool.affine_select(out=keep["sexp"][:, 1:2], in_=keep["sexp"][:, 1:2], compare_op=ALU.is_ge, fill=-1e4,
                           base=Q - 1, pattern=[[0, 1]], channel_multiplier=-1).then_inc(iot, 1)
        own = keep["own"]
        pool.memset(own[:], 1.0).then_inc(iot, 1)
        pool.wait_ge(iot, 7)
        pool.affine_select(out=own[:], in_=own[:], compare_op=ALU.is_ge, fill=0.0, base=0,
                           pattern=[[-NS, GE]], channel_multiplier=1).then_inc(iot, 1)
        pool.wait_ge(iot, 8)
        pool.affine_select(out=own[:], in_=own[:], compare_op=ALU.is_ge, fill=0.0, base=NS - 1,
                           pattern=[[NS, GE]], channel_multiplier=-1).then_inc(iot, 1)
        pool.wait_ge(iot, 9)

    def functions(self, act):
        abc, ex = self.abc, self.ex
        act.wait_ge(self.arrived, 64)
        act.activation(abc[:], abc[:], ACT.Sigmoid).then_inc(self.sigmoids, 1)
        act.wait_ge(self.sigmoids, 1)
        act.activation(self.lam[:], abc[:, 0, :, :], ACT.Ln).then_inc(self.sigmoids, 1)
        act.wait_ge(self.argument, 1)
        act.activation(ex[:], ex[:], ACT.Exp).then_inc(self.powers, 1)

    def work(self, pool):
        abc, cw, lags, t1, c2, kr, ex, u3 = (self.abc, self.cw, self.lags, self.t1, self.c2, self.kr, self.ex, self.u3)
        a = abc[:, 0, :, :]
        done = [0]
        tt = pool.tensor_tensor

        def link(ins):
            done[0] += 1
            ins.then_inc(self.step, 1)
            pool.wait_ge(self.step, done[0])

        def tap(j):
            return cw[:, :, j:j + 1].to_broadcast([EB, NBLK, NS])

        link(pool.memset(kr[:], 0.0))
        pool.wait_ge(self.arrived, 64)
        pool.wait_ge(self.sigmoids, 2)
        tt(ex[:].rearrange("p k n q -> p (k n) q"),
           self.lam[:].rearrange("p k n -> p (k n)").unsqueeze(2).to_broadcast([EB, NBLK * NS, Q]),
           self.mex[:, :].unsqueeze(1).to_broadcast([EB, NBLK * NS, Q]), ALU.mult).then_inc(self.argument, 1)
        link(tt(t1[:], a, tap(3), ALU.mult))
        link(tt(lags[:, 0, :, :], abc[:, 1, :, :], abc[:, 2, :, :], ALU.mult))
        for j in (2, 1):
            link(tt(t1[:], t1[:], tap(j), ALU.add))
            link(tt(t1[:], t1[:], a, ALU.mult))
        link(tt(t1[:], t1[:], tap(0), ALU.add))
        link(tt(c2[:], t1[:], lags[:, 0, :, :], ALU.mult))
        for lag in (1, 2):
            link(tt(lags[:, lag, :, :], lags[:, lag - 1, :, :], a, ALU.mult))
        n = NS // 2
        while n:
            link(tt(lags[:, :, :, 0:n], lags[:, :, :, 0:n], lags[:, :, :, n:2 * n], ALU.add))
            n //= 2
        for lag in range(3):
            col = kr[:, :, HALO + Q - 1 - lag]
            link(tt(col, lags[:, lag, :, 0], cw[:, :, 3], ALU.mult))
            for j in range(1, lag + 1):
                link(tt(u3[:], lags[:, lag - j, :, 0], cw[:, :, 3 - j], ALU.mult))
                link(tt(col, col, u3[:], ALU.add))
        pool.wait_ge(self.powers, 1)
        link(tt(ex[:].rearrange("p k n q -> p (k n) q"), ex[:].rearrange("p k n q -> p (k n) q"),
                c2[:].rearrange("p k n -> p (k n)").unsqueeze(2).to_broadcast([EB, NBLK * NS, Q]), ALU.mult))
        n = NS // 2
        while n > 1:
            link(tt(ex[:, :, 0:n, :], ex[:, :, 0:n, :], ex[:, :, n:2 * n, :], ALU.add))
            n //= 2
        link(tt(kr[:, :, 0:Q], ex[:, :, 0, :], ex[:, :, 1, :], ALU.add))
        pool.sem_inc(self.done_k, 1)


def hold(eng, tick):
    eng.sem_inc(tick, 1)


def normalise_in(nc, io, dr, keep, xn):
    with ExitStack() as ctx:
        def sb(name, shape, dt=F32):
            return ctx.enter_context(nc.sbuf_tensor(name, shape, dt))

        def sem(name):
            return ctx.enter_context(nc.semaphore(name))

        TS = 8
        NS4 = Q // TS
        PARTS4 = ((0, 3), (3, 6), (6, 9), (9, NS4 + 1))
        h = sb("h4", [CB, Q, D])
        st = sb("st4", [CB, Q, 6])
        df = sb("df4", [CB, Q])
        vv = sb("vv4", [CB, 2, Q])
        zs = sb("zs4", [CB, Q])
        nz = sb("nz4", [CB, Q])
        z = [[sb(f"z4{j}{k}", [CB, 2, D]) for k in range(2)] for j in range(2)]
        pz = [[bank(nc, ctx, f"pz{j}{k}", [HD, 4, CB]) for k in range(2)] for j in range(2)]
        h_in = [sem(f"h_in{n}") for n in range(len(PARTS4))]
        step = sem("s4")
        var_ok = sem("var4")
        root = sem("root4")
        zs_ok = sem("zs4s")
        ready = [sem("z_ready0"), sem("z_ready1")]
        turned = [sem("z_turned0"), sem("z_turned1")]
        taken = [sem("z_taken0"), sem("z_taken1")]
        ones = sem("ones4")
        tick = keep["tick"]
        tick_d = keep["tick_d"]
        block = ctx.enter_context(nc.Block())
        mu, rs = keep["mu"], keep["rs"]

        def tokens(n):
            lo, hi = PARTS4[n]
            return TS * lo, min(TS * hi, Q)

        def scatter_cols(t):
            full = xn[0:HD, :, :, :]
            return full[:, :, :, HALO:HALO + LP].rearrange("p k b (c t) -> p k b c t", c=NCHUNK)[:, :, :, :, bass.ds(t, 1)]

        def turned_token(j, k, i):
            return pz[j][k][:, 2 * i:2 * i + 2, :].rearrange("p k (b c) -> p k b c", c=NCHUNK).unsqueeze(4)

        def token(t):
            return h[:, bass.ds(t, 1), :].rearrange("p a d -> p (a d)")

        @block.sync
        def _(sp):
            hv = dr["h0"].rearrange("(p t) d -> p t d", t=Q)
            for n in range(len(PARTS4)):
                lo, hi = tokens(n)
                sp.dma_start(h[:, lo:hi, :], hv[:, lo:hi, :]).then_inc(h_in[n], 16)

        @block.gpsimd
        def _(pool):
            pool.memset(xn[0:HD, :, :, 0:HALO], 0.0).then_inc(ones, 1)
            pool.wait_ge(ones, 1)
            pool.memset(xn[HD:HD + 1, 1, :, HALO:], 1.0).then_inc(ones, 1)
            pool.memset(xn[HD:HD + 1, 1, :, 0:HALO], 0.0).then_inc(ones, 1)

        @block.vector
        def _(dve):
            done = [0]
            tt, ts, stt = dve.tensor_tensor, dve.tensor_scalar, dve.scalar_tensor_tensor

            def link(ins):
                done[0] += 1
                ins.then_inc(step, 1)
                dve.wait_ge(step, done[0])

            def stats(t):
                dve.bn_stats(st[:, bass.ds(t, 1), :].rearrange("p a s -> p (a s)"), token(t))

            def moments(n):
                lo, hi = tokens(n)
                link(dve.memset(zs[:, lo:hi], 0.0))
                tt(mu[:, lo:hi], st[:, lo:hi, 1], st[:, lo:hi, 4], ALU.add)
                tt(vv[:, 1, lo:hi], st[:, lo:hi, 2], st[:, lo:hi, 5], ALU.add)
                link(tt(df[:, lo:hi], st[:, lo:hi, 1], st[:, lo:hi, 4], ALU.subtract))
                ts(mu[:, lo:hi], mu[:, lo:hi], 0.5, None, ALU.mult)
                ts(vv[:, 1, lo:hi], vv[:, 1, lo:hi], 1.0 / D, None, ALU.mult)
                link(tt(df[:, lo:hi], df[:, lo:hi], df[:, lo:hi], ALU.mult))
                link(stt(out=vv[:, 1, lo:hi], in0=df[:, lo:hi], scalar=0.25, in1=vv[:, 1, lo:hi], op0=ALU.mult,
                         op1=ALU.add))
                ts(vv[:, 0, lo:hi], vv[:, 1, lo:hi], EPS, None, ALU.add).then_inc(var_ok, 1)

            def scales(n):
                lo, hi = tokens(n)
                s = zs[:, lo:hi]
                dve.wait_ge(root, n + 1)
                link(dve.reciprocal(rs[:, lo:hi], vv[:, 0, lo:hi]))
                link(tt(s, vv[:, 1, lo:hi], rs[:, lo:hi], ALU.mult))
                link(ts(s, s, 1e-6, None, ALU.add))
                link(dve.reciprocal(s, s))
                link(tt(s, s, rs[:, lo:hi], ALU.mult))
                stt(out=nz[:, lo:hi], in0=mu[:, lo:hi], scalar=-1.0, in1=s, op0=ALU.mult, op1=ALU.mult
                    ).then_inc(zs_ok, 1)
                dve.wait_ge(zs_ok, n + 1)

            def take(m, k):
                dve.wait_ge(turned[1], 2 * m + k + 1)
                hold(dve, tick_d)
                for i in range(2):
                    c = dve.tensor_copy(scatter_cols(TS * m + 4 * k + 2 + i), turned_token(1, k, i))
                c.then_inc(taken[1], 1)

            def make(m, k):
                for i in range(2):
                    t = TS * m + 4 * k + 2 + i
                    c = ts(z[1][k][:, i, :], token(t), zs[:, bass.ds(t, 1)], nz[:, bass.ds(t, 1)], ALU.mult, ALU.add)
                c.then_inc(ready[1], 1)

            def statistics(n):
                dve.wait_ge(h_in[n], 16)
                lo, hi = tokens(n)
                unroll = TS if (hi - lo) % TS == 0 else 5
                with dve.Fori(0, (hi - lo) // unroll) as i:
                    for a in range(unroll):
                        stats(unroll * i + lo + a)
                moments(n)

            statistics(0)
            scales(0)
            make(0, 0)
            make(0, 1)
            for n, (lo, hi) in enumerate(PARTS4):
                if n:
                    scales(n)
                more = n + 1 < len(PARTS4)
                if more:
                    statistics(n + 1)
                with dve.Fori(max(lo, 1), min(hi, NS4)) as m:
                    for k in range(2):
                        take(m - 1, k)
                        make(m, k)
            for k in range(2):
                take(NS4 - 1, k)
            dve.wait_ge(taken[1], 2 * NS4)

        @block.scalar
        def _(act):
            def take(m, k):
                act.wait_ge(turned[0], 2 * m + k + 1)
                hold(act, tick)
                for i in range(2):
                    c = act.activation(scatter_cols(TS * m + 4 * k + i), turned_token(0, k, i), ACT.Copy)
                c.then_inc(taken[0], 1)

            def make(m, k):
                for i in range(2):
                    t = TS * m + 4 * k + i
                    c = act.activation(z[0][k][:, i, :], token(t), ACT.Identity, scale=zs[:, bass.ds(t, 1)],
                                       bias=nz[:, bass.ds(t, 1)])
                c.then_inc(ready[0], 1)

            for n, (lo, hi) in enumerate(PARTS4):
                a, b = tokens(n)
                act.wait_ge(var_ok, n + 1)
                act.activation(vv[:, :, a:b], vv[:, :, a:b], ACT.Sqrt).then_inc(root, 1)
                act.wait_ge(zs_ok, n + 1)
                if not n:
                    make(0, 0)
                    make(0, 1)
                with act.Fori(max(lo, 1), min(hi, NS4)) as m:
                    for k in range(2):
                        take(m - 1, k)
                        make(m, k)
            take(NS4 - 1, 0)
            make(NS4, 0)
            take(NS4 - 1, 1)
            take(NS4, 0)

        @block.tensor
        def _(pe):
            def turn(m, j, k):
                pe.wait_ge(ready[j], 2 * m + k + 1)
                pe.wait_ge(taken[j], 2 * m + k + 1)
                for i in range(2):
                    for f in range(2):
                        t = pe.transpose(pz[j][k][:, 2 * i + f, :], z[j][k][:, i, f * HD:(f + 1) * HD], keep["ident"][:])
                t.then_inc(turned[j], 1)

            for j in range(2):
                pe.sem_inc(taken[j], 2)
            with pe.Fori(0, NS4) as m:
                for k in range(2):
                    for j in range(2):
                        turn(m, j, k)
            turn(NS4, 0, 0)


XU = CB // 4
IU = EB // 4
TU = [4] * 10 + [3] * 14
UNITS = XU + IU + len(TU)
PARTS = IU


def mix(nc, io, dr, keep, xn):
    with ExitStack() as ctx:
        def sb(name, shape, dt=F32):
            return ctx.enter_context(nc.sbuf_tensor(name, shape, dt))

        def sem(name):
            return ctx.enter_context(nc.semaphore(name))

        x = sb("x5", [W, CB, EB])
        y = sb("y5", [CB, EB, Q])
        gp = [sb(f"gp{j}", [96, GE * GPW + 32]) for j in range(2)]
        lg = [sb(f"lg{j}", [96, GE * NS]) for j in range(2)]
        sm = [sb(f"sm{j}", [CB, GE * NS]) for j in range(2)]
        ht = [sb(f"hs{j}", [128, B, NCHUNK]) for j in range(2)]
        rr = [sb(f"rr{j}", [128, Q]) for j in range(2)]
        bd = [sb(f"bd{j}", [128, GE, Q]) for j in range(2)]
        mc = sb("mc5", [128, NBLK * NG, GE])
        aq = sb("aq5", [128, NBLK * NG])
        yt = [sb(f"yt{j}", [EB, 4, CB]) for j in range(4)]
        pa = [bank(nc, ctx, f"pa{j}", [128, 4, 128]) for j in range(4)]
        pst = bank(nc, ctx, "pst", [128, B, NCHUNK])
        pb = [bank(nc, ctx, f"pb{j}", [128, 4, Q]) for j in range(2)]

        setup = sem("set5")
        aq_ok = sem("aq_ok")
        g_in = [sem("g_in0"), sem("g_in1")]
        p_ok = sem("p_ok")
        unit = sem("unit")
        free = [sem("free_act"), sem("free_dve")]
        s_ok = [sem("s_ok_act"), sem("s_ok_dve")]
        st_ok = sem("st_ok")
        h_ok = sem("h_ok")
        r_ok = sem("r_ok")
        bd_ok = sem("bd_ok")
        inter = sem("inter")
        added = sem("added")
        step = sem("s5")
        stored = [sem(f"yst{j}") for j in range(4)]
        tick = keep["tick"]
        tick_p = keep["tick_p"]
        tick_s = keep["tick_s"]
        block = ctx.enter_context(nc.Block())
        own, lamc, c2c, texp, sexp = (keep[k] for k in ("own", "lamc", "c2c", "texp", "sexp"))

        def cols(j, e):
            return gp[j][0:W, e * GPW:e * GPW + 128]

        @block.sync
        def _(sp):
            def load(k, g):
                j = g % 2
                last = XU + 2 * (g - 1) + UNITS if g >= 2 else XU + 2 * (NG + g - 1)
                sp.wait_ge(unit, k * UNITS + last)
                hold(sp, tick_s)
                first = k * EB + g * GE
                src = bass.AP(tensor=dr["kd"].tensor, offset=first * KREV, ap=[[1, 96], [KREV, GE], [1, Q]])
                sp.dma_start(gp[j][:, 0:GE * GPW].rearrange("r (e q) -> r e q", q=GPW)[:, :, 0:Q], src
                             ).then_inc(g_in[j], 16)
                lamsrc = bass.AP(tensor=dr["lamd"].tensor, offset=first * NS, ap=[[0, 96], [1, GE * NS]])
                sp.dma_start(lg[j][:], lamsrc).then_inc(g_in[j], 16)

            def store(k, n):
                t0 = sum(TU[:n])
                sp.wait_ge(free[n % 2], (k + 1) * (UNITS // 2) - len(TU) // 2 + n // 2 + 3)
                hold(sp, tick_s)
                sp.dma_start(dr["yd"][bass.ds(k * EB, EB), t0 * CB:(t0 + TU[n]) * CB],
                             yt[n % 4][:, 0:TU[n], :].rearrange("e t c -> e (t c)")).then_inc(stored[n % 4], 16)

            with sp.Fori(0, NBLK) as k:
                for g in range(NG):
                    load(k, g)
                for n in range(len(TU)):
                    store(k, n)
            for j in range(4):
                sp.wait_ge(stored[j], 16 * (NBLK * len(TU) // 4 + 1))

        @block.gpsimd
        def _(pool):
            for j in range(2):
                pool.memset(gp[j][:, GE * GPW:], 0.0).then_inc(setup, 1)
                pool.memset(ht[j][:, :, 0], 0.0).then_inc(setup, 1)
            pool.tensor_tensor(mc[:], own[:, :].unsqueeze(1).to_broadcast([128, NBLK * NG, GE]),
                               c2c[:, :].unsqueeze(2).to_broadcast([128, NBLK * NG, GE]), ALU.mult).then_inc(setup, 1)
            pool.wait_ge(setup, 5)
            pool.sem_inc(inter, 4)
            with pool.Fori(0, NBLK) as k:
                for g in range(NG):
                    n = k * NG + g
                    pool.wait_ge(r_ok, n + 1)
                    hold(pool, tick_p)
                    pool.wait_ge(inter, 2 * n + 2)
                    hold(pool, tick_p)
                    pool.tensor_tensor(bd[g % 2][:], rr[g % 2][:, :].unsqueeze(1).to_broadcast([128, GE, Q]),
                                       mc[:, bass.ds(n, 1), :].rearrange("p a e -> p (a e)").unsqueeze(2)
                                       .to_broadcast([128, GE, Q]), ALU.mult).then_inc(bd_ok, 1)

        def read_unit(eng, copy, k, m, who):
            eng.wait_ge(unit, (k + 1) * UNITS + m + 1)
            hold(eng, tick)
            p = pa[m % 4]
            if m < XU:
                copy(x[:, 4 * m:4 * m + 4, :].rearrange("w c e -> w (c e)"),
                     p[0:W, :, :].rearrange("w a b -> w (a b)")[:, 0:4 * EB]).then_inc(free[who], 1)
            elif m < XU + IU:
                n = m - XU
                g = n // 2
                eng.wait_ge(st_ok, k * NG + g + 1)
                copy(sm[g % 2][:, (n % 2) * 64:(n % 2) * 64 + 64].rearrange("c (e n) -> c e n", n=NS),
                     p[:, :, Q:GPW]).then_inc(s_ok[who], 1)
                copy(y[:, 4 * n:4 * n + 4, :], p[:, :, 0:Q]).then_inc(free[who], 1)
            else:
                n = m - XU - IU
                q = n % 4
                eng.wait_ge(stored[q], 16 * (k * (len(TU) // 4) + n // 4 + 1))
                copy(yt[q][:, 0:TU[n], :], p[0:EB, 0:TU[n], :]).then_inc(free[who], 1)

        @block.scalar
        def _(act):
            def copy(out, in_):
                return act.activation(out, in_, ACT.Copy)

            def tables(k, g):
                n = k * NG + g
                j = g % 2
                act.wait_ge(g_in[j], 32 * (k * (NG // 2) + g // 2 + 1))
                hold(act, tick)
                act.activation(gp[j][:, 0:GE * GPW].rearrange("r (e q) -> r e q", q=GPW)[:, :, Q:GPW],
                               lg[j][:, :].rearrange("r (e n) -> r e n", n=NS), ACT.Exp,
                               scale=sexp[:, 0:1], bias=sexp[:, 1:2]).then_inc(p_ok, 1)
                act.wait_ge(bd_ok, n + 1)
                hold(act, tick)
                act.activation(rr[j][:], texp[:, :], ACT.Exp, scale=lamc[:, bass.ds(n, 1)]).then_inc(r_ok, 1)

            act.activation(aq[:], lamc[:], ACT.Exp, scale=float(Q)).then_inc(aq_ok, 1)
            act.sem_inc(bd_ok, 2)
            act.sem_inc(st_ok, 2)
            act.sem_inc(stored[0], 16)
            act.sem_inc(stored[2], 16)
            with act.Fori(0, NBLK) as k:
                for m in range(0, XU, 2):
                    read_unit(act, copy, k, m, 0)
                tables(k, 0)
                tables(k, 1)
                for g in range(NG):
                    read_unit(act, copy, k, XU + 2 * g, 0)
                    if g + 2 < NG:
                        tables(k, g + 2)
                for m in range(XU + IU, UNITS, 2):
                    read_unit(act, copy, k, m, 0)

        @block.vector
        def _(dve):
            def carry(k, g):
                n = k * NG + g
                j = g % 2
                dve.wait_ge(st_ok, n + 3)
                dve.wait_ge(inter, 2 * n + 2)
                hold(dve, tick)
                dve.tensor_copy(ht[j][:, :, 1], pst[:, :, 0]).then_inc(step, 1)
                for c in range(2, NCHUNK):
                    dve.wait_ge(step, 3 * n + c - 1)
                    ins = dve.scalar_tensor_tensor(out=ht[j][:, :, c], in0=ht[j][:, :, c - 1],
                                                   scalar=aq[:, bass.ds(n, 1)], in1=pst[:, :, c - 1],
                                                   op0=ALU.mult, op1=ALU.add)
                    ins.then_inc(step, 1)
                dve.wait_ge(step, 3 * n + 3)
                hold(dve, h_ok)

            def add(k, g):
                n = k * NG + g
                for q in range(2):
                    dve.wait_ge(inter, 2 * n + q + 5)
                    dve.wait_ge(free[q], k * (UNITS // 2) + XU // 2 + g + 3)
                    hold(dve, tick)
                    e0 = g * GE + 4 * q
                    dve.tensor_tensor(y[:, e0:e0 + 4, :], y[:, e0:e0 + 4, :], pb[q][:], ALU.add).then_inc(added, 1)

            dve.sem_inc(stored[1], 16)
            dve.sem_inc(stored[3], 16)
            dve.wait_ge(setup, 5)
            dve.wait_ge(aq_ok, 1)
            with dve.Fori(0, NBLK) as k:
                for m in range(1, XU, 2):
                    read_unit(dve, dve.tensor_copy, k, m, 1)
                for g in range(NG):
                    read_unit(dve, dve.tensor_copy, k, XU + 2 * g + 1, 1)
                    if g >= 1:
                        carry(k, g - 1)
                    if g >= 2:
                        add(k, g - 2)
                carry(k, NG - 1)
                add(k, NG - 2)
                add(k, NG - 1)
                for m in range(XU + IU + 1, UNITS, 2):
                    read_unit(dve, dve.tensor_copy, k, m, 1)

        @block.tensor
        def _(pe):
            ident = keep["ident"]

            def bank(k, m):
                pe.wait_ge(free[m % 2], k * (UNITS // 2) + m // 2 + 1)
                return pa[m % 4]

            def turn_states(k, g):
                n = k * NG + g
                for who in range(2):
                    pe.wait_ge(s_ok[who], n + 1)
                pe.wait_ge(h_ok, n + 1)
                pe.transpose(pst[:, :, :].rearrange("s b c -> s (b c)"), sm[g % 2][:], ident[:]).then_inc(st_ok, 1)

            def reach(k, g):
                n = k * NG + g
                pe.wait_ge(h_ok, n + 2)
                pe.wait_ge(bd_ok, n + 3)
                for q in range(2):
                    pe.wait_ge(added, 2 * n + q + 1)
                    pe.matmul(pb[q][:].rearrange("c e t -> c (e t)"), ht[g % 2][:].rearrange("s b c -> s (b c)"),
                              bd[g % 2][:, 4 * q:4 * q + 4, :].rearrange("s e t -> s (e t)"),
                              start=True, stop=True).then_inc(inter, 1)

            pe.sem_inc(unit, UNITS)
            pe.sem_inc(free[0], 2)
            pe.sem_inc(free[1], 2)
            pe.sem_inc(h_ok, 1)
            pe.sem_inc(added, 2)
            pe.wait_ge(setup, 5)
            with pe.Fori(0, NBLK) as k:
                for m in range(XU):
                    p = bank(k, m)[0:W, :, :].rearrange("w a b -> w (a b)")
                    for i in range(4):
                        b, c = divmod(4 * m + i, NCHUNK)
                        for f in range(2):
                            rows = HD + f
                            mm = pe.matmul(p[:, i * EB:(i + 1) * EB], xn[0:rows, f, b, c * Q:c * Q + W],
                                           keep["wi"][0:rows, f, bass.ds(k * EB, EB)],
                                           start=(f == 0), stop=(f == 1))
                    mm.then_inc(unit, 1)
                for who in range(2):
                    pe.wait_ge(free[who], k * (UNITS // 2) + XU // 2 + 2)
                for g in range(NG):
                    pe.wait_ge(p_ok, k * NG + g + 1)
                    for q in range(2):
                        p = bank(k, XU + 2 * g + q)
                        for i in range(4):
                            e = 4 * q + i
                            mm = pe.matmul(p[:, i, :], x[:, :, g * GE + e], cols(g % 2, e), start=True, stop=True)
                        mm.then_inc(unit, 1)
                    if g >= 1:
                        turn_states(k, g - 1)
                    if g >= 2:
                        reach(k, g - 2)
                turn_states(k, NG - 1)
                reach(k, NG - 2)
                reach(k, NG - 1)
                pe.wait_ge(added, 2 * (k * NG + NG) + 2)
                t0 = 0
                for n, size in enumerate(TU):
                    p = bank(k, XU + IU + n)
                    for i in range(size):
                        tr = pe.transpose(p[0:EB, i, :], y[:, :, t0 + i], ident[:])
                    tr.then_inc(unit, 1)
                    t0 += size


def project_route(nc, io, dr, keep, late):
    with ExitStack() as ctx:
        def sb(name, shape, dt=F32):
            return ctx.enter_context(nc.sbuf_tensor(name, shape, dt))

        def sem(name):
            return ctx.enter_context(nc.semaphore(name))

        PG = 4
        TG = 2 * PG
        NFULL = Q // TG
        NP = Q // 2
        hb = [sb(f"hb{j}", [CB, 2, D]) for j in range(PG)]
        yt = [sb(f"y6{j}", [EB + 1, NBLK, 2, CB]) for j in range(PG)]
        row = [sb(f"row{j}", [CB, TG, ROW]) for j in range(2)]
        st = [sb(f"st6{j}", [CB, TG, 6]) for j in range(2)]
        zt = [sb(f"zt6{j}", [HD, 2, 2, CB]) for j in range(2)]
        s1 = sb("s1", [CB, Q])
        s2 = sb("s2", [CB, Q])
        ws = sb("ws", [HD, 2, NEX])
        bs = sb("bs", [CB, NEX])
        sm = sb("sm6", [CB, TG])
        df = sb("df", [CB, TG])
        vs = sb("vs", [CB, TG])
        sd = sb("sd6", [CB, TG])
        lo = sb("lo", [CB, TG, NEX])
        mx = sb("mx", [CB, TG])
        dl = sb("dl", [CB, TG, NEX])
        ex = sb("ex6", [CB, TG, NEX])
        scr = sb("scr", [CB, TG, NEX])
        oh = sb("oh", [CB, NEX * TG])
        inc = sb("inc", [CB, NEX * TG])
        incb = sb("incb", [CB, NEX * TG])
        base = sb("base", [CB, NEX])
        rk = sb("rk", [CB, NEX * TG])
        slf = sb("slf", [CB, TG])
        sli = [sb(f"sli{j}", [CB, TG], I32) for j in range(2)]
        ssum = sb("ssum", [CB, TG])
        w8 = sb("w8", [CB, NEX])
        ecap = sb("ecap", [CB, NEX])
        mask8 = sb("mask8", [CB, NEX, TG])
        mask2 = sb("mask2", [CB, NEX, 2])
        bm = sb("bm", [CB, CB])
        pad = sb("pad", [CB, Q])
        orow = sb("orow", [CB, Q], I32)
        orf = sb("orf", [CB, Q])
        pid = sb("pid", [CB, 1], I32)
        pint = sb("pint", [CB, 2], I32)
        pcol = sb("pcol", [CB, 4])
        xs0 = sb("xs06", [128, ROW])
        tint = sb("tint", [CB, NEX], I32)
        tiles = sb("tiles", [CB, NEX])
        tend = sb("tend", [CB, NEX])
        ei = sb("ei", [CB, NEX], I32)
        ef = sb("ef", [CB, NEX])
        tie = sb("tie", [1, NTILE])
        tsum = sb("tsum", [1, NTILE])
        tst = sb("tst", [1, NTILE])
        cmp_ = sb("cmp", [1, NTILE, NEX])
        po = [bank(nc, ctx, f"p6{j}", [CB, 2, 256]) for j in range(2)]
        pz = [bank(nc, ctx, f"pz6{j}", [HD, 4, CB]) for j in range(2)]
        pl = [bank(nc, ctx, f"pl{j}", [CB, TG, NEX]) for j in range(2)]
        pr = bank(nc, ctx, "pr", [CB, NEX * TG])
        pc = bank(nc, ctx, "pc6", [CB, NEX])

        y_in = [sem(f"y_in{j}") for j in range(PG)]
        w_in = sem("w6_in")
        iot = sem("iot6")
        xs_z = sem("xs_z")
        sc_ok = sem("sc_ok")
        tab_ok = sem("tab_ok")
        wsum = sem("wsum")
        hb_ok = sem("hb_ok")
        out_ok = sem("out_ok")
        h_done = sem("h_done")
        tz = sem("tz")
        zt_ok = sem("zt_ok6")
        lg_ok = sem("lg_ok")
        var_ok = sem("var6")
        root = sem("root6")
        l_taken = sem("l_taken")
        d_ok = sem("d_ok")
        ex_ok = sem("ex_ok")
        oh_ok = sem("oh_ok")
        rank_ok = sem("rank_ok")
        rows_ok = sem("rows_ok")
        row_free = sem("row_free")
        step = sem("s6")
        fstep = sem("f6")
        cnt_in = sem("cnt_in")
        cnt_ok = sem("cnt_ok")
        tail_ok = sem("tail_ok")
        sent = keep["scattered"]
        spared = sem("spared")
        tick = keep["tick"]
        tick_s = keep["tick_s"]
        tick_p = keep["tick_p"]
        wl = keep["wl"]
        block = ctx.enter_context(nc.Block())
        mu, rs = keep["mu"], keep["rs"]
        w1, w2, b2 = late["w1"], late["w2"], late["b2"]

        def groups(eng, body):
            body(0, 0, True)
            body(1, 1, False)
            with eng.Fori(1, NFULL // 2) as i:
                for a in range(2):
                    body(2 * i + a, a, False)

        @block.sync
        def _(sp):
            ydv = dr["yd"].rearrange("(k p) (t c) -> p k t c", p=EB, c=CB)
            hv = dr["h0"].rearrange("(p t) d -> p t d", t=Q)

            def load(p, q):
                sp.wait_ge(h_done, p + 1)
                hold(sp, tick_s)
                sp.dma_start(yt[q][0:EB, :, :, :], ydv[:, :, bass.ds(Q - 2 - 2 * p, 2), :]).then_inc(y_in[q], 16)
                sp.dma_start(hb[q][:], hv[:, bass.ds(2 * p, 2), :]).then_inc(y_in[q], 16)

            sp.sem_inc(h_done, 4)
            with sp.Fori(0, NFULL) as g:
                for q in range(PG):
                    load(PG * g + q, q)
            load(NP - 1, 0)

        @block.gpsimd
        def _(pool):
            for j in range(PG):
                pool.memset(yt[j][EB:EB + 1, :, :, :], 1.0).then_inc(iot, 1)
            pool.wait_ge(iot, PG)
            pool.iota(pid[:], pattern=[[0, 1]], base=0, channel_multiplier=1).then_inc(iot, 1)
            fl = dict(allow_small_or_imprecise_dtypes=True)
            pool.iota(orf[:], pattern=[[1, Q]], base=0, channel_multiplier=Q, **fl).then_inc(iot, 1)
            pool.iota(tie[:], pattern=[[1, NTILE]], base=0, channel_multiplier=0, **fl).then_inc(iot, 1)
            pool.iota(w8[:], pattern=[[-1, NEX]], base=NEX, channel_multiplier=0, **fl).then_inc(iot, 1)
            pool.iota(ecap[:], pattern=[[CAP, NEX]], base=0, channel_multiplier=0, **fl).then_inc(iot, 1)
            pool.memset(xs0[:], 0.0).then_inc(xs_z, 1)
            pool.wait_ge(xs_z, 1)
            pool.memset(xs0[:, ROW - 1:ROW].bitcast(I32), FAR).then_inc(xs_z, 1)
            bound = pool.to_reg(NEX * CAP - 1)
            pool.sem_inc(row_free, 2)

            def scatter(g, j, n):
                pool.wait_ge(rows_ok, g + 2)
                hold(pool, tick_p)
                for t in range(n):
                    pool.indirect_dma_start(dr["xs"], bass.IndirectOffsetOnAxis(ap=sli[j][:, t:t + 1], axis=0),
                                            row[j][:, t, :], None, bounds_check=bound, oob_is_err=False
                                            ).then_inc(sent, 16)
                pool.wait_ge(sent, 16 * TG * g + 16 * n)
                hold(pool, row_free)

            with pool.Fori(0, NFULL // 2) as i:
                for a in range(2):
                    scatter(2 * i + a, a, TG)
            scatter(NFULL, 0, 2)
            pool.wait_ge(tail_ok, 1)
            pool.wait_ge(xs_z, 2)
            for e in range(NEX):
                pool.indirect_dma_start(dr["xs"], bass.IndirectOffsetOnAxis(ap=ei[:, e:e + 1], axis=0),
                                        xs0[:, :], None, bounds_check=bound, oob_is_err=False).then_inc(sent, 16)
            pool.wait_ge(sent, 16 * (Q + NEX))

        @block.scalar
        def _(act):
            act.dma_start(ws[:, 0, :], io["L0_ffn_Ws"][0:HD, :]).then_inc(w_in, 16)
            act.dma_start(ws[:, 1, :], io["L0_ffn_Ws"][HD:D, :]).then_inc(w_in, 16)
            act.dma_start(bs[:], io["L0_ffn_bs"].partition_broadcast(CB)).then_inc(w_in, 16)
            act.wait_ge(xs_z, 2)
            act.dma_start(dr["xs"][NEX * CAP:NEX * CAP + SPARE * 128, :].rearrange("(p n) d -> p n d", p=128),
                          xs0[:, :].unsqueeze(1).to_broadcast([128, SPARE, ROW])).then_inc(spared, 16)
            for k in range(2):
                act.dma_start(w1[0:HD, k, :].rearrange("p (e f) -> p e f", e=NEX),
                              io["L0_ffn_W1"][:, k * HD:(k + 1) * HD, :].rearrange("e p f -> p e f")).then_inc(wl, 16)
            act.dma_start(w1[HD:HD + 1, 1, :], io["L0_ffn_b1"].rearrange("e f -> (e f)").unsqueeze(0)).then_inc(wl, 16)
            for k in range(FC):
                act.dma_start(w2[:, k, :].rearrange("p (e d) -> p e d", e=NEX),
                              io["L0_ffn_W2"][:, k * 128:(k + 1) * 128, :].rearrange("e p d -> p e d")).then_inc(wl, 16)
            act.dma_start(b2[:, :], io["L0_ffn_b2"].rearrange("e d -> (e d)").partition_broadcast(128)).then_inc(wl, 16)

            def residual(g, q):
                act.wait_ge(y_in[q], 32 * (g + 1))
                hold(act, tick)
                for k in range(2):
                    t = 2 * (PG * g + q) + k
                    a = act.activation(hb[q][:, k, :], hb[q][:, k, :], ACT.Identity,
                                       scale=s1[:, bass.ds(t, 1)], bias=s2[:, bass.ds(t, 1)])
                a.then_inc(hb_ok, 1)

            def take(p, j):
                act.wait_ge(tz, p + 1)
                act.wait_ge(lg_ok, p + 1)
                act.activation(zt[j][:].rearrange("d a k c -> d (a k) c"), pz[j][:], ACT.Copy).then_inc(zt_ok, 1)

            def root_of(g, n):
                act.wait_ge(var_ok, g + 1)
                act.activation(sd[:, 0:n], sd[:, 0:n], ACT.Sqrt).then_inc(root, 1)

            def exp_of(g, n):
                act.wait_ge(d_ok, g + 1)
                act.activation(ex[:, 0:n, :], dl[:, 0:n, :], ACT.Exp).then_inc(ex_ok, 1)

            def body(g, par, first):
                for q in range(PG):
                    residual(g, q)
                    if not (first and q == 0):
                        take(PG * g + q - 1, (q - 1) % 2)
                    if not first and q == 0:
                        root_of(g - 1, TG)
                    if not first and q == 2:
                        exp_of(g - 1, TG)

            act.sem_inc(lg_ok, 2)
            act.wait_ge(sc_ok, 1)
            groups(act, body)
            residual(NFULL, 0)
            take(NP - 2, 1)
            root_of(NFULL - 1, TG)
            take(NP - 1, 0)
            exp_of(NFULL - 1, TG)
            root_of(NFULL, 2)
            exp_of(NFULL, 2)
            act.wait_ge(spared, 16)

        @block.tensor
        def _(pe):
            ident, ones = keep["ident"], keep["ones"]

            def project(p, g, q):
                pe.wait_ge(y_in[q], 32 * (g + 1))
                pe.wait_ge(h_done, p + 3)
                for i in range(2):
                    for k in range(NBLK):
                        rows = EB + (k == NBLK - 1)
                        m = pe.matmul(po[q % 2][:, i, 0:D], yt[q][0:rows, k, 1 - i, :], keep["wo"][0:rows, k, :],
                                      start=(k == 0), stop=(k == NBLK - 1))
                m.then_inc(out_ok, 1)

            def turn(p, par, q):
                pe.wait_ge(h_done, p + 5)
                pe.wait_ge(zt_ok, p + 1)
                for i in range(2):
                    for k in range(2):
                        t = pe.transpose(pz[q % 2][:, 2 * i + k, :], row[par][:, 2 * q + i, k * HD:(k + 1) * HD], ident[:])
                t.then_inc(tz, 1)

            def logits(p, g, par, q):
                pe.wait_ge(zt_ok, p + 3)
                pe.wait_ge(l_taken, g + 1)
                for i in range(2):
                    for k in range(2):
                        m = pe.matmul(pl[par][:, 2 * q + i, :], zt[q % 2][:, i, k, :], ws[:, k, :],
                                      start=(k == 0), stop=(k == 1))
                m.then_inc(lg_ok, 1)

            def rank(g, n):
                pe.wait_ge(oh_ok, g + 1)
                pe.wait_ge(rows_ok, g + 1)
                pe.matmul(pr[:, 0:NEX * n], bm[:], oh[:, 0:NEX * n], start=True, stop=False)
                pe.matmul(pr[:, 0:NEX * n], ones[:], incb[:, 0:NEX * n], start=False, stop=True).then_inc(rank_ok, 1)

            def body(g, par, first):
                for q in range(PG):
                    p = PG * g + q
                    project(p, g, q)
                    if q:
                        turn(p - 1, par, q - 1)
                    elif not first:
                        turn(p - 1, 1 - par, PG - 1)
                    if q > 1:
                        logits(p - 2, g, par, q - 2)
                    elif not first:
                        logits(p - 2, g - 1, 1 - par, PG - 2 + q)
                    if q == 2 and not first:
                        rank(g - 1, TG)

            pe.wait_ge(iot, PG + 5)
            pe.wait_ge(w_in, 48)
            for k in range(2):
                m = pe.matmul(pc[0:HD, :], ones[0:HD, 0:HD], ws[:, k, :], start=(k == 0), stop=(k == 1))
            m.then_inc(wsum, 1)
            pe.sem_inc(zt_ok, 2)
            pe.sem_inc(l_taken, 2)
            pe.wait_ge(tab_ok, 1)
            groups(pe, body)
            project(NP - 1, NFULL, 0)
            turn(NP - 2, 1, PG - 1)
            logits(NP - 3, NFULL - 1, 1, PG - 2)
            turn(NP - 1, 0, 0)
            logits(NP - 2, NFULL - 1, 1, PG - 1)
            logits(NP - 1, NFULL, 0, 0)
            rank(NFULL - 1, TG)
            rank(NFULL, 2)
            pe.wait_ge(cnt_in, 1)
            pe.matmul(pc[:, :], ones[:], base[:], start=True, stop=True).then_inc(cnt_ok, 1)

        @block.vector
        def _(dve):
            tt, ts, stt = dve.tensor_tensor, dve.tensor_scalar, dve.scalar_tensor_tensor
            done = [0]

            def link(ins):
                done[0] += 1
                ins.then_inc(fstep, 1)
                dve.wait_ge(fstep, done[0])

            ts(s1[:], rs[:], 1.0, None, ALU.add)
            stt(out=s2[:], in0=mu[:], scalar=-1.0, in1=rs[:], op0=ALU.mult, op1=ALU.mult).then_inc(sc_ok, 1)
            dve.wait_ge(iot, PG + 5)
            dve.memset(mask8[:], 1.0)
            dve.memset(mask2[:], 1.0)
            dve.memset(pad[:], 0.0)
            dve.memset(base[:], 0.0)
            tt(bm[:], keep["before"][:], keep["ones"][:], ALU.subtract)
            link(ts(pint[:, 0:1], pid[:], NCHUNK - 1, None, ALU.bitwise_and))
            dve.memset(mask8[:, :, 0], 0.0)
            dve.memset(mask2[:, :, 0], 0.0)
            link(ts(pint[:, 1:2], pid[:], 2, None, ALU.arith_shift_right))
            ts(pcol[:, 0:1], pint[:, 0:1], float(NCHUNK - 1), None, ALU.is_equal)
            link(ts(pcol[:, 1:2], pint[:, 1:2], float(L - LP), None, ALU.mult))
            link(ts(pad[:, Q - HALO:Q], pcol[:, 0:1].to_broadcast([CB, HALO]), float(FAR), None, ALU.mult))
            link(ts(orow[:], orf[:], pcol[:, 1:2], None, ALU.add))
            dve.wait_ge(wsum, 1)
            link(stt(out=ws[:], in0=pc[0:HD, :].unsqueeze(1).to_broadcast([HD, 2, NEX]), scalar=-1.0 / D, in1=ws[:],
                     op0=ALU.mult, op1=ALU.add))
            dve.sem_inc(tab_ok, 1)

            def finish(g, par, q):
                p = PG * g + q
                dve.wait_ge(hb_ok, p + 1)
                dve.wait_ge(out_ok, p + 1)
                if q == 0:
                    dve.wait_ge(row_free, g + 1)
                tt(row[par][:, 2 * q:2 * q + 2, 0:D], hb[q][:], po[q % 2][:, :, 0:D], ALU.add).then_inc(h_done, 1)

            def stats(g, par, q):
                dve.wait_ge(h_done, PG * g + q + 5)
                for i in range(2):
                    b = dve.bn_stats(st[par][:, 2 * q + i, :], row[par][:, 2 * q + i, 0:D])
                return b

            class Chain:
                def __init__(self):
                    self.n = 0

                def __call__(self, g, ins):
                    self.n += 1
                    ins.then_inc(step, 1)
                    dve.wait_ge(step, g * LINKS + self.n)

            def route1(g, par, n, last, c):
                c(g, last)
                s = st[par]
                tt(sm[:, 0:n], s[:, 0:n, 1], s[:, 0:n, 4], ALU.add)
                tt(df[:, 0:n], s[:, 0:n, 1], s[:, 0:n, 4], ALU.subtract)
                c(g, tt(vs[:, 0:n], s[:, 0:n, 2], s[:, 0:n, 5], ALU.add))
                ts(row[par][:, 0:n, D], sm[:, 0:n], 0.5, None, ALU.mult)
                tt(df[:, 0:n], df[:, 0:n], df[:, 0:n], ALU.mult)
                c(g, ts(vs[:, 0:n], vs[:, 0:n], 1.0 / D, EPS, ALU.mult, ALU.add))
                stt(out=sd[:, 0:n], in0=df[:, 0:n], scalar=0.25, in1=vs[:, 0:n], op0=ALU.mult, op1=ALU.add
                    ).then_inc(var_ok, 1)

            def route2(g, par, n, t0, mask, c):
                def bc(a):
                    return a.unsqueeze(2).to_broadcast([CB, n, NEX])

                def em(a):
                    return a[:, 0:NEX * n].rearrange("c (e t) -> c e t", e=NEX)

                dve.wait_ge(root, g + 1)
                c(g, dve.reciprocal(sd[:, 0:n], sd[:, 0:n]))
                dve.tensor_copy(row[par][:, 0:n, D + 1], sd[:, 0:n])
                dve.wait_ge(lg_ok, PG * g + n // 2 + 2)
                tt(lo[:, 0:n, :], pl[par][:, 0:n, :], bc(sd[:, 0:n]), ALU.mult).then_inc(l_taken, 1)
                dve.wait_ge(l_taken, g + 3)
                c(g, tt(lo[:, 0:n, :], lo[:, 0:n, :], bs[:, :].unsqueeze(1).to_broadcast([CB, n, NEX]), ALU.add))
                c(g, dve.tensor_reduce(mx[:, 0:n], lo[:, 0:n, :], AX.X, ALU.max))
                tt(dl[:, 0:n, :], lo[:, 0:n, :], bc(mx[:, 0:n]), ALU.subtract).then_inc(d_ok, 1)
                dve.wait_ge(d_ok, g + 1)
                c(g, stt(out=scr[:, 0:n, :], in0=dl[:, 0:n, :], scalar=0.0,
                         in1=w8[:, :].unsqueeze(1).to_broadcast([CB, n, NEX]), op0=ALU.is_ge, op1=ALU.mult))
                c(g, dve.tensor_reduce(mx[:, 0:n], scr[:, 0:n, :], AX.X, ALU.max))
                c(g, tt(mx[:, 0:n], mx[:, 0:n], pad[:, bass.ds(t0, n)], ALU.add))
                c(g, tt(em(oh), scr[:, 0:n, :].rearrange("c t e -> c e t"),
                        mx[:, 0:n].unsqueeze(1).to_broadcast([CB, NEX, n]), ALU.is_equal))
                c(g, dve.tensor_tensor_scan(inc[:, 0:NEX * n], mask[:].rearrange("c e t -> c (e t)"),
                                            oh[:, 0:NEX * n], 0.0, ALU.mult, ALU.add))
                c(g, tt(em(incb), em(inc), base[:, :].unsqueeze(2).to_broadcast([CB, NEX, n]), ALU.add))
                dve.tensor_copy(base[:], em(incb)[:, :, n - 1]).then_inc(oh_ok, 1)

            def route3(g, par, n, t0, c):
                def em(a):
                    return a[:, 0:NEX * n].rearrange("c (e t) -> c e t", e=NEX)

                dve.wait_ge(rank_ok, g + 1)
                c(g, tt(em(rk), em(pr), ecap[:, :].unsqueeze(2).to_broadcast([CB, NEX, n]), ALU.add))
                c(g, tt(rk[:, 0:NEX * n], rk[:, 0:NEX * n], oh[:, 0:NEX * n], ALU.mult))
                dve.wait_ge(ex_ok, g + 1)
                dve.tensor_reduce(slf[:, 0:n], em(rk).rearrange("c e t -> c t e"), AX.X, ALU.add)
                c(g, dve.tensor_reduce(ssum[:, 0:n], ex[:, 0:n, :], AX.X, ALU.add))
                tt(sli[par][:, 0:n], slf[:, 0:n], pad[:, bass.ds(t0, n)], ALU.add)
                c(g, dve.reciprocal(ssum[:, 0:n], ssum[:, 0:n]))
                dve.tensor_copy(row[par][:, 0:n, D + 3].bitcast(I32), orow[:, bass.ds(t0, n)])
                dve.tensor_copy(row[par][:, 0:n, D + 2], ssum[:, 0:n]).then_inc(rows_ok, 1)
                assert c.n == LINKS

            LINKS = 16

            def body(g, par, first):
                c = Chain()
                finish(g, par, 0)
                if not first:
                    route1(g - 1, 1 - par, TG, stats(g - 1, 1 - par, PG - 1), c)
                finish(g, par, 1)
                stats(g, par, 0)
                if not first:
                    route2(g - 1, 1 - par, TG, TG * (g - 1), mask8, c)
                finish(g, par, 2)
                stats(g, par, 1)
                if not first:
                    route3(g - 1, 1 - par, TG, TG * (g - 1), c)
                finish(g, par, 3)
                stats(g, par, 2)

            dve.sem_inc(rows_ok, 1)
            groups(dve, body)
            finish(NFULL, 0, 0)
            c = Chain()
            route1(NFULL - 1, 1, TG, stats(NFULL - 1, 1, PG - 1), c)
            route2(NFULL - 1, 1, TG, TG * (NFULL - 1), mask8, c)
            route3(NFULL - 1, 1, TG, TG * (NFULL - 1), c)
            c = Chain()
            route1(NFULL, 0, 2, stats(NFULL, 0, 0), c)
            route2(NFULL, 0, 2, TG * NFULL, mask2, c)
            route3(NFULL, 0, 2, TG * NFULL, c)
            dve.wait_ge(rows_ok, NFULL + 2)
            dve.sem_inc(cnt_in, 1)
            dve.wait_ge(cnt_ok, 1)
            ts(tint[:], pc[:, :], 127.0, None, ALU.add)
            link(tt(ef[:], pc[:, :], ecap[:], ALU.add))
            dve.tensor_copy(pcol[:, 2:3], pid[:])
            link(ts(tint[:], tint[:], 7, None, ALU.arith_shift_right))
            dve.tensor_copy(tiles[:], tint[:])
            link(ts(ei[:], ef[:], pcol[:, 2:3], None, ALU.add))
            dve.sem_inc(tail_ok, 1)
            link(dve.tensor_tensor_scan(tend[:], keep["ones"][:, 0:NEX], tiles[:], 0.0, ALU.mult, ALU.add))
            ends = tend[0:1, :].unsqueeze(1).to_broadcast([1, NTILE, NEX])
            link(tt(cmp_[:], tie[:, :].unsqueeze(2).to_broadcast([1, NTILE, NEX]), ends, ALU.is_ge))
            link(dve.tensor_reduce(tsum[:], cmp_[:], AX.X, ALU.add))
            link(tt(cmp_[:], cmp_[:], ends, ALU.mult))
            link(dve.tensor_reduce(tst[:], cmp_[:], AX.X, ALU.max))
            ts(late["te"][:], tsum[:], float(NEX - 1), None, ALU.min)
            link(tt(tst[:], tie[:], tst[:], ALU.subtract))
            link(ts(tsum[:], tsum[:], float(CAP), None, ALU.mult))
            link(stt(out=late["tb"][:], in0=tst[:], scalar=128.0, in1=tsum[:], op0=ALU.mult, op1=ALU.add))


def experts(nc, io, dr, keep, late, out):
    with ExitStack() as ctx:
        def sb(name, shape, dt=F32):
            return ctx.enter_context(nc.sbuf_tensor(name, shape, dt))

        def sem(name):
            return ctx.enter_context(nc.semaphore(name))

        w1, w2, b2, te = late["w1"], late["w2"], late["b2"], late["te"]
        xr = [sb(f"xr{j}", [128, ROW]) for j in range(NB)]
        z = [sb(f"z7{j}", [128, D]) for j in range(NB)]
        zt = [sb(f"zt7{j}", [HD + 1, 2, 128]) for j in range(NB)]
        wc = [sb(f"wc{j}", [HD + 1, 2, FF]) for j in range(NB)]
        ht = [sb(f"ht7{j}", [128, FC, 128]) for j in range(NB)]
        ob = [sb(f"ob{j}", [128, D]) for j in range(NB)]
        yb = [sb(f"yb{j}", [128, D]) for j in range(NB)]
        oi = [sb(f"oi{j}", [128, 1], I32) for j in range(NB)]
        pz = bank(nc, ctx, "pz7", [HD, 2, 128])
        ph = [bank(nc, ctx, f"ph7{k}", [128, 3, 128]) for k in range(2)]
        py = bank(nc, ctx, "py7", [128, D])
        x_in = [sem(f"x7_in{j}") for j in range(NB)]
        z_ok = sem("z7_ok")
        turned = sem("t7")
        zt_ok = sem("zt7_ok")
        hid = sem("hid7")
        act_ok = sem("act7")
        wc_ok = sem("wc_ok")
        y_ok = sem("y7_ok")
        y_b = sem("y7_b")
        o_ok = sem("o7_ok")
        sent = keep["outputs_sent"]
        iot = sem("iot7")
        tick = keep["tick"]
        tickp = keep["tick_p"]
        tick_d = keep["tick_d"]
        tick_s = keep["tick_s"]
        block = ctx.enter_context(nc.Block())
        N = NTILE
        HEAD = NB + 1
        assert (N - HEAD - 1) % NB == 0

        def steps(eng, body):
            for i in range(HEAD):
                body(i, i % NB, i // NB)
            with eng.Fori(0, (N - HEAD - 1) // NB) as p:
                for j in range(HEAD, HEAD + NB):
                    body(NB * p + j, j % NB, p + j // NB)
            body(N - 1, (N - 1) % NB, (N - 1) // NB)

        @block.sync
        def _(sp):
            def load(i, j, use):
                first = sp.value_load(late["tb"][0:1, bass.ds(i, 1)], min_val=0, max_val=XROWS - 128)
                sp.wait_ge(o_ok, i + 1)
                hold(sp, tick_s)
                sp.dma_start(xr[j][:], dr["xs"][bass.ds(first, 128), :]).then_inc(x_in[j], 16)

            sp.sem_inc(o_ok, 3)
            steps(sp, load)

        @block.gpsimd
        def _(pool):
            for j in range(NB):
                pool.memset(zt[j][HD:HD + 1, :, :], 1.0).then_inc(iot, 1)
            bound = pool.to_reg(B * L - 1)

            def send(i, j, use):
                pool.wait_ge(o_ok, i + 4)
                hold(pool, tickp)
                pool.indirect_dma_start(out, bass.IndirectOffsetOnAxis(ap=oi[j][:, 0:1], axis=0), ob[j][:], None,
                                        bounds_check=bound, oob_is_err=False).then_inc(sent[j], 16)

            steps(pool, send)
            for j in range(NB):
                pool.wait_ge(sent[j], 16 * len(range(j, N, NB)))

        @block.scalar
        def _(act):
            def take(i, j):
                act.wait_ge(turned, i + 3)
                act.wait_ge(hid, 2 * i + 2)
                act.activation(zt[j][0:HD, :, :], pz[:], ACT.Copy).then_inc(zt_ok, 1)

            def body(i, j, use):
                act.wait_ge(y_ok, i + 1)
                for k in range(2):
                    act.wait_ge(hid, 2 * i + k + 5)
                    act.activation(ht[j][:, 3 * k:3 * k + 3, :], ph[k][:], ACT.Gelu).then_inc(act_ok, 1)
                if not isinstance(i, int) or i < N - 1:
                    take(i + 1, (j + 1) % NB)

            act.wait_ge(iot, 3)
            act.activation(ht[0][:, 0, 0:1], keep["ident"][:, 0:1], ACT.Gelu)
            act.sem_inc(hid, 4)
            take(0, 0)
            steps(act, body)

        @block.vector
        def _(dve):
            def normal(i, j, use):
                dve.wait_ge(x_in[j], 16 * (use + 1))
                dve.wait_ge(turned, i + 1)
                dve.tensor_scalar(z[j][:], xr[j][:, 0:D], xr[j][:, D:D + 1], xr[j][:, D + 1:D + 2],
                                  ALU.subtract, ALU.mult).then_inc(z_ok, 1)

            def finish(i, j, use):
                ex = dve.value_load(te[0:1, bass.ds(i, 1)], min_val=0, max_val=NEX - 1)
                dve.wait_ge(y_ok, i + 3)
                dve.tensor_tensor(yb[j][:], py[:], b2[:, bass.ds(ex * D, D)], ALU.add).then_inc(y_b, 1)
                if not isinstance(use, int) or use > 0:
                    dve.wait_ge(sent[j], 16 * use)
                dve.tensor_copy(oi[j][:], xr[j][:, ROW - 1:ROW].bitcast(I32))
                dve.wait_ge(y_b, i + 2)
                dve.scalar_tensor_tensor(out=ob[j][:], in0=yb[j][:], scalar=xr[j][:, D + 2:D + 3], in1=xr[j][:, 0:D],
                                         op0=ALU.mult, op1=ALU.add).then_inc(o_ok, 1)

            def stage_weights(i, j):
                ex = dve.value_load(te[0:1, bass.ds(i, 1)], min_val=0, max_val=NEX - 1)
                dve.wait_ge(hid, 2 * i + 2)
                hold(dve, tick_d)
                dve.tensor_copy(wc[j][0:HD, 0, :], w1[0:HD, 0, bass.ds(ex * FF, FF)])
                dve.tensor_copy(wc[j][:, 1, :], w1[:, 1, bass.ds(ex * FF, FF)]).then_inc(wc_ok, 1)

            def body(i, j, use):
                if not isinstance(i, int) or i < N - 1:
                    normal(i + 1, (j + 1) % NB, use + (j + 1) // NB)
                    stage_weights(i + 1, (j + 1) % NB)
                if not isinstance(i, int) or i > 0:
                    finish(i - 1, (j - 1) % NB, use - (1 if j == 0 else 0))

            dve.sem_inc(y_ok, 2)
            dve.sem_inc(y_b, 1)
            dve.wait_ge(keep["wl"], WLOADS)
            normal(0, 0, 0)
            stage_weights(0, 0)
            steps(dve, body)
            finish(N - 1, (N - 1) % NB, (N - 1) // NB)

        @block.tensor
        def _(pe):
            ident = keep["ident"]

            def turn(i, j):
                pe.wait_ge(z_ok, i + 1)
                pe.wait_ge(zt_ok, i + 1)
                for k in range(2):
                    t = pe.transpose(pz[:, k, :], z[j][:, k * HD:(k + 1) * HD], ident[:])
                t.then_inc(turned, 1)

            def second(i, j):
                ex = pe.value_load(te[0:1, bass.ds(i, 1)], min_val=0, max_val=NEX - 1)
                pe.wait_ge(act_ok, 2 * i + 4)
                pe.wait_ge(y_b, i + 1)
                for k in range(FC):
                    m = pe.matmul(py[:], ht[j][:, k, :], w2[:, k, bass.ds(ex * D, D)], start=(k == 0),
                                  stop=(k == FC - 1))
                m.then_inc(y_ok, 1)

            def body(i, j, use):
                pe.wait_ge(zt_ok, i + 2)
                pe.wait_ge(wc_ok, i + 1)
                for k in range(2):
                    pe.wait_ge(act_ok, 2 * i + k + 1)
                    for c in range(3):
                        f = (3 * k + c) * 128
                        for d in range(2):
                            m = pe.matmul(ph[k][:, c, :], wc[j][0:HD + d, d, f:f + 128], zt[j][0:HD + d, d, :],
                                          start=(d == 0), stop=(d == 1))
                    m.then_inc(hid, 1)
                if not isinstance(i, int) or i > 0:
                    second(i - 1, (j - 1) % NB)
                if not isinstance(i, int) or i < N - 1:
                    turn(i + 1, (j + 1) % NB)

            pe.sem_inc(zt_ok, 1)
            pe.sem_inc(turned, 2)
            pe.sem_inc(act_ok, 2)
            pe.wait_ge(keep["wl"], WLOADS)
            turn(0, 0)
            steps(pe, body)
            second(N - 1, (N - 1) % NB)


WLOADS = 16 * (2 + 1 + FC + 1)


def build(nc, io, out):
    def dram(name, shape):
        return nc.dram_tensor(name, shape, F32).ap()

    dr = {"h0": dram("h0", (B * LP, D)), "xs": dram("xs", (XROWS, ROW)), "var_tab": dram("var_tab", (NVAR, 70)),
          "kd": dram("kd", (E, KREV)), "lamd": dram("lamd", (E * NS,)), "c2d": dram("c2d", (E * NS,)),
          "yd": dram("yd", (E, Q * CB))}
    with ExitStack() as ctx:
        def sb(name, shape, dt=F32):
            return ctx.enter_context(nc.sbuf_tensor(name, shape, dt))

        keep = {"ident": sb("ident", [128, 128]), "before": sb("before", [128, 128]), "ones": sb("ones", [128, 128]),
                "wi": sb("wi", [HD + 1, 2, E]), "wo": sb("wo", [EB + 1, NBLK, D]),
                "mu": sb("mu", [CB, Q]), "rs": sb("rs", [CB, Q]),
                "lamc": sb("lamc", [128, NBLK * NG]), "c2c": sb("c2c", [128, NBLK * NG]),
                "texp": sb("texp", [128, Q]), "sexp": sb("sexp", [96, 2]), "own": sb("own", [128, GE]),
                "wl": ctx.enter_context(nc.semaphore("expert_weights_in")),
                "tick": ctx.enter_context(nc.semaphore("tick")), "tick_s": ctx.enter_context(nc.semaphore("tick_s")),
                "tick_p": ctx.enter_context(nc.semaphore("tick_p")), "tick_d": ctx.enter_context(nc.semaphore("tick_d")),
                "gathered": ctx.enter_context(nc.semaphore("gathered")),
                "scattered": ctx.enter_context(nc.semaphore("scattered")),
                "outputs_sent": [ctx.enter_context(nc.semaphore(f"outputs_sent{j}")) for j in range(NB)]}
        with ExitStack() as early:
            def esb(name, shape, dt=F32):
                return early.enter_context(nc.sbuf_tensor(name, shape, dt))

            keep |= {"shift": esb("shift", [128, 128]), "tk": esb("tk", [128, B * 6]), "vr": esb("vr", [128, B * 70]),
                     "tid": esb("tid", [128, B], I32), "vid": esb("vid", [128, B], I32)}
            embed_images(nc, io, dr, keep)
            embed_text(nc, io, dr, keep)
        with nc.sbuf_tensor("xn", [HD + 1, 2, B, HALO + LP], F32) as xn:
            normalise_in(nc, io, dr, keep, xn)
            mix(nc, io, dr, keep, xn)
        late = {"w1": sb("w1e", [HD + 1, 2, NEX * FF]), "w2": sb("w2e", [128, FC, NEX * D]),
                "b2": sb("b2e", [128, NEX * D]), "te": sb("te", [1, NTILE], I32),
                "tb": sb("tb", [1, NTILE], I32)}
        project_route(nc, io, dr, keep, late)
        experts(nc, io, dr, keep, late, out)


_TOK = ["token_has_int", "token_signed_norm", "token_log_norm", "token_is_zero", "token_is_pow2", "token_is_one"]


def kernel(**inputs):
    import numpy as _np
    import concourse.bacc as _bacc
    from concourse import mybir as _mybir
    from concourse.bass_utils import run_bass_kernel_spmd as _run

    nc = _bacc.Bacc("TRN2", target_bir_lowering=False, num_devices=1)
    named = {k: _np.asarray(v) for k, v in inputs.items() if k[7:] not in _TOK}
    named["tok_tab"] = _np.stack([_np.asarray(inputs["L0_txt_" + k]) for k in _TOK], axis=1)
    arrays, io = {}, {}
    for name, a in named.items():
        a = _np.ascontiguousarray(a).reshape(a.shape or (1,))
        arrays[f"in_{name}"] = a
        io[name] = nc.dram_tensor(f"in_{name}", a.shape, _mybir.dt.from_np(a.dtype), kind="ExternalInput").ap()
    out = nc.dram_tensor("out_dram", (B * L, D), F32, kind="ExternalOutput").ap()
    build(nc, io, out)
    r = _run(nc, [arrays], core_ids=[0])
    return r.results[0]["out_dram"].reshape(B, L, D)
```

```python
from contextlib import ExitStack

import concourse.bass as bass
from concourse import mybir

F32 = mybir.dt.float32
I32 = mybir.dt.int32
ALU = mybir.AluOpType
ACT = mybir.ActivationFunctionType
AX = mybir.AxisListType

B = 32
D = 192
HD = D // 2
IMG, PATCH, CH = 224, 16, 3
GRID = IMG // PATCH
NIMG = GRID * GRID
TXT = 128
L = 1 + NIMG + TXT
NCHUNK, Q = 4, 82
LP = NCHUNK * Q
CB = B * NCHUNK
E = 384
NS = 16
TAPS = 4
HALO = TAPS - 1
W = Q + HALO
EB = 96
NBLK = E // EB
KO = E // 128
GE = 8
NG = EB // GE
GPW = Q + NS
KREV = 180
NEX, FF = 8, 768
FC = FF // 128
V = 50257
NVAR = 1024
NF = 64
FEAT = 85
NTILE = (B * L + NEX * 127) // 128
CAP = (B * L + 128 + 127) // 128 * 128
SPARE = NTILE - (B * L + 127) // 128
XROWS = NEX * CAP + SPARE * 128
ROW = D + 4
FAR = 1 << 20
EPS = 1e-5
HR = D + 6
NB = 4

GB = 8
GP_ROWS = GB * GRID
NGRP = B // GB
PD = PATCH * PATCH * CH
KC = PD // 128



def bank(nc, ctx, name, shape):
    t = ctx.enter_context(nc.psum_tensor(name, [128, 512], F32))
    n = 1
    for s in shape[1:]:
        n *= s
    v = t[0:shape[0], 0:n]
    if len(shape) == 3:
        v = v.rearrange("p (a b) -> p a b", a=shape[1])
    return v


def embed_images(nc, io, dr, keep):
    with ExitStack() as ctx:
        def sb(name, shape, dt=F32):
            return ctx.enter_context(nc.sbuf_tensor(name, shape, dt))

        def sem(name):
            return ctx.enter_context(nc.semaphore(name))

        R = GP_ROWS
        xg = [sb(f"xg{j}", [R, CH * PATCH, IMG]) for j in range(2)]
        xc = [sb(f"xc{j}", [R, CH * PATCH, PATCH]) for j in range(2)]
        xt = [sb(f"xt{j}", [128, KC, R]) for j in range(2)]
        wp = sb("wp", [128, KC, D])
        g1 = sb("g1", [128, KC])
        b1 = sb("b1", [128, KC])
        b1w = sb("b1w", [128, KC, R])
        wg = sb("wg", [128, KC, D])
        bias1 = sb("bias1", [R, D])
        g2 = sb("g2", [R, D])
        b2 = sb("b2", [R, D])
        pos = sb("pos", [R, GRID, D])
        NY = 3
        yg = [sb(f"yg{j}", [R, GRID, HR]) for j in range(NY)]
        st = sb("st1", [R, GRID, 2, 6])
        mx = [sb(f"mx1{j}", [R, GRID]) for j in range(2)]
        ve = [sb(f"ve1{j}", [R, GRID]) for j in range(2)]
        dev = sb("dev1", [R, GRID, 4])
        d2 = sb("d21", [R, GRID])
        m2 = sb("m21", [R, GRID])
        rs = [sb(f"rs1{j}", [R, GRID]) for j in range(2)]
        nb = [sb(f"nb1{j}", [R, GRID]) for j in range(2)]
        sty = sb("sty", [R, GRID, 6])
        muy = sb("muy", [R, GRID])
        dfy = sb("dfy", [R, GRID])
        vey = sb("vey", [R, GRID])
        rsy = sb("rsy", [R, GRID])
        cls = sb("cls", [B, 2, D])
        cls_row = sb("cls_row", [B, HR])
        zrow = sb("zrow", [B, HALO * HR])

        ps_t = [[bank(nc, ctx, f"ps_t{j}{k}", [128, 3, R]) for k in range(2)]
                for j in range(2)]
        ps_y = [bank(nc, ctx, f"ps_y{j}", [R, D]) for j in range(2)]
        ps_b = bank(nc, ctx, "ps_b", [R, D])

        x_in = [[sem(f"x_in{j}{n}") for n in range(2)] for j in range(2)]
        w_in = sem("w_in")
        w_ready = sem("w_ready")
        x_std = sem("x_std")
        x_sqrt = sem("x_sqrt")
        x_rstd = sem("x_rstd")
        x_normed = sem("x_normed")
        turned = sem("turned")
        turned_out = sem("turned_out")
        projected = sem("projected")
        y_taken = sem("y_taken")
        bias_mm = sem("bias_mm")
        y_var = sem("y_var")
        y_sqrt = sem("y_sqrt")
        y_mid = sem("y_mid")
        y_scaled = sem("y_scaled")
        row_done = sem("row_done")
        tick = keep["tick"]
        y_out = [sem("y_out_first"), sem("y_out_rest")]
        assert NGRP == NY + 1
        pos_in = sem("pos_in")
        cls_ok = sem("cls_ok")
        step = sem("step1")
        const = sem("const1")
        ids_in = sem("ids_in")
        gath = keep["gathered"]
        tab = sem("tab")
        misc = sem("misc")
        block = ctx.enter_context(nc.Block())

        xv = io["x"].rearrange("b c (h p) w -> b h c p w", p=PATCH)
        wv = io["L0_tok_W_proj"].rearrange("(f c) d -> c f d", c=CH)
        gv = io["L0_tok_ln1_g"].rearrange("(f c) -> c f", c=CH)
        bv = io["L0_tok_ln1_b"].rearrange("(f c) -> c f", c=CH)
        posv = io["L0_tok_pos_embedding"]
        h0 = dr["h0"]
        PIECES = ((0, 8), (8, GRID))
        W_LOADS = 3 * KC + 3

        @block.sync
        def _(sp):
            for g in range(2):
                if g:
                    sp.wait_ge(x_in[0][0], 16 * GB)
                    sp.wait_ge(w_in, 16 * W_LOADS)
                for b in range(GB):
                    sp.dma_start(xg[g][b * GRID:(b + 1) * GRID, :, :].rearrange("r (c p) w -> r c (p w)", c=CH),
                                 xv[g * GB + b].rearrange("h c p w -> h c (p w)")).then_inc(x_in[g % 2][0], 16)
            for g in range(2, NGRP):
                for n, (lo, hi) in enumerate(PIECES):
                    sp.wait_ge(x_normed, GRID * (g - 2) + hi)
                    for b in range(GB):
                        for c in range(CH):
                            sp.dma_start(xg[g % 2][b * GRID:(b + 1) * GRID, c * PATCH:(c + 1) * PATCH,
                                                   lo * PATCH:hi * PATCH],
                                         xv[g * GB + b][:, c, :, lo * PATCH:hi * PATCH]).then_inc(x_in[g % 2][n], 16)
            for g in range(NGRP):
                for lo, hi in ((0, GRID),) if g + 1 < NGRP else ((0, GRID // 2), (GRID // 2, GRID)):
                    sp.wait_ge(row_done, GRID * g + hi)
                    for b in range(GB):
                        row = (g * GB + b) * LP + 1
                        sp.dma_start(h0[row:row + NIMG, :].rearrange("(h w) d -> h (w d)", w=GRID)[:, lo * HR:hi * HR],
                                     yg[g % NY][b * GRID:(b + 1) * GRID, lo:hi, :].rearrange("r w d -> r (w d)")
                                     ).then_inc(y_out[min(g, 1)], 16)
            sp.wait_ge(y_out[0], 16 * GB)
            sp.wait_ge(y_out[1], 16 * GB * NGRP)

        @block.gpsimd
        def _(pool):
            pool.memset(keep["ident"][:], 0.0).then_inc(const, 1)
            pool.memset(keep["before"][:], 1.0).then_inc(const, 1)
            pool.memset(keep["shift"][:], 0.0).then_inc(const, 1)
            pool.memset(keep["ones"][:], 1.0).then_inc(const, 1)
            pool.wait_ge(const, 4)
            pool.affine_select(out=keep["ident"][:], in_=keep["ident"][:], compare_op=ALU.not_equal, fill=1.0,
                               base=0, pattern=[[-1, 128]], channel_multiplier=1).then_inc(const, 1)
            pool.affine_select(out=keep["before"][:], in_=keep["before"][:], compare_op=ALU.is_gt, fill=0.0,
                               base=0, pattern=[[1, 128]], channel_multiplier=-1).then_inc(const, 1)
            pool.affine_select(out=keep["shift"][:], in_=keep["shift"][:], compare_op=ALU.not_equal, fill=1.0,
                               base=-1, pattern=[[1, 128]], channel_multiplier=-1).then_inc(const, 1)
            pool.memset(zrow[:], 0.0).then_inc(misc, 1)
            pool.wait_ge(ids_in, 32)
            for b in range(B):
                pool.indirect_dma_start(keep["tk"][:, b * 6:(b + 1) * 6], None, io["tok_tab"],
                                        bass.IndirectOffsetOnAxis(ap=keep["tid"][:, b:b + 1], axis=0)
                                        ).then_inc(gath, 16)
            pool.wait_ge(tab, 16 * 7)
            for b in range(B):
                pool.indirect_dma_start(keep["vr"][:, b * 70:(b + 1) * 70], None, dr["var_tab"],
                                        bass.IndirectOffsetOnAxis(ap=keep["vid"][:, b:b + 1], axis=0)
                                        ).then_inc(gath, 16)
            pool.wait_ge(gath, 16 * 2 * B)

        @block.scalar
        def _(act):
            for k in range(KC):
                c, p0 = k // 2, (k % 2) * 128
                act.dma_start(wp[:, k, :], wv[c, p0:p0 + 128, :]).then_inc(w_in, 16)
            for tile, name in ((bias1, "L0_tok_b_proj"), (g2, "L0_tok_ln2_g"), (b2, "L0_tok_ln2_b")):
                act.dma_start(tile[:], io[name].partition_broadcast(R)).then_inc(w_in, 16)
            with nc.allow_non_contiguous_dma(reason="per-feature vectors of a few values"):
                for k in range(KC):
                    c, p0 = k // 2, (k % 2) * 128
                    act.dma_start(g1[:, k:k + 1], gv[c, p0:p0 + 128].unsqueeze(1)).then_inc(w_in, 16)
                    act.dma_start(b1[:, k:k + 1], bv[c, p0:p0 + 128].unsqueeze(1)).then_inc(w_in, 16)
                act.dma_start(keep["tid"][:], io["x_txt"].rearrange("b s -> s b")).then_inc(ids_in, 16)
                act.dma_start(keep["vid"][:], io["itok_BS_0_4095"].rearrange("b s -> s b")).then_inc(ids_in, 16)
                vt = dr["var_tab"]
                act.dma_start(vt[:, 0:NF], io["L0_txt_var_family_onehot"]).then_inc(tab, 16)
                for n, name in enumerate(["var_outer_norm", "var_inner_norm", "var_has_outer", "var_has_inner"]):
                    act.dma_start(vt[:, NF + n:NF + n + 1], io["L0_txt_" + name].unsqueeze(1)).then_inc(tab, 16)
                for n, name in enumerate(["var_family_id", "var_group_id"]):
                    act.dma_start(vt[:, NF + 4 + n:NF + 5 + n].bitcast(I32), io["L0_txt_" + name].unsqueeze(1)
                                  ).then_inc(tab, 16)
            act.wait_ge(misc, 1)
            act.dma_start(h0.rearrange("(b t) d -> b t d", t=LP)[:, L:LP, :].rearrange("b t d -> b (t d)"),
                          zrow[:]).then_inc(misc, 16)

            def root(g):
                act.wait_ge(x_std, g + 1)
                act.activation(rs[g % 2][:], ve[g % 2][:], ACT.Sqrt).then_inc(x_sqrt, 1)

            def normalise(g, w, j):
                act.activation(xc[j][:], xg[g % 2][:, :, bass.ds(w * PATCH, PATCH)], ACT.Identity,
                               bias=nb[g % 2][:, bass.ds(w, 1)], scale=rs[g % 2][:, bass.ds(w, 1)]
                               ).then_inc(x_normed, 1)

            def take(i, j):
                act.wait_ge(turned, i + 1)
                act.wait_ge(projected, i + 1)
                act.copy(xt[j][:, 0:3, :], ps_t[j][0][:])
                act.copy(xt[j][:, 3:6, :], ps_t[j][1][:]).then_inc(turned_out, 1)

            act.sem_inc(projected, 2)
            def root_y(g):
                act.wait_ge(y_var, g + 1)
                act.activation(rsy[:], vey[:], ACT.Sqrt).then_inc(y_sqrt, 1)

            def steps(g, lo, hi):
                with act.Fori(lo, hi) as p:
                    for j in range(2):
                        take(g * GRID + 2 * p + j, j)
                        normalise(g, 2 * p + 2 + j, j)

            root(0)
            act.wait_ge(x_rstd, 1)
            normalise(0, 0, 0)
            normalise(0, 1, 1)
            for b in range(GB):
                act.dma_start(pos[b * GRID:(b + 1) * GRID, :, :].rearrange("r w d -> r (w d)"),
                              posv[0, 1:1 + NIMG, :].rearrange("(h w) d -> h (w d)", w=GRID)).then_inc(pos_in, 16)
            act.dma_start(cls[:, 0, :], posv[0, 0, :].partition_broadcast(B)).then_inc(pos_in, 16)
            act.dma_start(cls[:, 1, :], io["L0_tok_cls_token"][0, 0, :].partition_broadcast(B)).then_inc(pos_in, 16)
            for g in range(NGRP):
                steps(g, 0, EARLY)
                if g:
                    root_y(g - 1)
                steps(g, EARLY, GRID // 2 - 1)
                for j in range(2):
                    take(g * GRID + GRID - 2 + j, j)
                    if g + 1 < NGRP:
                        if j == 0:
                            root(g + 1)
                            act.wait_ge(x_rstd, g + 2)
                        normalise(g + 1, j, j)
            root_y(NGRP - 1)
            act.wait_ge(misc, 1 + 16)
            act.wait_ge(cls_ok, 1)
            act.dma_start(h0.rearrange("(b t) d -> b t d", t=LP)[:, 0, :], cls_row[:]).then_inc(misc, 16)
            act.wait_ge(misc, 1 + 32)

        @block.tensor
        def _(pe):
            def turn(i, j):
                pe.wait_ge(x_normed, i + 1)
                pe.wait_ge(turned_out, i + 1)
                flat = xc[j][:, :, :].rearrange("r a q -> r (a q)")
                for k in range(KC):
                    t = pe.transpose(ps_t[j][k // 3][:, k % 3, :], flat[:, k * 128:(k + 1) * 128],
                                     keep["ident"][0:R, 0:R])
                t.then_inc(turned, 1)

            def project(i, j):
                pe.wait_ge(turned_out, i + 3)
                pe.wait_ge(y_taken, i + 1)
                for k in range(KC):
                    m = pe.matmul(ps_y[j][:], xt[j][:, k, :], wg[:, k, :], start=(k == 0), stop=(k == KC - 1))
                m.then_inc(projected, 1)

            pe.sem_inc(turned_out, 2)
            pe.sem_inc(y_taken, 2)
            pe.wait_ge(const, 7)
            turn(0, 0)
            pe.wait_ge(w_ready, 1)
            for k in range(KC):
                m = pe.matmul(ps_b[:], b1w[:, k, :], wp[:, k, :], start=(k == 0), stop=(k == KC - 1))
            m.then_inc(bias_mm, 1)
            n = NGRP * GRID
            with pe.Fori(0, n // 2 - 1) as p:
                for j in range(2):
                    turn(2 * p + 1 + j, 1 - j)
                    project(2 * p + j, j)
            turn(n - 1, 1)
            project(n - 2, 0)
            project(n - 1, 1)

        @block.vector
        def _(dve):
            done = [0]

            def link(ins):
                done[0] += 1
                ins.then_inc(step, 1)
                dve.wait_ge(step, done[0])

            def x_arrived(g, n):
                loads = sum(((n == 0) if i < 2 else CH) * GB for i in range(g % 2, g + 1, 2))
                dve.wait_ge(x_in[g % 2][n], 16 * loads)

            def x_stats(g, w):
                half = CH * PATCH // 2
                for k in range(2):
                    dve.bn_stats(st[:, bass.ds(w, 1), k, :].rearrange("r a b -> r (a b)"),
                                 xg[g % 2][:, k * half:(k + 1) * half, bass.ds(w * PATCH, PATCH)])

            def x_moments(g):
                q = st[:, :, :, :].rearrange("r w k (h s) -> r w (k h) s", h=2)
                if g >= 2:
                    dve.wait_ge(x_normed, GRID * (g - 1))
                link(dve.memset(d2[:], 0.0))
                dve.tensor_reduce(m2[:], q[:, :, :, 2], AX.X, ALU.add)
                link(dve.tensor_reduce(mx[g % 2][:], q[:, :, :, 1], AX.X, ALU.add))
                link(dve.tensor_scalar(mx[g % 2][:], mx[g % 2][:], 0.25, None, ALU.mult))
                link(dve.tensor_tensor(dev[:], q[:, :, :, 1], mx[g % 2][:, :].unsqueeze(2).to_broadcast([R, GRID, 4]),
                                       ALU.subtract))
                link(dve.tensor_tensor(dev[:], dev[:], dev[:], ALU.mult))
                dve.tensor_scalar(m2[:], m2[:], 1.0 / PD, EPS, ALU.mult, ALU.add)
                link(dve.tensor_reduce(d2[:], dev[:], AX.X, ALU.add))
                dve.scalar_tensor_tensor(out=ve[g % 2][:], in0=d2[:], scalar=0.25, in1=m2[:], op0=ALU.mult,
                                         op1=ALU.add).then_inc(x_std, 1)

            def x_scales(g):
                dve.wait_ge(x_sqrt, g + 1)
                link(dve.reciprocal(rs[g % 2][:], rs[g % 2][:]))
                dve.scalar_tensor_tensor(out=nb[g % 2][:], in0=mx[g % 2][:], scalar=-1.0, in1=rs[g % 2][:],
                                         op0=ALU.mult, op1=ALU.mult).then_inc(x_rstd, 1)

            def y_moments(g):
                link(dve.memset(dfy[:], 0.0))
                dve.tensor_tensor(muy[:], sty[:, :, 1], sty[:, :, 4], ALU.add)
                dve.tensor_tensor(vey[:], sty[:, :, 2], sty[:, :, 5], ALU.add)
                link(dve.tensor_tensor(dfy[:], sty[:, :, 1], sty[:, :, 4], ALU.subtract))
                dve.tensor_scalar(muy[:], muy[:], 0.5, None, ALU.mult)
                dve.tensor_scalar(vey[:], vey[:], 1.0 / D, EPS, ALU.mult, ALU.add)
                link(dve.tensor_tensor(dfy[:], dfy[:], dfy[:], ALU.mult))
                dve.scalar_tensor_tensor(out=vey[:], in0=dfy[:], scalar=0.25, in1=vey[:], op0=ALU.mult, op1=ALU.add
                                         ).then_inc(y_var, 1)

            def col(t, w):
                return t[:, bass.ds(w, 1), :].rearrange("r a d -> r (a d)")

            def y_col(g, w):
                return yg[g % NY][:, bass.ds(w, 1), 0:D].rearrange("r a d -> r (a d)")

            def y_take(g, w, j):
                i = g * GRID + w
                dve.wait_ge(projected, i + 3)
                dve.tensor_tensor(y_col(g, w), ps_y[j][:], bias1[:], ALU.add).then_inc(y_taken, 1)

            def y_stat(g, w):
                dve.wait_ge(y_taken, g * GRID + w + 3)
                hold(dve, tick)
                dve.bn_stats(col(sty, w), y_col(g, w))

            def scale_mul(g, w, n):
                for a in range(n):
                    r = y_col(g, w + a)
                    dve.scalar_tensor_tensor(out=r, in0=r, scalar=muy[:, bass.ds(w + a, 1)], in1=g2[:],
                                             op0=ALU.subtract, op1=ALU.mult).then_inc(y_mid, 1)

            def scale_add(g, w, n):
                for a in range(n):
                    dve.wait_ge(y_mid, g * GRID + w + a + 1)
                    r = y_col(g, w + a)
                    dve.scalar_tensor_tensor(out=r, in0=r, scalar=rsy[:, bass.ds(w + a, 1)], in1=col(pos, w + a),
                                             op0=ALU.mult, op1=ALU.add).then_inc(y_scaled, 1)

            def scale_stats(g, w, n):
                dve.wait_ge(y_scaled, g * GRID + w + n)
                hold(dve, tick)
                for a in range(n):
                    dve.bn_stats(yg[g % NY][:, bass.ds(w + a, 1), D:HR].rearrange("r a d -> r (a d)"),
                                 y_col(g, w + a)).then_inc(row_done, 1)

            def steps(g, lo, hi, more=False, scale=0, w0=0):
                with dve.Fori(lo, hi) as p:
                    w = scale * p + (w0 - scale * lo)
                    for j in range(2):
                        y_take(g, 2 * p + j, j)
                        if more:
                            x_stats(g + 1, 2 * p + GRID - 2 * LATE + j)
                        if scale:
                            (scale_mul, scale_add)[j](g - 1, w, scale)
                        y_stat(g, 2 * p + j)
                    if scale:
                        scale_stats(g - 1, w, scale)

            x_arrived(0, 0)
            with dve.Fori(0, GRID // 7) as i:
                for a in range(7):
                    x_stats(0, 7 * i + a)
            x_moments(0)
            x_scales(0)
            dve.wait_ge(w_in, 16 * W_LOADS)
            for k in range(KC):
                dve.tensor_scalar(wg[:, k, :], wp[:, k, :], g1[:, k:k + 1], None, ALU.mult)
                dve.tensor_copy(b1w[:, k, :], b1[:, k:k + 1].to_broadcast([128, R]))
            link(dve.memset(muy[:], 0.0))
            dve.sem_inc(w_ready, 1)
            dve.wait_ge(bias_mm, 1)
            link(dve.tensor_tensor(bias1[:], bias1[:], ps_b[:], ALU.add))
            for g in range(NGRP):
                more = g + 1 < NGRP
                if g >= NY:
                    dve.wait_ge(y_out[g - NY], 16 * GB)
                extra = GRID - 2 * LATE
                if more:
                    x_arrived(g + 1, 0)
                for n in range(2):
                    if g and n == EARLY:
                        dve.wait_ge(y_sqrt, g)
                        link(dve.reciprocal(rsy[:], rsy[:]))
                    steps(g, n, n + 1, more, 2 if g and n >= EARLY else 0, 2 * (n - EARLY))
                    if more:
                        for w in range(n * extra // 2, (n + 1) * extra // 2):
                            x_stats(g + 1, w)
                    if not g:
                        dve.wait_ge(pos_in, 16 * (GB + 2))
                        part = pos[:, n * GRID // 2:(n + 1) * GRID // 2, :]
                        link(dve.tensor_tensor(part, part, b2[:, :].unsqueeze(1).to_broadcast([R, GRID // 2, D]), ALU.add))
                if more and g:
                    x_arrived(g + 1, 1)
                if not g:
                    link(dve.tensor_tensor(cls_row[:, 0:D], cls[:, 0, :], cls[:, 1, :], ALU.add))
                    link(dve.bn_stats(cls_row[:, D:HR], cls_row[:, 0:D]))
                    dve.sem_inc(cls_ok, 1)
                steps(g, 2, LATE, more, 2 if g else 0, 2 * (2 - EARLY))
                if more:
                    x_moments(g + 1)
                    x_scales(g + 1)
                steps(g, LATE, GRID // 2, False, 3 if g else 0, 2 * (LATE - EARLY))
                y_moments(g)
            dve.wait_ge(y_sqrt, NGRP)
            link(dve.reciprocal(rsy[:], rsy[:]))
            for w in (0, GRID // 2):
                for part in (scale_mul, scale_add, scale_stats):
                    part(NGRP - 1, w, GRID // 2)


EARLY, LATE = 1, 5
assert 2 * (LATE - EARLY) + 3 * (GRID // 2 - LATE) == GRID


def embed_text(nc, io, dr, keep):
    with ExitStack() as ctx:
        def sb(name, shape, dt=F32):
            return ctx.enter_context(nc.sbuf_tensor(name, shape, dt))

        def sem(name):
            return ctx.enter_context(nc.semaphore(name))

        tk = keep["tk"][:, :].rearrange("p (b f) -> p b f", f=6)
        vr = keep["vr"][:, :].rearrange("p (b f) -> p b f", f=70)
        vri = keep["vr"][:, :].bitcast(I32).rearrange("p (b f) -> p b f", f=70)
        NU = 4
        HB = B // NU
        NG4 = B // 4
        HN = NG4 // NU
        ft = sb("ft", [128, B, FEAT])
        mo = sb("mo", [128, B, 4 * NF + 2])
        sel = sb("sel", [128, B, 2, NF])
        pk = sb("pk", [128, HB, 4 * NF])
        ps4 = sb("ps4", [128, B, 4])
        pc = sb("pc", [128, B, 2])
        io64 = sb("io64", [128, NF])
        tf = sb("tf", [128, B])
        ff = sb("ff", [128, B, 2])
        va = sb("va", [128, B])
        va2 = sb("va2", [128, B])
        tlv = sb("tlv", [128, B])
        shi = sb("shi", [128, 2, B])
        rc = sb("rc", [128, B])
        posn = sb("posn", [128, 1])
        st = sb("stt", [128, B, 6])
        ve = sb("vet", [128, B])
        mu = sb("mut", [128, B])
        df = sb("dft", [128, B])
        nz = sb("nzt", [128, B])
        xt = [sb(f"xtt{j}", [FEAT, 4, 128]) for j in range(2)]
        ht = [sb(f"htt{j}", [NF + 1, 4, 128]) for j in range(2)]
        ot = [sb(f"ott{j}", [128, 4, HR]) for j in range(4)]
        w1 = sb("w1t", [FEAT, NF])
        w2 = sb("w2t", [NF + 1, D])
        sc = sb("sct", [NF + 1, 1])
        lg = sb("lgt", [FEAT, 1])
        lb = sb("lbt", [FEAT, 1])
        bb = sb("bbt", [NF, 1])
        gam = sb("gam4", [HD, 2])
        win_row = sb("win_row", [128, E // 128, D])
        wout_row = sb("wout_row", [HD, 2, E])
        pp = [bank(nc, ctx, f"pp{j}", [128, 512]) for j in range(2)]
        pt = [bank(nc, ctx, f"pt{j}", [FEAT, 4, 128]) for j in range(2)]
        po = [bank(nc, ctx, f"po{j}", [128, 2, 256]) for j in range(2)]
        ph = [bank(nc, ctx, f"ph{j}", [128, 512]) for j in range(2)]

        w_in = sem("tw_in")
        iot = sem("iot")
        step = sem("step2")
        mo_ready = sem("mo_ready")
        summed = sem("summed")
        sum_taken = sem("sum_taken")
        ft_copied = sem("ft_copied")
        ft_std = sem("ft_std")
        ft_sqrt = sem("ft_sqrt")
        ft_scale = sem("ft_scale")
        ft_ready = sem("ft_ready")
        w2_ready = sem("w2_ready")
        turned = sem("t_turned")
        xt_ready = sem("t_xt")
        hid = sem("t_hid")
        ht_ready = sem("t_ht")
        outp = sem("t_outp")
        taken = sem("t_taken")
        rows_done = sem("t_rows")
        stored = [sem("t_st0"), sem("t_st1")]
        p_in = sem("p_in")
        p_turned = sem("p_turned")
        p_taken = sem("p_taken")
        tables = MixerTables(nc, io, dr, keep, sb, sem)
        block = ctx.enter_context(nc.Block())
        T = "L0_txt_"
        wi, wo = keep["wi"], keep["wo"]

        @block.sync
        def _(sp):
            tables.load(sp)
            sp.dma_start(w1[:], io[T + "W1"]).then_inc(w_in, 16)
            sp.dma_start(w2[0:NF, :], io[T + "W2"]).then_inc(w_in, 16)
            sp.dma_start(w2[NF:NF + 1, :], io[T + "b2"].unsqueeze(0)).then_inc(w_in, 16)
            sp.dma_start(sc[:], io[T + "scale"].partition_broadcast(NF + 1)).then_inc(w_in, 16)
            with nc.allow_non_contiguous_dma(reason="one value per partition"):
                sp.dma_start(lg[:], io[T + "ln_g"].unsqueeze(1)).then_inc(w_in, 16)
                sp.dma_start(lb[:], io[T + "ln_b"].unsqueeze(1)).then_inc(w_in, 16)
                sp.dma_start(bb[:], io[T + "b1"].unsqueeze(1)).then_inc(w_in, 16)
                sp.dma_start(gam[:], io["L0_attn_gamma"].rearrange("(k p) -> p k", p=HD)).then_inc(p_in, 16)
            sp.dma_start(win_row[:, :, :], io["L0_attn_W_in"].rearrange("(k p) d -> p k d", p=128)).then_inc(p_in, 16)
            sp.dma_start(wi[HD:HD + 1, 1, :], io["L0_attn_b_in"].unsqueeze(0)).then_inc(p_in, 16)
            for n in range(2):
                sp.dma_start(wout_row[:, n, :], io["L0_attn_W_out"][n * HD:(n + 1) * HD, :]).then_inc(p_in, 16)
            tables.store(sp)
            hv = dr["h0"].rearrange("(b t) d -> t b d", t=LP)
            for n in range(NG4):
                sp.wait_ge(rows_done, n + 1)
                if n >= 2:
                    sp.wait_ge(stored[n % 2], 16 * (n // 2))
                sp.dma_start(hv[1 + NIMG:L, 4 * n:4 * n + 4, :], ot[n % 4][:]).then_inc(stored[n % 2], 16)
            for j in range(2):
                sp.wait_ge(stored[j], 16 * (NG4 // 2))

        @block.gpsimd
        def _(pool):
            pool.iota(io64[:], pattern=[[1, NF]], base=0, channel_multiplier=0,
                      allow_small_or_imprecise_dtypes=True).then_inc(iot, 1)
            pool.iota(posn[:], pattern=[[0, 1]], base=0, channel_multiplier=1,
                      allow_small_or_imprecise_dtypes=True).then_inc(iot, 1)
            pool.wait_ge(iot, 2)
            for j in range(2):
                pool.memset(ht[j][NF:NF + 1, :, :], 1.0).then_inc(iot, 1)
            pool.wait_ge(iot, 4)
            tables.constants(pool)
            tables.work(pool)

        @block.vector
        def _(dve):
            done = [0]

            def link(ins):
                done[0] += 1
                ins.then_inc(step, 1)
                dve.wait_ge(step, done[0])

            tt, ts = dve.tensor_tensor, dve.tensor_scalar
            dve.wait_ge(iot, 4)
            dve.tensor_copy(shi[:, 0, :], tk[:, :, 2])
            dve.tensor_copy(shi[:, 1, :], tk[:, :, 1]).then_inc(mo_ready, 1)
            ts(ff[:, :, :], vri[:, :, 68:70], 0.0, None, ALU.max)
            ts(va2[:, :], vri[:, :, 69], 0.0, None, ALU.is_gt)
            ts(tf[:, :], keep["tid"][:, :], 2.5, None, ALU.is_gt)
            link(ts(va[:, :], tk[:, :, 0], 0.0, None, ALU.is_gt))
            link(tt(va[:, :], va[:, :], tf[:, :], ALU.mult))
            link(tt(tlv[:, :], tk[:, :, 2], va[:, :], ALU.mult))

            def inputs(u):
                s = slice(u * HB, (u + 1) * HB)

                def bc(ap):
                    return ap.unsqueeze(2).to_broadcast([128, HB, NF])

                cols = io64[:, :].unsqueeze(1).to_broadcast([128, HB, NF])
                tt(sel[:, s, 0, :], vri[:, s, 68:69].to_broadcast([128, HB, NF]), cols, ALU.is_equal)
                link(tt(sel[:, s, 1, :], bc(ff[:, s, 1]), cols, ALU.is_equal))
                tt(mo[:, s, 0:NF], vr[:, s, 0:NF], bc(va[:, s]), ALU.mult)
                link(tt(sel[:, s, 1, :], sel[:, s, 1, :], bc(va2[:, s]), ALU.mult))
                tt(mo[:, s, NF:2 * NF], vr[:, s, 0:NF], bc(tlv[:, s]), ALU.mult)
                tt(mo[:, s, 2 * NF:3 * NF], sel[:, s, 1, :], bc(va[:, s]), ALU.mult)
                tt(mo[:, s, 3 * NF:4 * NF], sel[:, s, 1, :], bc(tlv[:, s]), ALU.mult)
                dve.tensor_copy(mo[:, s, 4 * NF], va[:, s])
                dve.tensor_copy(mo[:, s, 4 * NF + 1], tlv[:, s]).then_inc(mo_ready, 1)

            def sums(u):
                for b in range(u * HB, (u + 1) * HB):
                    dve.wait_ge(summed, b + 2)
                    p = pp[b % 2]
                    tt(pk[:, b % HB, :].rearrange("p (g c f) -> p g c f", g=2, c=2),
                       p[:, 0:4 * NF].rearrange("p (g c f) -> p g c f", g=2, c=2),
                       sel[:, b, :, :].unsqueeze(2).to_broadcast([128, 2, 2, NF]), ALU.mult)
                    dve.tensor_copy(pc[:, b, :], p[:, 4 * NF:4 * NF + 2]).then_inc(sum_taken, 1)
                dve.wait_ge(sum_taken, (u + 1) * HB + 1)

            def features(u):
                s = slice(u * HB, (u + 1) * HB)
                link(dve.tensor_reduce(ps4[:, s, :], pk[:, :, :].rearrange("p b (k f) -> p b k f", f=NF), AX.X,
                                       ALU.add))
                link(ts(rc[:, s], pc[:, s, 0], 1.0, None, ALU.max))
                link(dve.reciprocal(rc[:, s], rc[:, s]))
                inv = 1.0 / (TXT - 1)
                ts(ft[:, s, 74:76], pc[:, s, :], inv, None, ALU.mult)
                ts(ft[:, s, 76:78], ps4[:, s, 0:2], inv, None, ALU.mult)
                tt(ft[:, s, 78], ps4[:, s, 0], rc[:, s], ALU.mult)
                ts(ft[:, s, 79:81], ps4[:, s, 2:4], inv, None, ALU.mult)
                link(tt(ft[:, s, 81], ps4[:, s, 2], rc[:, s], ALU.mult))
                dve.wait_ge(ft_copied, u + 1)
                for b in range(u * HB, (u + 1) * HB):
                    a = dve.bn_stats(st[:, b, :], ft[:, b, :])
                link(a)
                ev, od = (FEAT + 1) // 2, FEAT // 2
                ts(mu[:, s], st[:, s, 1], ev / FEAT, None, ALU.mult)
                tt(ve[:, s], st[:, s, 2], st[:, s, 5], ALU.add)
                link(tt(df[:, s], st[:, s, 1], st[:, s, 4], ALU.subtract))
                dve.scalar_tensor_tensor(out=mu[:, s], in0=st[:, s, 4], scalar=od / FEAT, in1=mu[:, s],
                                         op0=ALU.mult, op1=ALU.add)
                ts(ve[:, s], ve[:, s], 1.0 / FEAT, EPS, ALU.mult, ALU.add)
                link(tt(df[:, s], df[:, s], df[:, s], ALU.mult))
                dve.scalar_tensor_tensor(out=ve[:, s], in0=df[:, s], scalar=ev * od / FEAT ** 2, in1=ve[:, s],
                                         op0=ALU.mult, op1=ALU.add).then_inc(ft_std, 1)

            def row_stats(n):
                dve.wait_ge(taken, 2 * (n + 1))
                for b in range(4):
                    a = dve.bn_stats(ot[n % 4][:, b, D:HR], ot[n % 4][:, b, 0:D])
                a.then_inc(rows_done, 1)

            def scales(u):
                s = slice(u * HB, (u + 1) * HB)
                dve.wait_ge(ft_sqrt, u + 1)
                link(dve.reciprocal(ve[:, s], ve[:, s]))
                dve.scalar_tensor_tensor(out=nz[:, s], in0=mu[:, s], scalar=-1.0, in1=ve[:, s], op0=ALU.mult,
                                         op1=ALU.mult).then_inc(ft_scale, 1)

            inputs(0)
            dve.tensor_copy(ft[:, :, 0:5], tk[:, :, 0:5])
            ts(ft[:, :, 73], posn[:, :].to_broadcast([128, B]), 1.0 / (TXT - 1), None, ALU.mult)
            dve.tensor_copy(ft[:, :, 84], tk[:, :, 5])
            dve.wait_ge(summed, 1)
            dve.tensor_copy(ft[:, :, 82:84].rearrange("p b c -> p c b"),
                            pp[1][:, 0:2 * B].rearrange("p (c b) -> p c b", c=2)).then_inc(sum_taken, 1)
            inputs(1)
            sums(0)
            features(0)
            scales(0)
            inputs(2)
            dve.wait_ge(w_in, 16 * 7)
            ts(w2[:, :], w2[:, :], sc[:, 0:1], None, ALU.mult).then_inc(w2_ready, 1)
            for u in range(1, NU):
                sums(u)
                features(u)
                scales(u)
                if u + 2 < NU:
                    inputs(u + 2)
            for n in range(NG4):
                row_stats(n)

        @block.scalar
        def _(act):
            for u in range(NU):
                s = slice(u * HB, (u + 1) * HB)
                act.activation(ft[:, s, 5:5 + NF + 4], vr[:, s, 0:NF + 4], ACT.Copy).then_inc(ft_copied, 1)
            tables.functions(act)
            act.wait_ge(p_in, 80)
            for k in range(2):
                act.wait_ge(p_turned, k + 1)
                act.activation(wi[0:HD, k, :], ph[k][0:HD, 0:E], ACT.Identity, scale=gam[:, k:k + 1]).then_inc(p_taken, 1)
            for k, n in enumerate((2, KO - 2)):
                act.wait_ge(p_turned, 2 + k + 1)
                act.activation(wo[:, 2 * k:2 * k + n, :].rearrange("p a d -> p (a d)"), ph[k][:, 0:n * D], ACT.Copy
                               ).then_inc(p_taken, 1)

            def root(u):
                act.wait_ge(ft_std, u + 1)
                act.activation(ve[:, u * HB:(u + 1) * HB], ve[:, u * HB:(u + 1) * HB], ACT.Sqrt).then_inc(ft_sqrt, 1)
                act.wait_ge(ft_scale, u + 1)

            def normalise(n):
                for b in range(4 * n, 4 * n + 4):
                    a = act.activation(ft[:, b, :], ft[:, b, :], ACT.Identity, scale=ve[:, b:b + 1], bias=nz[:, b:b + 1])
                a.then_inc(ft_ready, 1)

            act.wait_ge(w_in, 16 * 7)
            act.wait_ge(iot, 4)
            root(0)
            normalise(0)
            for m in range(NG4 + 2):
                if m < NG4:
                    act.wait_ge(turned, m + 1)
                    if m >= 2:
                        act.wait_ge(hid, m - 1)
                    act.activation(xt[m % 2][:, :, :], pt[m % 2][:], ACT.Identity, bias=lb[:, 0:1], scale=lg[:, 0:1]
                                   ).then_inc(xt_ready, 1)
                if 1 <= m <= NG4:
                    n = m - 1
                    act.wait_ge(hid, n + 1)
                    if n >= 2:
                        act.wait_ge(outp, 2 * (n - 1))
                    act.activation(ht[n % 2][0:NF, :, :].rearrange("p a b -> p (a b)"), ph[n % 2][0:NF, :], ACT.Gelu,
                                   bias=bb[:, 0:1]).then_inc(ht_ready, 1)
                if m + 1 < NG4:
                    if (m + 1) % HN == 0:
                        root((m + 1) // HN)
                    normalise(m + 1)
                if m >= 2:
                    n = m - 2
                    if n >= 4:
                        act.wait_ge(stored[n % 2], 16 * (n // 2 - 1))
                    for k in range(2):
                        act.wait_ge(outp, 2 * n + k + 1)
                        act.activation(ot[n % 4][:, 2 * k:2 * k + 2, 0:D], po[k][:, :, 0:D], ACT.Copy).then_inc(taken, 1)

        @block.tensor
        def _(pe):
            ident = keep["ident"]
            pe.wait_ge(mo_ready, 1)
            pe.matmul(pp[1][:, 0:2 * B], keep["shift"][:], shi[:, :, :].rearrange("p c b -> p (c b)"),
                      start=True, stop=True).then_inc(summed, 1)

            def sums(lo, hi):
                for b in range(lo, hi):
                    pe.wait_ge(sum_taken, b if b else 1)
                    pe.matmul(pp[b % 2][:, 0:4 * NF + 2], keep["before"][:], mo[:, b, :], start=True, stop=True
                              ).then_inc(summed, 1)

            def turn(n):
                pe.wait_ge(ft_ready, n + 1)
                if n >= 2:
                    pe.wait_ge(xt_ready, n - 1)
                for k in range(4):
                    t = pe.transpose(pt[n % 2][:, k, :], ft[:, 4 * n + k, :], ident[:])
                t.then_inc(turned, 1)

            pe.wait_ge(mo_ready, 2)
            sums(0, HB)
            pe.wait_ge(p_in, 80)
            for k in range(2):
                for m in range(3):
                    t = pe.transpose(ph[k][0:HD, m * 128:(m + 1) * 128], win_row[:, m, k * HD:(k + 1) * HD], ident[:])
                t.then_inc(p_turned, 1)
            for k in range(2):
                pe.wait_ge(p_taken, k + 1)
                for n in range(2 * (2, KO - 2)[k]):
                    t = pe.transpose(ph[k][:, n * HD:(n + 1) * HD],
                                     wout_row[:, n % 2, (2 * k + n // 2) * 128:(2 * k + n // 2 + 1) * 128],
                                     ident[0:HD, 0:HD])
                t.then_inc(p_turned, 1)
            pe.wait_ge(w_in, 16 * 7)
            for m in range(NG4 + 2):
                u = m // HN + 1
                if m % HN == 0 and u < NU:
                    pe.wait_ge(mo_ready, u + 2)
                    sums(u * HB, u * HB + 2)
                if m < NG4:
                    turn(m)
                if m % HN < HN - 1 and u < NU:
                    sums(u * HB + 2 + m % HN * (HB - 2) // (HN - 1), u * HB + 2 + (m % HN + 1) * (HB - 2) // (HN - 1))
                if 1 <= m <= NG4:
                    n = m - 1
                    pe.wait_ge(xt_ready, n + 1)
                    if n < 2:
                        pe.wait_ge(p_taken, 2 + n + 1)
                    else:
                        pe.wait_ge(ht_ready, n - 1)
                    pe.matmul(ph[n % 2][0:NF, :], w1[:], xt[n % 2][:, :, :].rearrange("p a b -> p (a b)"), start=True,
                              stop=True).then_inc(hid, 1)
                if m >= 2:
                    n = m - 2
                    pe.wait_ge(ht_ready, n + 1)
                    pe.wait_ge(w2_ready, 1)
                    for k in range(2):
                        if n:
                            pe.wait_ge(taken, 2 * (n - 1) + k + 1)
                        for q in range(2):
                            a = pe.matmul(po[k][:, q, 0:D], ht[n % 2][:, 2 * k + q, :], w2[:], start=True, stop=True)
                        a.then_inc(outp, 1)


class MixerTables:

    def __init__(self, nc, io, dr, keep, sb, sem):
        self.nc, self.io, self.dr, self.keep = nc, io, dr, keep
        self.abc = sb("abc", [EB, 3, NBLK, NS])
        self.cw = sb("cw", [EB, NBLK, TAPS])
        self.lam = sb("lam", [EB, NBLK, NS])
        self.c2 = sb("c2", [EB, NBLK, NS])
        self.t1 = sb("t1", [EB, NBLK, NS])
        self.lags = sb("lags", [EB, 3, NBLK, NS])
        self.u3 = sb("u3", [EB, NBLK])
        self.ex = sb("ex", [EB, NBLK, NS, Q])
        self.mex = sb("mex", [EB, Q])
        self.kr = sb("kr", [EB, NBLK, KREV])
        self.arrived = sem("m_in")
        self.sigmoids = sem("m_sg")
        self.consts = sem("m_iot")
        self.step = sem("m_step")
        self.argument = sem("m_arg")
        self.powers = sem("m_exp")
        self.done_k = sem("m_done")
        self.out = sem("m_out")

    def load(self, sp):
        io = self.io
        for n, name in enumerate(["A", "Bp", "C"]):
            sp.dma_start(self.abc[:, n, :, :], io["L0_attn_" + name].rearrange("(k p) n -> p k n", p=EB)
                         ).then_inc(self.arrived, 16)
        sp.dma_start(self.cw[:, :, :], io["L0_attn_conv_w"].rearrange("(k p) n -> p k n", p=EB)).then_inc(self.arrived, 16)

    def store(self, sp):
        dr, keep, out = self.dr, self.keep, self.out
        sp.wait_ge(self.done_k, 1)
        sp.dma_start(dr["kd"].rearrange("(k p) n -> p k n", p=EB), self.kr[:]).then_inc(out, 16)
        sp.dma_start(dr["lamd"].rearrange("(k p n) -> p k n", p=EB, n=NS), self.lam[:]).then_inc(out, 16)
        sp.dma_start(dr["c2d"].rearrange("(k p n) -> p k n", p=EB, n=NS), self.c2[:]).then_inc(out, 16)
        sp.wait_ge(out, 48)
        with self.nc.allow_non_contiguous_dma(reason="one value per partition"):
            sp.dma_start(keep["lamc"][:], dr["lamd"].rearrange("(g p) -> p g", p=128)).then_inc(out, 16)
            sp.dma_start(keep["c2c"][:], dr["c2d"].rearrange("(g p) -> p g", p=128)).then_inc(out, 16)
        sp.wait_ge(out, 80)

    def constants(self, pool):
        keep, iot, mex = self.keep, self.consts, self.mex
        pool.iota(mex[:], pattern=[[-1, Q]], base=Q - 1, channel_multiplier=0,
                  allow_small_or_imprecise_dtypes=True).then_inc(iot, 1)
        pool.iota(keep["texp"][:], pattern=[[-1, Q]], base=Q, channel_multiplier=0,
                  allow_small_or_imprecise_dtypes=True).then_inc(iot, 1)
        pool.iota(keep["sexp"][:, 0:1], pattern=[[0, 1]], base=Q - 1, channel_multiplier=-1,
                  allow_small_or_imprecise_dtypes=True).then_inc(iot, 1)
        pool.memset(keep["sexp"][:, 1:2], 0.0).then_inc(iot, 1)
        pool.wait_ge(iot, 4)
        pool.affine_select(out=keep["sexp"][:, 0:1], in_=keep["sexp"][:, 0:1], compare_op=ALU.is_ge, fill=0.0,
                           base=Q - 1, pattern=[[0, 1]], channel_multiplier=-1).then_inc(iot, 1)
        pool.affine_select(out=keep["sexp"][:, 1:2], in_=keep["sexp"][:, 1:2], compare_op=ALU.is_ge, fill=-1e4,
                           base=Q - 1, pattern=[[0, 1]], channel_multiplier=-1).then_inc(iot, 1)
        own = keep["own"]
        pool.memset(own[:], 1.0).then_inc(iot, 1)
        pool.wait_ge(iot, 7)
        pool.affine_select(out=own[:], in_=own[:], compare_op=ALU.is_ge, fill=0.0, base=0,
                           pattern=[[-NS, GE]], channel_multiplier=1).then_inc(iot, 1)
        pool.wait_ge(iot, 8)
        pool.affine_select(out=own[:], in_=own[:], compare_op=ALU.is_ge, fill=0.0, base=NS - 1,
                           pattern=[[NS, GE]], channel_multiplier=-1).then_inc(iot, 1)
        pool.wait_ge(iot, 9)

    def functions(self, act):
        abc, ex = self.abc, self.ex
        act.wait_ge(self.arrived, 64)
        act.activation(abc[:], abc[:], ACT.Sigmoid).then_inc(self.sigmoids, 1)
        act.wait_ge(self.sigmoids, 1)
        act.activation(self.lam[:], abc[:, 0, :, :], ACT.Ln).then_inc(self.sigmoids, 1)
        act.wait_ge(self.argument, 1)
        act.activation(ex[:], ex[:], ACT.Exp).then_inc(self.powers, 1)

    def work(self, pool):
        abc, cw, lags, t1, c2, kr, ex, u3 = (self.abc, self.cw, self.lags, self.t1, self.c2, self.kr, self.ex, self.u3)
        a = abc[:, 0, :, :]
        done = [0]
        tt = pool.tensor_tensor

        def link(ins):
            done[0] += 1
            ins.then_inc(self.step, 1)
            pool.wait_ge(self.step, done[0])

        def tap(j):
            return cw[:, :, j:j + 1].to_broadcast([EB, NBLK, NS])

        link(pool.memset(kr[:], 0.0))
        pool.wait_ge(self.arrived, 64)
        pool.wait_ge(self.sigmoids, 2)
        tt(ex[:].rearrange("p k n q -> p (k n) q"),
           self.lam[:].rearrange("p k n -> p (k n)").unsqueeze(2).to_broadcast([EB, NBLK * NS, Q]),
           self.mex[:, :].unsqueeze(1).to_broadcast([EB, NBLK * NS, Q]), ALU.mult).then_inc(self.argument, 1)
        link(tt(t1[:], a, tap(3), ALU.mult))
        link(tt(lags[:, 0, :, :], abc[:, 1, :, :], abc[:, 2, :, :], ALU.mult))
        for j in (2, 1):
            link(tt(t1[:], t1[:], tap(j), ALU.add))
            link(tt(t1[:], t1[:], a, ALU.mult))
        link(tt(t1[:], t1[:], tap(0), ALU.add))
        link(tt(c2[:], t1[:], lags[:, 0, :, :], ALU.mult))
        for lag in (1, 2):
            link(tt(lags[:, lag, :, :], lags[:, lag - 1, :, :], a, ALU.mult))
        n = NS // 2
        while n:
            link(tt(lags[:, :, :, 0:n], lags[:, :, :, 0:n], lags[:, :, :, n:2 * n], ALU.add))
            n //= 2
        for lag in range(3):
            col = kr[:, :, HALO + Q - 1 - lag]
            link(tt(col, lags[:, lag, :, 0], cw[:, :, 3], ALU.mult))
            for j in range(1, lag + 1):
                link(tt(u3[:], lags[:, lag - j, :, 0], cw[:, :, 3 - j], ALU.mult))
                link(tt(col, col, u3[:], ALU.add))
        pool.wait_ge(self.powers, 1)
        link(tt(ex[:].rearrange("p k n q -> p (k n) q"), ex[:].rearrange("p k n q -> p (k n) q"),
                c2[:].rearrange("p k n -> p (k n)").unsqueeze(2).to_broadcast([EB, NBLK * NS, Q]), ALU.mult))
        n = NS // 2
        while n > 1:
            link(tt(ex[:, :, 0:n, :], ex[:, :, 0:n, :], ex[:, :, n:2 * n, :], ALU.add))
            n //= 2
        link(tt(kr[:, :, 0:Q], ex[:, :, 0, :], ex[:, :, 1, :], ALU.add))
        pool.sem_inc(self.done_k, 1)


def hold(eng, tick):
    eng.sem_inc(tick, 1)


def normalise_in(nc, io, dr, keep, xn):
    with ExitStack() as ctx:
        def sb(name, shape, dt=F32):
            return ctx.enter_context(nc.sbuf_tensor(name, shape, dt))

        def sem(name):
            return ctx.enter_context(nc.semaphore(name))

        TS = 8
        NS4 = Q // TS
        PARTS4 = ((0, 2), (2, 4), (4, 7), (7, NS4 + 1))
        h = sb("h4", [CB, Q, HR])
        st = h[:, :, D:HR]
        df = sb("df4", [CB, Q])
        vv = sb("vv4", [CB, 2, Q])
        zs = sb("zs4", [CB, Q])
        nz = sb("nz4", [CB, Q])
        z = [[sb(f"z4{j}{k}", [CB, 2, D]) for k in range(2)] for j in range(2)]
        pz = [[bank(nc, ctx, f"pz{j}{k}", [HD, 4, CB]) for k in range(2)] for j in range(2)]
        h_in = [sem(f"h_in{n}") for n in range(len(PARTS4))]
        step = sem("s4")
        var_ok = sem("var4")
        root = sem("root4")
        zs_ok = sem("zs4s")
        ready = [sem("z_ready0"), sem("z_ready1")]
        turned = [sem("z_turned0"), sem("z_turned1")]
        taken = [sem("z_taken0"), sem("z_taken1")]
        ones = sem("ones4")
        tick = keep["tick"]
        tick_d = keep["tick_d"]
        block = ctx.enter_context(nc.Block())
        mu, rs = keep["mu"], keep["rs"]

        def tokens(n):
            lo, hi = PARTS4[n]
            return TS * lo, min(TS * hi, Q)

        def scatter_cols(t):
            full = xn[0:HD, :, :, :]
            return full[:, :, :, HALO:HALO + LP].rearrange("p k b (c t) -> p k b c t", c=NCHUNK)[:, :, :, :, bass.ds(t, 1)]

        def turned_token(j, k, i):
            return pz[j][k][:, 2 * i:2 * i + 2, :].rearrange("p k (b c) -> p k b c", c=NCHUNK).unsqueeze(4)

        def token(t):
            return h[:, bass.ds(t, 1), 0:D].rearrange("p a d -> p (a d)")

        @block.sync
        def _(sp):
            hv = dr["h0"].rearrange("(p t) d -> p t d", t=Q)
            for n in range(len(PARTS4)):
                lo, hi = tokens(n)
                sp.dma_start(h[:, lo:hi, :], hv[:, lo:hi, :]).then_inc(h_in[n], 16)

        @block.gpsimd
        def _(pool):
            pool.memset(xn[0:HD, :, :, 0:HALO], 0.0).then_inc(ones, 1)
            pool.wait_ge(ones, 1)
            pool.memset(xn[HD:HD + 1, 1, :, HALO:], 1.0).then_inc(ones, 1)
            pool.memset(xn[HD:HD + 1, 1, :, 0:HALO], 0.0).then_inc(ones, 1)

        @block.vector
        def _(dve):
            done = [0]
            tt, ts, stt = dve.tensor_tensor, dve.tensor_scalar, dve.scalar_tensor_tensor

            def link(ins):
                done[0] += 1
                ins.then_inc(step, 1)
                dve.wait_ge(step, done[0])

            def moments(n):
                lo, hi = tokens(n)
                link(dve.memset(zs[:, lo:hi], 0.0))
                tt(mu[:, lo:hi], st[:, lo:hi, 1], st[:, lo:hi, 4], ALU.add)
                tt(vv[:, 1, lo:hi], st[:, lo:hi, 2], st[:, lo:hi, 5], ALU.add)
                link(tt(df[:, lo:hi], st[:, lo:hi, 1], st[:, lo:hi, 4], ALU.subtract))
                ts(mu[:, lo:hi], mu[:, lo:hi], 0.5, None, ALU.mult)
                ts(vv[:, 1, lo:hi], vv[:, 1, lo:hi], 1.0 / D, None, ALU.mult)
                link(tt(df[:, lo:hi], df[:, lo:hi], df[:, lo:hi], ALU.mult))
                link(stt(out=vv[:, 1, lo:hi], in0=df[:, lo:hi], scalar=0.25, in1=vv[:, 1, lo:hi], op0=ALU.mult,
                         op1=ALU.add))
                ts(vv[:, 0, lo:hi], vv[:, 1, lo:hi], EPS, None, ALU.add).then_inc(var_ok, 1)

            def scales(n):
                lo, hi = tokens(n)
                s = zs[:, lo:hi]
                dve.wait_ge(root, n + 1)
                link(dve.reciprocal(rs[:, lo:hi], vv[:, 0, lo:hi]))
                link(tt(s, vv[:, 1, lo:hi], rs[:, lo:hi], ALU.mult))
                link(ts(s, s, 1e-6, None, ALU.add))
                link(dve.reciprocal(s, s))
                link(tt(s, s, rs[:, lo:hi], ALU.mult))
                stt(out=nz[:, lo:hi], in0=mu[:, lo:hi], scalar=-1.0, in1=s, op0=ALU.mult, op1=ALU.mult
                    ).then_inc(zs_ok, 1)
                dve.wait_ge(zs_ok, n + 1)

            def take(m, k):
                dve.wait_ge(turned[1], 2 * m + k + 1)
                hold(dve, tick_d)
                for i in range(2):
                    c = dve.tensor_copy(scatter_cols(TS * m + 4 * k + 2 + i), turned_token(1, k, i))
                c.then_inc(taken[1], 1)

            def make(m, k):
                for i in range(2):
                    t = TS * m + 4 * k + 2 + i
                    c = ts(z[1][k][:, i, :], token(t), zs[:, bass.ds(t, 1)], nz[:, bass.ds(t, 1)], ALU.mult, ALU.add)
                c.then_inc(ready[1], 1)

            def statistics(n):
                dve.wait_ge(h_in[n], 16)
                moments(n)

            statistics(0)
            scales(0)
            make(0, 0)
            make(0, 1)
            for n, (lo, hi) in enumerate(PARTS4):
                if n:
                    scales(n)
                more = n + 1 < len(PARTS4)
                if more:
                    statistics(n + 1)
                if hi > 1:
                    with dve.Fori(max(lo, 1), min(hi, NS4)) as m:
                        for k in range(2):
                            take(m - 1, k)
                            make(m, k)
            for k in range(2):
                take(NS4 - 1, k)
            dve.wait_ge(taken[1], 2 * NS4)

        @block.scalar
        def _(act):
            def take(m, k):
                act.wait_ge(turned[0], 2 * m + k + 1)
                hold(act, tick)
                for i in range(2):
                    c = act.activation(scatter_cols(TS * m + 4 * k + i), turned_token(0, k, i), ACT.Copy)
                c.then_inc(taken[0], 1)

            def make(m, k):
                for i in range(2):
                    t = TS * m + 4 * k + i
                    c = act.activation(z[0][k][:, i, :], token(t), ACT.Identity, scale=zs[:, bass.ds(t, 1)],
                                       bias=nz[:, bass.ds(t, 1)])
                c.then_inc(ready[0], 1)

            for n, (lo, hi) in enumerate(PARTS4):
                a, b = tokens(n)
                act.wait_ge(var_ok, n + 1)
                act.activation(vv[:, :, a:b], vv[:, :, a:b], ACT.Sqrt).then_inc(root, 1)
                act.wait_ge(zs_ok, n + 1)
                if not n:
                    make(0, 0)
                    make(0, 1)
                if hi > 1:
                    with act.Fori(max(lo, 1), min(hi, NS4)) as m:
                        for k in range(2):
                            take(m - 1, k)
                            make(m, k)
            take(NS4 - 1, 0)
            make(NS4, 0)
            take(NS4 - 1, 1)
            take(NS4, 0)

        @block.tensor
        def _(pe):
            def turn(m, j, k):
                pe.wait_ge(ready[j], 2 * m + k + 1)
                pe.wait_ge(taken[j], 2 * m + k + 1)
                for i in range(2):
                    for f in range(2):
                        t = pe.transpose(pz[j][k][:, 2 * i + f, :], z[j][k][:, i, f * HD:(f + 1) * HD], keep["ident"][:])
                t.then_inc(turned[j], 1)

            for j in range(2):
                pe.sem_inc(taken[j], 2)
            with pe.Fori(0, NS4) as m:
                for k in range(2):
                    for j in range(2):
                        turn(m, j, k)
            turn(NS4, 0, 0)


XU = CB // 4
IU = EB // 4
TU = [4] * 10 + [3] * 14
UNITS = XU + IU + len(TU)
XHEAD = 8
NYT = 4


def unit_order(last):
    order = [("I", n) for n in range(IU)]
    if last:
        return order + [("T", n) for n in range(len(TU))]
    order += [("X", n) for n in range(XHEAD)]
    for n in range(len(TU)):
        order += [("T", n), ("X", XHEAD + n)]
    assert len(order) == UNITS and XHEAD + len(TU) == XU
    return order


def mix(nc, io, dr, keep, xn):
    with ExitStack() as ctx:
        def sb(name, shape, dt=F32):
            return ctx.enter_context(nc.sbuf_tensor(name, shape, dt))

        def sem(name):
            return ctx.enter_context(nc.semaphore(name))

        x = sb("x5", [W, CB, EB])
        y = sb("y5", [CB, EB, Q])
        gp = [sb(f"gp{j}", [96, GE * GPW + 32]) for j in range(3)]
        lg = [sb(f"lg{j}", [96, GE * NS]) for j in range(3)]
        sm = [sb(f"sm{j}", [CB, GE * NS]) for j in range(2)]
        ht = [sb(f"hs{j}", [128, B, NCHUNK]) for j in range(2)]
        rr = [sb(f"rr{j}", [128, Q]) for j in range(2)]
        bd = [sb(f"bd{j}", [128, GE, Q]) for j in range(2)]
        mc = sb("mc5", [128, NBLK * NG, GE])
        aq = sb("aq5", [128, NBLK * NG])
        yt = [sb(f"yt{j}", [EB, 4, CB]) for j in range(NYT)]
        pa = [bank(nc, ctx, f"pa{j}", [128, 4, 128]) for j in range(4)]
        pst = bank(nc, ctx, "pst", [128, B, NCHUNK])
        pb = [bank(nc, ctx, f"pb{j}", [128, 4, Q]) for j in range(2)]

        setup = sem("set5")
        aq_ok = sem("aq_ok")
        g_in = [sem(f"g_in{j}") for j in range(3)]
        p_ok = sem("p_ok")
        unit = sem("unit")
        free = [sem("free_act"), sem("free_dve")]
        s_ok = [sem("s_ok_act"), sem("s_ok_dve")]
        st_ok = sem("st_ok")
        h_ok = sem("h_ok")
        r_ok = sem("r_ok")
        bd_ok = sem("bd_ok")
        inter = sem("inter")
        added = sem("added")
        step = sem("s5")
        stored = [sem(f"yst{j}") for j in range(NYT)]
        tick = keep["tick"]
        tick_p = keep["tick_p"]
        tick_s = keep["tick_s"]
        tick_d = keep["tick_d"]
        block = ctx.enter_context(nc.Block())
        own, lamc, c2c, texp, sexp = (keep[k] for k in ("own", "lamc", "c2c", "texp", "sexp"))

        def start(k):
            return k * UNITS + XU

        def cols(j, e):
            return gp[j][0:W, e * GPW:e * GPW + 128]

        @block.sync
        def _(sp):
            def load(k, g, done=None):
                j = g % 3
                if done is not None:
                    sp.wait_ge(unit, done)
                    hold(sp, tick_s)
                first = k * EB + g * GE
                src = bass.AP(tensor=dr["kd"].tensor, offset=first * KREV, ap=[[1, 96], [KREV, GE], [1, Q]])
                sp.dma_start(gp[j][:, 0:GE * GPW].rearrange("r (e q) -> r e q", q=GPW)[:, :, 0:Q], src
                             ).then_inc(g_in[j], 16)
                lamsrc = bass.AP(tensor=dr["lamd"].tensor, offset=first * NS, ap=[[0, 96], [1, GE * NS]])
                sp.dma_start(lg[j][:], lamsrc).then_inc(g_in[j], 16)

            def body(k, last):
                for g in range(3, NG):
                    load(k, g, start(k) + 2 * (g - 2))
                if not last:
                    for g in range(3):
                        load(k + 1, g, start(k) + 2 * (NG - 2 + g))
                for m, (kind, n) in enumerate(unit_order(last)):
                    if kind == "T":
                        t0 = sum(TU[:n])
                        sp.wait_ge(free[m % 2], start(k) // 2 + m // 2 + 3)
                        hold(sp, tick_s)
                        sp.dma_start(dr["yd"][bass.ds(k * EB, EB), t0 * CB:(t0 + TU[n]) * CB],
                                     yt[n % NYT][:, 0:TU[n], :].rearrange("e t c -> e (t c)")
                                     ).then_inc(stored[n % NYT], 16)

            for g in range(3):
                load(0, g)
            with sp.Fori(0, NBLK - 1) as k:
                body(k, False)
            body(NBLK - 1, True)
            for j in range(NYT):
                sp.wait_ge(stored[j], 16 * (NBLK * len(TU) // NYT + 1))

        @block.gpsimd
        def _(pool):
            for j in range(3):
                pool.memset(gp[j][:, GE * GPW:], 0.0).then_inc(setup, 1)
            for j in range(2):
                pool.memset(ht[j][:, :, 0], 0.0).then_inc(setup, 1)
            pool.tensor_tensor(mc[:], own[:, :].unsqueeze(1).to_broadcast([128, NBLK * NG, GE]),
                               c2c[:, :].unsqueeze(2).to_broadcast([128, NBLK * NG, GE]), ALU.mult).then_inc(setup, 1)
            pool.wait_ge(setup, 6)
            pool.sem_inc(inter, 4)
            with pool.Fori(0, NBLK) as k:
                for g in range(NG):
                    n = k * NG + g
                    pool.wait_ge(r_ok, n + 1)
                    hold(pool, tick_p)
                    pool.wait_ge(inter, 2 * n + 2)
                    hold(pool, tick_p)
                    pool.tensor_tensor(bd[g % 2][:], rr[g % 2][:, :].unsqueeze(1).to_broadcast([128, GE, Q]),
                                       mc[:, bass.ds(n, 1), :].rearrange("p a e -> p (a e)").unsqueeze(2)
                                       .to_broadcast([128, GE, Q]), ALU.mult).then_inc(bd_ok, 1)

        def read_unit(eng, copy, k, first, m, kind, n):
            who = m % 2
            eng.wait_ge(unit, first + m + 1)
            hold(eng, tick if who == 0 else tick_d)
            p = pa[m % 4]
            if kind == "X":
                copy(x[:, 4 * n:4 * n + 4, :].rearrange("w c e -> w (c e)"),
                     p[0:W, :, :].rearrange("w a b -> w (a b)")[:, 0:4 * EB]).then_inc(free[who], 1)
            elif kind == "I":
                g = n // 2
                eng.wait_ge(st_ok, k * NG + g + 1)
                copy(sm[g % 2][:, (n % 2) * 64:(n % 2) * 64 + 64].rearrange("c (e n) -> c e n", n=NS),
                     p[:, :, Q:GPW]).then_inc(s_ok[who], 1)
                copy(y[:, 4 * n:4 * n + 4, :], p[:, :, 0:Q]).then_inc(free[who], 1)
            else:
                q = n % NYT
                eng.wait_ge(stored[q], 16 * (k * (len(TU) // NYT) + n // NYT + 1))
                hold(eng, tick if who == 0 else tick_d)
                copy(yt[q][:, 0:TU[n], :], p[0:EB, 0:TU[n], :]).then_inc(free[who], 1)

        @block.scalar
        def _(act):
            def copy(out, in_):
                return act.activation(out, in_, ACT.Copy)

            def tables(k, g):
                n = k * NG + g
                j = g % 2
                v = g % 3
                act.wait_ge(g_in[v], 32 * (k * (NG // 3) + g // 3 + 1))
                hold(act, tick)
                act.activation(gp[v][:, 0:GE * GPW].rearrange("r (e q) -> r e q", q=GPW)[:, :, Q:GPW],
                               lg[v][:, :].rearrange("r (e n) -> r e n", n=NS), ACT.Exp,
                               scale=sexp[:, 0:1], bias=sexp[:, 1:2]).then_inc(p_ok, 1)
                act.wait_ge(bd_ok, n + 1)
                hold(act, tick)
                act.activation(rr[j][:], texp[:, :], ACT.Exp, scale=lamc[:, bass.ds(n, 1)]).then_inc(r_ok, 1)

            act.activation(aq[:], lamc[:], ACT.Exp, scale=float(Q)).then_inc(aq_ok, 1)
            act.sem_inc(bd_ok, 2)
            act.sem_inc(st_ok, 2)
            for j in range(NYT):
                act.sem_inc(stored[j], 16)
            for m in range(0, XU, 2):
                read_unit(act, copy, 0, 0, m, "X", m)
                if m in (8, 16):
                    tables(0, m // 8 - 1)

            def body(k, last):
                for m, (kind, n) in enumerate(unit_order(last)):
                    if m % 2 == 0:
                        read_unit(act, copy, k, start(k), m, kind, n)
                        if kind == "I" and n // 2 + 2 < NG:
                            tables(k, n // 2 + 2)
                        if not last and kind == "T" and n in (4, 10):
                            tables(k + 1, 0 if n == 4 else 1)

            with act.Fori(0, NBLK - 1) as k:
                body(k, False)
            body(NBLK - 1, True)

        @block.vector
        def _(dve):
            def carry(k, g):
                n = k * NG + g
                j = g % 2
                dve.wait_ge(st_ok, n + 3)
                dve.wait_ge(inter, 2 * n + 2)
                hold(dve, tick)
                dve.tensor_copy(ht[j][:, :, 1], pst[:, :, 0]).then_inc(step, 1)
                for c in range(2, NCHUNK):
                    dve.wait_ge(step, 3 * n + c - 1)
                    ins = dve.scalar_tensor_tensor(out=ht[j][:, :, c], in0=ht[j][:, :, c - 1],
                                                   scalar=aq[:, bass.ds(n, 1)], in1=pst[:, :, c - 1],
                                                   op0=ALU.mult, op1=ALU.add)
                    ins.then_inc(step, 1)
                dve.wait_ge(step, 3 * n + 3)
                hold(dve, h_ok)

            def add(k, g):
                n = k * NG + g
                for q in range(2):
                    dve.wait_ge(inter, 2 * n + q + 5)
                    dve.wait_ge(free[q], k * (UNITS // 2) + XU // 2 + g + 3)
                    hold(dve, tick)
                    e0 = g * GE + 4 * q
                    dve.tensor_tensor(y[:, e0:e0 + 4, :], y[:, e0:e0 + 4, :], pb[q][:], ALU.add).then_inc(added, 1)

            dve.wait_ge(setup, 6)
            dve.wait_ge(aq_ok, 1)
            for m in range(1, XU, 2):
                read_unit(dve, dve.tensor_copy, 0, 0, m, "X", m)

            def body(k, last):
                for m, (kind, n) in enumerate(unit_order(last)):
                    if m % 2 == 0:
                        continue
                    if m == IU + (1 if last else 5):
                        add(k, NG - 2)
                        add(k, NG - 1)
                    read_unit(dve, dve.tensor_copy, k, start(k), m, kind, n)
                    if kind == "I":
                        g = n // 2
                        if g >= 1:
                            carry(k, g - 1)
                        if g >= 2:
                            add(k, g - 2)
                        if g == NG - 1:
                            carry(k, g)

            with dve.Fori(0, NBLK - 1) as k:
                body(k, False)
            body(NBLK - 1, True)

        @block.tensor
        def _(pe):
            ident = keep["ident"]

            def bank(before, m):
                pe.wait_ge(free[m % 2], before // 2 + m // 2 + 1)
                return pa[m % 4]

            def input_unit(k, before, m, n):
                p = bank(before, m)[0:W, :, :].rearrange("w a b -> w (a b)")
                for i in range(4):
                    b, c = divmod(4 * n + i, NCHUNK)
                    for f in range(2):
                        rows = HD + f
                        mm = pe.matmul(p[:, i * EB:(i + 1) * EB], xn[0:rows, f, b, c * Q:c * Q + W],
                                       keep["wi"][0:rows, f, bass.ds(k * EB, EB)],
                                       start=(f == 0), stop=(f == 1))
                mm.then_inc(unit, 1)

            def turn_states(k, g):
                n = k * NG + g
                for who in range(2):
                    pe.wait_ge(s_ok[who], n + 1)
                pe.wait_ge(h_ok, n + 1)
                pe.transpose(pst[:, :, :].rearrange("s b c -> s (b c)"), sm[g % 2][:], ident[:]).then_inc(st_ok, 1)

            def reach(k, g):
                n = k * NG + g
                pe.wait_ge(h_ok, n + 2)
                pe.wait_ge(bd_ok, n + 3)
                for q in range(2):
                    pe.wait_ge(added, 2 * n + q + 1)
                    pe.matmul(pb[q][:].rearrange("c e t -> c (e t)"), ht[g % 2][:].rearrange("s b c -> s (b c)"),
                              bd[g % 2][:, 4 * q:4 * q + 4, :].rearrange("s e t -> s (e t)"),
                              start=True, stop=True).then_inc(inter, 1)

            pe.sem_inc(free[0], 2)
            pe.sem_inc(free[1], 2)
            pe.sem_inc(h_ok, 1)
            pe.sem_inc(added, 2)
            pe.wait_ge(setup, 6)
            for m in range(XU):
                input_unit(0, 0, m, m)

            def body(k, last):
                for who in range(2):
                    pe.wait_ge(free[who], start(k) // 2 + 2)
                for m, (kind, n) in enumerate(unit_order(last)):
                    if m == IU + (0 if last else 4):
                        reach(k, NG - 2)
                        reach(k, NG - 1)
                    if kind == "X":
                        input_unit(k + 1, start(k), m, n)
                    elif kind == "I":
                        g = n // 2
                        if n % 2 == 0:
                            pe.wait_ge(p_ok, k * NG + g + 1)
                        p = bank(start(k), m)
                        for i in range(4):
                            e = 4 * (n % 2) + i
                            mm = pe.matmul(p[:, i, :], x[:, :, g * GE + e], cols(g % 3, e), start=True, stop=True)
                        mm.then_inc(unit, 1)
                        if n % 2:
                            if g >= 1:
                                turn_states(k, g - 1)
                            if g >= 2:
                                reach(k, g - 2)
                            if g == NG - 1:
                                turn_states(k, g)
                    else:
                        if n == 0:
                            pe.wait_ge(added, 2 * (k * NG + NG) + 2)
                        p = bank(start(k), m)
                        for i in range(TU[n]):
                            tr = pe.transpose(p[0:EB, i, :], y[:, :, sum(TU[:n]) + i], ident[:])
                        tr.then_inc(unit, 1)

            with pe.Fori(0, NBLK - 1) as k:
                body(k, False)
            body(NBLK - 1, True)


def project_route(nc, io, dr, keep, late):
    with ExitStack() as ctx:
        def sb(name, shape, dt=F32):
            return ctx.enter_context(nc.sbuf_tensor(name, shape, dt))

        def sem(name):
            return ctx.enter_context(nc.semaphore(name))

        PG = 4
        TG = 2 * PG
        NFULL = Q // TG
        assert NFULL % 3 == 1
        F1, F2 = (NFULL - 1) % 3, NFULL % 3
        NP = Q // 2
        hb = [sb(f"hb{j}", [CB, 2, D]) for j in range(PG)]
        yt = [sb(f"y6{j}", [128, KO, 2, CB]) for j in range(PG)]
        bo = sb("bo", [CB, D])
        row = [sb(f"row{j}", [CB, TG, ROW]) for j in range(3)]
        st = [sb(f"st6{j}", [CB, TG, 6]) for j in range(3)]
        zt = [sb(f"zt6{j}", [HD, 2, 2, CB]) for j in range(2)]
        s1 = sb("s1", [CB, Q])
        s2 = sb("s2", [CB, Q])
        ws = sb("ws", [HD, 2, NEX])
        bs = sb("bs", [CB, NEX])
        sm = sb("sm6", [CB, TG])
        df = sb("df", [CB, TG])
        vs = sb("vs", [CB, TG])
        sd = sb("sd6", [CB, TG])
        lo = sb("lo", [CB, TG, NEX])
        mx = sb("mx", [CB, TG])
        dl = sb("dl", [CB, TG, NEX])
        ex = sb("ex6", [CB, TG, NEX])
        scr = sb("scr", [CB, TG, NEX])
        oh = sb("oh", [CB, NEX * TG])
        inc = sb("inc", [CB, NEX * TG])
        incb = sb("incb", [CB, NEX * TG])
        base = sb("base", [CB, NEX])
        rk = sb("rk", [CB, NEX * TG])
        slf = sb("slf", [CB, TG])
        sli = [sb(f"sli{j}", [CB, TG], I32) for j in range(3)]
        ssum = sb("ssum", [CB, TG])
        w8 = sb("w8", [CB, NEX])
        ecap = sb("ecap", [CB, NEX])
        mask8 = sb("mask8", [CB, NEX, TG])
        mask2 = sb("mask2", [CB, NEX, 2])
        bm = sb("bm", [CB, CB])
        pad = sb("pad", [CB, Q])
        orow = sb("orow", [CB, Q], I32)
        orf = sb("orf", [CB, Q])
        pid = sb("pid", [CB, 1], I32)
        pint = sb("pint", [CB, 2], I32)
        pcol = sb("pcol", [CB, 4])
        xs0 = sb("xs06", [128, ROW])
        tint = sb("tint", [CB, NEX], I32)
        tiles = sb("tiles", [CB, NEX])
        tend = sb("tend", [CB, NEX])
        ei = sb("ei", [CB, NEX], I32)
        ef = sb("ef", [CB, NEX])
        tie = sb("tie", [1, NTILE])
        tsum = sb("tsum", [1, NTILE])
        tst = sb("tst", [1, NTILE])
        cmp_ = sb("cmp", [1, NTILE, NEX])
        po = [bank(nc, ctx, f"p6{j}", [CB, 2, 256]) for j in range(2)]
        pz = [bank(nc, ctx, f"pz6{j}", [HD, 4, CB]) for j in range(2)]
        pl = [bank(nc, ctx, f"pl{j}", [CB, TG, NEX]) for j in range(3)]
        pr = bank(nc, ctx, "pr", [CB, NEX * TG])
        pc = pr[:, 0:NEX]

        y_in = [sem(f"y_in{j}") for j in range(PG)]
        w_in = sem("w6_in")
        iot = sem("iot6")
        xs_z = sem("xs_z")
        sc_ok = sem("sc_ok")
        tab_ok = sem("tab_ok")
        wsum = sem("wsum")
        hb_ok = sem("hb_ok")
        biased = sem("biased")
        out_ok = sem("out_ok")
        h_done = sem("h_done")
        tz = sem("tz")
        zt_ok = sem("zt_ok6")
        lg_ok = sem("lg_ok")
        var_ok = sem("var6")
        root = sem("root6")
        l_taken = sem("l_taken")
        d_ok = sem("d_ok")
        ex_ok = sem("ex_ok")
        oh_ok = sem("oh_ok")
        rank_ok = sem("rank_ok")
        rows_ok = sem("rows_ok")
        row_free = sem("row_free")
        step = sem("s6")
        fstep = sem("f6")
        cnt_in = sem("cnt_in")
        cnt_ok = sem("cnt_ok")
        tail_ok = sem("tail_ok")
        sent = keep["scattered"]
        emptied = sem("emptied")
        spared = sem("spared")
        tick = keep["tick"]
        tick_s = keep["tick_s"]
        tick_p = keep["tick_p"]
        wl = keep["wl"]
        block = ctx.enter_context(nc.Block())
        mu, rs = keep["mu"], keep["rs"]
        w1, w2, b2 = late["w1"], late["w2"], late["b2"]

        def groups(eng, body):
            body(0, 0, True)
            with eng.Fori(0, NFULL // 3) as i:
                for a in range(1, 4):
                    body(3 * i + a, a % 3, False)

        def empty_rows(eng, experts):
            eng.wait_ge(xs_z, 2)
            eng.wait_ge(tail_ok, 1)
            for e in experts:
                first = eng.value_load(ei[0:1, e:e + 1], min_val=0, max_val=XROWS - 128)
                eng.dma_start(dr["xs"][bass.ds(first, 128), :], xs0[:]).then_inc(emptied, 16)

        @block.sync
        def _(sp):
            ydv = dr["yd"].rearrange("(k p) (t c) -> p k t c", p=128, c=CB)
            hv = dr["h0"].rearrange("(p t) d -> p t d", t=Q)
            w1v, w2v = io["L0_ffn_W1"], io["L0_ffn_W2"]

            def load(p, q):
                sp.wait_ge(h_done, p + 1)
                hold(sp, tick_s)
                sp.dma_start(yt[q][:], ydv[:, :, bass.ds(Q - 2 - 2 * p, 2), :]).then_inc(y_in[q], 16)
                sp.dma_start(hb[q][:], hv[:, bass.ds(2 * p, 2), 0:D]).then_inc(y_in[q], 16)

            sp.sem_inc(h_done, 4)
            def expert_weights(e):
                for k in range(2):
                    sp.dma_start(w1[0:HD, k, bass.ds(e * FF, FF)],
                                 w1v[bass.ds(e, 1), k * HD:(k + 1) * HD, :].rearrange("e p f -> (e p) f")
                                 ).then_inc(wl, 16)
                sp.dma_start(w2[:, :, bass.ds(e * D, D)],
                             w2v[bass.ds(e, 1), :, :].rearrange("e (k p) d -> p (e k) d", p=128)).then_inc(wl, 16)

            for q in range(PG):
                load(q, q)
            with sp.Fori(0, NEX) as e:
                for q in range(PG):
                    load(PG * e + PG + q, q)
                expert_weights(e)
            for g in range(NEX + 1, NFULL):
                for q in range(PG):
                    load(PG * g + q, q)
            load(NP - 1, 0)
            empty_rows(sp, range(NEX // 2))
            sp.wait_ge(emptied, 16 * NEX)

        @block.gpsimd
        def _(pool):
            pool.iota(pid[:], pattern=[[0, 1]], base=0, channel_multiplier=1).then_inc(iot, 1)
            fl = dict(allow_small_or_imprecise_dtypes=True)
            pool.iota(orf[:], pattern=[[1, Q]], base=0, channel_multiplier=Q, **fl).then_inc(iot, 1)
            pool.iota(tie[:], pattern=[[1, NTILE]], base=0, channel_multiplier=0, **fl).then_inc(iot, 1)
            pool.iota(w8[:], pattern=[[-1, NEX]], base=NEX, channel_multiplier=0, **fl).then_inc(iot, 1)
            pool.iota(ecap[:], pattern=[[CAP, NEX]], base=0, channel_multiplier=0, **fl).then_inc(iot, 1)
            pool.memset(xs0[:], 0.0).then_inc(xs_z, 1)
            pool.wait_ge(xs_z, 1)
            pool.memset(xs0[:, ROW - 1:ROW].bitcast(I32), FAR).then_inc(xs_z, 1)
            bound = pool.to_reg(NEX * CAP - 1)
            pool.sem_inc(row_free, 3)

            def scatter(g, j, n, reused=True):
                pool.wait_ge(rows_ok, g + 2)
                hold(pool, tick_p)
                for t in range(n):
                    pool.indirect_dma_start(dr["xs"], bass.IndirectOffsetOnAxis(ap=sli[j][:, t:t + 1], axis=0),
                                            row[j][:, t, :], None, bounds_check=bound, oob_is_err=False
                                            ).then_inc(sent, 16)
                if reused:
                    pool.wait_ge(sent, 16 * TG * g + 16 * n)
                    hold(pool, row_free)

            with pool.Fori(0, NFULL // 3) as i:
                for a in range(3):
                    scatter(3 * i + a, a, TG)
            scatter(NFULL - 1, (NFULL - 1) % 3, TG, False)
            scatter(NFULL, NFULL % 3, 2, False)
            pool.wait_ge(sent, 16 * Q)

        @block.scalar
        def _(act):
            act.dma_start(ws[:, 0, :], io["L0_ffn_Ws"][0:HD, :]).then_inc(w_in, 16)
            act.dma_start(ws[:, 1, :], io["L0_ffn_Ws"][HD:D, :]).then_inc(w_in, 16)
            act.dma_start(bs[:], io["L0_ffn_bs"].partition_broadcast(CB)).then_inc(w_in, 16)
            act.dma_start(bo[:], io["L0_attn_b_out"].partition_broadcast(CB)).then_inc(w_in, 16)
            act.wait_ge(xs_z, 2)
            act.dma_start(dr["xs"][NEX * CAP:NEX * CAP + SPARE * 128, :].rearrange("(p n) d -> p n d", p=128),
                          xs0[:, :].unsqueeze(1).to_broadcast([128, SPARE, ROW])).then_inc(spared, 16)
            act.dma_start(w1[HD:HD + 1, 1, :], io["L0_ffn_b1"].rearrange("e f -> (e f)").unsqueeze(0)).then_inc(wl, 16)
            act.dma_start(b2[:, :], io["L0_ffn_b2"].rearrange("e d -> (e d)").partition_broadcast(128)).then_inc(wl, 16)

            def residual(g, q):
                act.wait_ge(y_in[q], 32 * (g + 1))
                hold(act, tick)
                for k in range(2):
                    t = 2 * (PG * g + q) + k
                    a = act.activation(hb[q][:, k, :], hb[q][:, k, :], ACT.Identity,
                                       scale=s1[:, bass.ds(t, 1)], bias=s2[:, bass.ds(t, 1)])
                a.then_inc(hb_ok, 1)

            def take(p, j):
                act.wait_ge(tz, p + 1)
                act.wait_ge(lg_ok, p + 1)
                act.activation(zt[j][:].rearrange("d a k c -> d (a k) c"), pz[j][:], ACT.Copy).then_inc(zt_ok, 1)

            def root_of(g, n):
                act.wait_ge(var_ok, g + 1)
                act.activation(sd[:, 0:n], sd[:, 0:n], ACT.Sqrt).then_inc(root, 1)

            def exp_of(g, n):
                act.wait_ge(d_ok, g + 1)
                act.activation(ex[:, 0:n, :], dl[:, 0:n, :], ACT.Exp).then_inc(ex_ok, 1)

            def body(g, par, first):
                for q in range(PG):
                    residual(g, q)
                    if not (first and q == 0):
                        take(PG * g + q - 1, (q - 1) % 2)
                    if not first and q == 0:
                        root_of(g - 1, TG)
                    if not first and q == 2:
                        exp_of(g - 1, TG)

            act.sem_inc(lg_ok, 2)
            act.wait_ge(sc_ok, 1)
            groups(act, body)
            residual(NFULL, 0)
            take(NP - 2, 1)
            root_of(NFULL - 1, TG)
            take(NP - 1, 0)
            exp_of(NFULL - 1, TG)
            root_of(NFULL, 2)
            exp_of(NFULL, 2)
            empty_rows(act, range(NEX // 2, NEX))
            act.wait_ge(spared, 16)

        @block.tensor
        def _(pe):
            ident, ones = keep["ident"], keep["ones"]

            def project(p, g, q):
                pe.wait_ge(y_in[q], 32 * (g + 1))
                pe.wait_ge(h_done, p + 3)
                for i in range(2):
                    for k in range(KO):
                        m = pe.matmul(po[q % 2][:, i, 0:D], yt[q][:, k, 1 - i, :], keep["wo"][:, k, :],
                                      start=(k == 0), stop=(k == KO - 1))
                m.then_inc(out_ok, 1)

            def turn(p, par, q):
                pe.wait_ge(h_done, p + 5)
                pe.wait_ge(zt_ok, p + 1)
                for i in range(2):
                    for k in range(2):
                        t = pe.transpose(pz[q % 2][:, 2 * i + k, :], row[par][:, 2 * q + i, k * HD:(k + 1) * HD], ident[:])
                t.then_inc(tz, 1)

            def logits(p, g, par, q):
                pe.wait_ge(zt_ok, p + 3)
                pe.wait_ge(l_taken, g + 1)
                for i in range(2):
                    for k in range(2):
                        m = pe.matmul(pl[par][:, 2 * q + i, :], zt[q % 2][:, i, k, :], ws[:, k, :],
                                      start=(k == 0), stop=(k == 1))
                m.then_inc(lg_ok, 1)

            def rank(g, n):
                pe.wait_ge(oh_ok, g + 1)
                pe.wait_ge(rows_ok, g + 1)
                pe.matmul(pr[:, 0:NEX * n], bm[:], oh[:, 0:NEX * n], start=True, stop=False)
                pe.matmul(pr[:, 0:NEX * n], ones[:], incb[:, 0:NEX * n], start=False, stop=True).then_inc(rank_ok, 1)

            def body(g, par, first):
                for q in range(PG):
                    p = PG * g + q
                    project(p, g, q)
                    if q:
                        turn(p - 1, par, q - 1)
                    elif not first:
                        turn(p - 1, (par - 1) % 3, PG - 1)
                    if q > 1:
                        logits(p - 2, g, par, q - 2)
                    elif not first:
                        logits(p - 2, g - 1, (par - 1) % 3, PG - 2 + q)
                    if q == 2 and not first:
                        rank(g - 1, TG)

            pe.wait_ge(iot, 5)
            pe.wait_ge(w_in, 64)
            for k in range(2):
                m = pe.matmul(pc[0:HD, :], ones[0:HD, 0:HD], ws[:, k, :], start=(k == 0), stop=(k == 1))
            m.then_inc(wsum, 1)
            pe.sem_inc(zt_ok, 2)
            pe.sem_inc(l_taken, 3)
            pe.wait_ge(tab_ok, 1)
            groups(pe, body)
            project(NP - 1, NFULL, 0)
            turn(NP - 2, F1, PG - 1)
            logits(NP - 3, NFULL - 1, F1, PG - 2)
            turn(NP - 1, F2, 0)
            logits(NP - 2, NFULL - 1, F1, PG - 1)
            logits(NP - 1, NFULL, F2, 0)
            rank(NFULL - 1, TG)
            rank(NFULL, 2)
            pe.wait_ge(cnt_in, 1)
            pe.matmul(pc[:, :], ones[:], base[:], start=True, stop=True).then_inc(cnt_ok, 1)

        @block.vector
        def _(dve):
            tt, ts, stt = dve.tensor_tensor, dve.tensor_scalar, dve.scalar_tensor_tensor
            done = [0]

            def link(ins):
                done[0] += 1
                ins.then_inc(fstep, 1)
                dve.wait_ge(fstep, done[0])

            ts(s1[:], rs[:], 1.0, None, ALU.add)
            stt(out=s2[:], in0=mu[:], scalar=-1.0, in1=rs[:], op0=ALU.mult, op1=ALU.mult).then_inc(sc_ok, 1)
            dve.wait_ge(iot, 5)
            dve.memset(mask8[:], 1.0)
            dve.memset(mask2[:], 1.0)
            dve.memset(pad[:], 0.0)
            dve.memset(base[:], 0.0)
            tt(bm[:], keep["before"][:], keep["ones"][:], ALU.subtract)
            link(ts(pint[:, 0:1], pid[:], NCHUNK - 1, None, ALU.bitwise_and))
            dve.memset(mask8[:, :, 0], 0.0)
            dve.memset(mask2[:, :, 0], 0.0)
            link(ts(pint[:, 1:2], pid[:], 2, None, ALU.arith_shift_right))
            ts(pcol[:, 0:1], pint[:, 0:1], float(NCHUNK - 1), None, ALU.is_equal)
            link(ts(pcol[:, 1:2], pint[:, 1:2], float(L - LP), None, ALU.mult))
            link(ts(pad[:, Q - HALO:Q], pcol[:, 0:1].to_broadcast([CB, HALO]), float(FAR), None, ALU.mult))
            link(ts(orow[:], orf[:], pcol[:, 1:2], None, ALU.add))
            dve.wait_ge(wsum, 1)
            link(stt(out=ws[:], in0=pc[0:HD, :].unsqueeze(1).to_broadcast([HD, 2, NEX]), scalar=-1.0 / D, in1=ws[:],
                     op0=ALU.mult, op1=ALU.add))
            dve.sem_inc(tab_ok, 1)

            def finish(g, par, q):
                p = PG * g + q
                dve.wait_ge(hb_ok, p + 1)
                tt(hb[q][:], hb[q][:], bo[:, :].unsqueeze(1).to_broadcast([CB, 2, D]), ALU.add).then_inc(biased, 1)
                dve.wait_ge(biased, p + 1)
                dve.wait_ge(out_ok, p + 1)
                if q == 0:
                    dve.wait_ge(row_free, g + 1)
                tt(row[par][:, 2 * q:2 * q + 2, 0:D], hb[q][:], po[q % 2][:, :, 0:D], ALU.add).then_inc(h_done, 1)

            def stats(g, par, q):
                dve.wait_ge(h_done, PG * g + q + 5)
                for i in range(2):
                    b = dve.bn_stats(st[par][:, 2 * q + i, :], row[par][:, 2 * q + i, 0:D])
                return b

            class Chain:
                def __init__(self):
                    self.n = 0

                def __call__(self, g, ins):
                    self.n += 1
                    ins.then_inc(step, 1)
                    dve.wait_ge(step, g * LINKS + self.n)

            def route1(g, par, n, last, c):
                c(g, last)
                s = st[par]
                tt(sm[:, 0:n], s[:, 0:n, 1], s[:, 0:n, 4], ALU.add)
                tt(df[:, 0:n], s[:, 0:n, 1], s[:, 0:n, 4], ALU.subtract)
                c(g, tt(vs[:, 0:n], s[:, 0:n, 2], s[:, 0:n, 5], ALU.add))
                ts(row[par][:, 0:n, D], sm[:, 0:n], 0.5, None, ALU.mult)
                tt(df[:, 0:n], df[:, 0:n], df[:, 0:n], ALU.mult)
                c(g, ts(vs[:, 0:n], vs[:, 0:n], 1.0 / D, EPS, ALU.mult, ALU.add))
                stt(out=sd[:, 0:n], in0=df[:, 0:n], scalar=0.25, in1=vs[:, 0:n], op0=ALU.mult, op1=ALU.add
                    ).then_inc(var_ok, 1)

            def route2(g, par, n, t0, mask, c):
                def bc(a):
                    return a.unsqueeze(2).to_broadcast([CB, n, NEX])

                def em(a):
                    return a[:, 0:NEX * n].rearrange("c (e t) -> c e t", e=NEX)

                dve.wait_ge(root, g + 1)
                c(g, dve.reciprocal(sd[:, 0:n], sd[:, 0:n]))
                dve.tensor_copy(row[par][:, 0:n, D + 1], sd[:, 0:n])
                dve.wait_ge(lg_ok, PG * g + n // 2 + 2)
                tt(lo[:, 0:n, :], pl[par][:, 0:n, :], bc(sd[:, 0:n]), ALU.mult).then_inc(l_taken, 1)
                dve.wait_ge(l_taken, g + 4)
                c(g, tt(lo[:, 0:n, :], lo[:, 0:n, :], bs[:, :].unsqueeze(1).to_broadcast([CB, n, NEX]), ALU.add))
                c(g, dve.tensor_reduce(mx[:, 0:n], lo[:, 0:n, :], AX.X, ALU.max))
                tt(dl[:, 0:n, :], lo[:, 0:n, :], bc(mx[:, 0:n]), ALU.subtract).then_inc(d_ok, 1)
                dve.wait_ge(d_ok, g + 1)
                c(g, stt(out=scr[:, 0:n, :], in0=dl[:, 0:n, :], scalar=0.0,
                         in1=w8[:, :].unsqueeze(1).to_broadcast([CB, n, NEX]), op0=ALU.is_ge, op1=ALU.mult))
                c(g, dve.tensor_reduce(mx[:, 0:n], scr[:, 0:n, :], AX.X, ALU.max))
                c(g, tt(mx[:, 0:n], mx[:, 0:n], pad[:, bass.ds(t0, n)], ALU.add))
                c(g, tt(em(oh), scr[:, 0:n, :].rearrange("c t e -> c e t"),
                        mx[:, 0:n].unsqueeze(1).to_broadcast([CB, NEX, n]), ALU.is_equal))
                c(g, dve.tensor_tensor_scan(inc[:, 0:NEX * n], mask[:].rearrange("c e t -> c (e t)"),
                                            oh[:, 0:NEX * n], 0.0, ALU.mult, ALU.add))
                c(g, tt(em(incb), em(inc), base[:, :].unsqueeze(2).to_broadcast([CB, NEX, n]), ALU.add))
                dve.tensor_copy(base[:], em(incb)[:, :, n - 1]).then_inc(oh_ok, 1)

            def route3(g, par, n, t0, c):
                def em(a):
                    return a[:, 0:NEX * n].rearrange("c (e t) -> c e t", e=NEX)

                dve.wait_ge(rank_ok, g + 1)
                c(g, tt(em(rk), em(pr), ecap[:, :].unsqueeze(2).to_broadcast([CB, NEX, n]), ALU.add))
                c(g, tt(rk[:, 0:NEX * n], rk[:, 0:NEX * n], oh[:, 0:NEX * n], ALU.mult))
                dve.wait_ge(ex_ok, g + 1)
                dve.tensor_reduce(slf[:, 0:n], em(rk).rearrange("c e t -> c t e"), AX.X, ALU.add)
                c(g, dve.tensor_reduce(ssum[:, 0:n], ex[:, 0:n, :], AX.X, ALU.add))
                tt(sli[par][:, 0:n], slf[:, 0:n], pad[:, bass.ds(t0, n)], ALU.add)
                c(g, dve.reciprocal(ssum[:, 0:n], ssum[:, 0:n]))
                dve.tensor_copy(row[par][:, 0:n, D + 3].bitcast(I32), orow[:, bass.ds(t0, n)])
                dve.tensor_copy(row[par][:, 0:n, D + 2], ssum[:, 0:n]).then_inc(rows_ok, 1)
                assert c.n == LINKS

            LINKS = 16

            def body(g, par, first):
                c = Chain()
                finish(g, par, 0)
                if not first:
                    route1(g - 1, (par - 1) % 3, TG, stats(g - 1, (par - 1) % 3, PG - 1), c)
                finish(g, par, 1)
                stats(g, par, 0)
                if not first:
                    route2(g - 1, (par - 1) % 3, TG, TG * (g - 1), mask8, c)
                finish(g, par, 2)
                stats(g, par, 1)
                if not first:
                    route3(g - 1, (par - 1) % 3, TG, TG * (g - 1), c)
                finish(g, par, 3)
                stats(g, par, 2)

            dve.sem_inc(rows_ok, 1)
            groups(dve, body)
            finish(NFULL, F2, 0)
            c = Chain()
            route1(NFULL - 1, F1, TG, stats(NFULL - 1, F1, PG - 1), c)
            route2(NFULL - 1, F1, TG, TG * (NFULL - 1), mask8, c)
            route3(NFULL - 1, F1, TG, TG * (NFULL - 1), c)
            c = Chain()
            route1(NFULL, F2, 2, stats(NFULL, F2, 0), c)
            route2(NFULL, F2, 2, TG * NFULL, mask2, c)
            route3(NFULL, F2, 2, TG * NFULL, c)
            dve.wait_ge(rows_ok, NFULL + 2)
            dve.sem_inc(cnt_in, 1)
            dve.wait_ge(cnt_ok, 1)
            ts(tint[:], pc[:, :], 127.0, None, ALU.add)
            link(tt(ef[:], pc[:, :], ecap[:], ALU.add))
            link(ts(tint[:], tint[:], 7, None, ALU.arith_shift_right))
            dve.tensor_copy(ei[:], ef[:]).then_inc(tail_ok, 1)
            link(dve.tensor_copy(tiles[:], tint[:]))
            link(dve.tensor_tensor_scan(tend[:], keep["ones"][:, 0:NEX], tiles[:], 0.0, ALU.mult, ALU.add))
            ends = tend[0:1, :].unsqueeze(1).to_broadcast([1, NTILE, NEX])
            link(tt(cmp_[:], tie[:, :].unsqueeze(2).to_broadcast([1, NTILE, NEX]), ends, ALU.is_ge))
            link(dve.tensor_reduce(tsum[:], cmp_[:], AX.X, ALU.add))
            link(tt(cmp_[:], cmp_[:], ends, ALU.mult))
            link(dve.tensor_reduce(tst[:], cmp_[:], AX.X, ALU.max))
            ts(late["te"][:], tsum[:], float(NEX - 1), None, ALU.min)
            link(tt(tst[:], tie[:], tst[:], ALU.subtract))
            link(ts(tsum[:], tsum[:], float(CAP), None, ALU.mult))
            link(stt(out=late["tb"][:], in0=tst[:], scalar=128.0, in1=tsum[:], op0=ALU.mult, op1=ALU.add))


def experts(nc, io, dr, keep, late, out):
    with ExitStack() as ctx:
        def sb(name, shape, dt=F32):
            return ctx.enter_context(nc.sbuf_tensor(name, shape, dt))

        def sem(name):
            return ctx.enter_context(nc.semaphore(name))

        w1, w2, b2, te = late["w1"], late["w2"], late["b2"], late["te"]
        xr = [sb(f"xr{j}", [128, ROW]) for j in range(NB)]
        z = [sb(f"z7{j}", [128, D]) for j in range(NB)]
        zt = [sb(f"zt7{j}", [HD + 1, 2, 128]) for j in range(NB)]
        wc = [sb(f"wc{j}", [HD + 1, 2, FF]) for j in range(NB)]
        ht = [sb(f"ht7{j}", [128, FC, 128]) for j in range(NB)]
        ob = [sb(f"ob{j}", [128, D]) for j in range(NB)]
        yb = [sb(f"yb{j}", [128, D]) for j in range(NB)]
        oi = [sb(f"oi{j}", [128, 1], I32) for j in range(NB)]
        pz = bank(nc, ctx, "pz7", [HD, 2, 128])
        ph = [bank(nc, ctx, f"ph7{k}", [128, 3, 128]) for k in range(2)]
        py = bank(nc, ctx, "py7", [128, D])
        x_in = [sem(f"x7_in{j}") for j in range(NB)]
        z_ok = sem("z7_ok")
        turned = sem("t7")
        zt_ok = sem("zt7_ok")
        hid = sem("hid7")
        act_ok = sem("act7")
        wc_ok = sem("wc_ok")
        y_ok = sem("y7_ok")
        y_b = sem("y7_b")
        o_ok = sem("o7_ok")
        sent = keep["outputs_sent"]
        iot = sem("iot7")
        tick = keep["tick"]
        tickp = keep["tick_p"]
        tick_d = keep["tick_d"]
        tick_s = keep["tick_s"]
        block = ctx.enter_context(nc.Block())
        N = NTILE
        HEAD = NB + (N - 1) % NB + NB * ((N - 1) % NB == 0)
        assert (N - HEAD - 1) % NB == 0

        def steps(eng, body):
            for i in range(HEAD):
                body(i, i % NB, i // NB)
            with eng.Fori(0, (N - HEAD - 1) // NB) as p:
                for j in range(HEAD, HEAD + NB):
                    body(NB * p + j, j % NB, p + j // NB)
            body(N - 1, (N - 1) % NB, (N - 1) // NB)

        @block.sync
        def _(sp):
            def load(i, j, use):
                first = sp.value_load(late["tb"][0:1, bass.ds(i, 1)], min_val=0, max_val=XROWS - 128)
                sp.wait_ge(o_ok, i + 1)
                hold(sp, tick_s)
                sp.dma_start(xr[j][:], dr["xs"][bass.ds(first, 128), :]).then_inc(x_in[j], 16)

            sp.sem_inc(o_ok, NB)
            steps(sp, load)

        @block.gpsimd
        def _(pool):
            for j in range(NB):
                pool.memset(zt[j][HD:HD + 1, :, :], 1.0).then_inc(iot, 1)
            bound = pool.to_reg(B * L - 1)

            def send(i, j, use):
                pool.wait_ge(o_ok, i + NB + 1)
                hold(pool, tickp)
                pool.indirect_dma_start(out, bass.IndirectOffsetOnAxis(ap=oi[j][:, 0:1], axis=0), ob[j][:], None,
                                        bounds_check=bound, oob_is_err=False).then_inc(sent[j], 16)

            steps(pool, send)
            for j in range(NB):
                pool.wait_ge(sent[j], 16 * len(range(j, N, NB)))

        @block.scalar
        def _(act):
            def take(i, j):
                act.wait_ge(turned, i + 3)
                act.wait_ge(hid, 2 * i + 2)
                act.activation(zt[j][0:HD, :, :], pz[:], ACT.Copy).then_inc(zt_ok, 1)

            def body(i, j, use):
                act.wait_ge(y_ok, i + 1)
                for k in range(2):
                    act.wait_ge(hid, 2 * i + k + 5)
                    act.activation(ht[j][:, 3 * k:3 * k + 3, :], ph[k][:], ACT.Gelu).then_inc(act_ok, 1)
                if not isinstance(i, int) or i < N - 1:
                    take(i + 1, (j + 1) % NB)

            act.wait_ge(iot, NB)
            act.activation(ht[0][:, 0, 0:1], keep["ident"][:, 0:1], ACT.Gelu)
            act.sem_inc(hid, 4)
            take(0, 0)
            steps(act, body)

        @block.vector
        def _(dve):
            def normal(i, j, use):
                dve.wait_ge(x_in[j], 16 * (use + 1))
                dve.wait_ge(turned, i + 1)
                dve.tensor_scalar(z[j][:], xr[j][:, 0:D], xr[j][:, D:D + 1], xr[j][:, D + 1:D + 2],
                                  ALU.subtract, ALU.mult).then_inc(z_ok, 1)

            def finish(i, j, use):
                ex = dve.value_load(te[0:1, bass.ds(i, 1)], min_val=0, max_val=NEX - 1)
                dve.wait_ge(y_ok, i + 3)
                dve.tensor_tensor(yb[j][:], py[:], b2[:, bass.ds(ex * D, D)], ALU.add).then_inc(y_b, 1)
                if not isinstance(use, int) or use > 0:
                    dve.wait_ge(sent[j], 16 * use)
                dve.tensor_copy(oi[j][:], xr[j][:, ROW - 1:ROW].bitcast(I32))
                dve.wait_ge(y_b, i + 2)
                dve.scalar_tensor_tensor(out=ob[j][:], in0=yb[j][:], scalar=xr[j][:, D + 2:D + 3], in1=xr[j][:, 0:D],
                                         op0=ALU.mult, op1=ALU.add).then_inc(o_ok, 1)

            def stage_weights(i, j):
                ex = dve.value_load(te[0:1, bass.ds(i, 1)], min_val=0, max_val=NEX - 1)
                dve.wait_ge(hid, 2 * i + 2)
                hold(dve, tick_d)
                dve.tensor_copy(wc[j][0:HD, 0, :], w1[0:HD, 0, bass.ds(ex * FF, FF)])
                dve.tensor_copy(wc[j][:, 1, :], w1[:, 1, bass.ds(ex * FF, FF)]).then_inc(wc_ok, 1)

            def body(i, j, use):
                if not isinstance(i, int) or i < N - 1:
                    normal(i + 1, (j + 1) % NB, use + (j + 1) // NB)
                    stage_weights(i + 1, (j + 1) % NB)
                if not isinstance(i, int) or i > 0:
                    finish(i - 1, (j - 1) % NB, use - (1 if j == 0 else 0))

            dve.sem_inc(y_ok, 2)
            dve.sem_inc(y_b, 1)
            dve.wait_ge(keep["wl"], WLOADS)
            normal(0, 0, 0)
            stage_weights(0, 0)
            steps(dve, body)
            finish(N - 1, (N - 1) % NB, (N - 1) // NB)

        @block.tensor
        def _(pe):
            ident = keep["ident"]

            def turn(i, j):
                pe.wait_ge(z_ok, i + 1)
                pe.wait_ge(zt_ok, i + 1)
                for k in range(2):
                    t = pe.transpose(pz[:, k, :], z[j][:, k * HD:(k + 1) * HD], ident[:])
                t.then_inc(turned, 1)

            def second(i, j):
                ex = pe.value_load(te[0:1, bass.ds(i, 1)], min_val=0, max_val=NEX - 1)
                pe.wait_ge(act_ok, 2 * i + 4)
                pe.wait_ge(y_b, i + 1)
                for k in range(FC):
                    m = pe.matmul(py[:], ht[j][:, k, :], w2[:, k, bass.ds(ex * D, D)], start=(k == 0),
                                  stop=(k == FC - 1))
                m.then_inc(y_ok, 1)

            def body(i, j, use):
                pe.wait_ge(zt_ok, i + 2)
                pe.wait_ge(wc_ok, i + 1)
                for k in range(2):
                    pe.wait_ge(act_ok, 2 * i + k + 1)
                    for c in range(3):
                        f = (3 * k + c) * 128
                        for d in range(2):
                            m = pe.matmul(ph[k][:, c, :], wc[j][0:HD + d, d, f:f + 128], zt[j][0:HD + d, d, :],
                                          start=(d == 0), stop=(d == 1))
                    m.then_inc(hid, 1)
                if not isinstance(i, int) or i < N - 1:
                    turn(i + 1, (j + 1) % NB)
                if not isinstance(i, int) or i > 0:
                    second(i - 1, (j - 1) % NB)

            pe.sem_inc(zt_ok, 1)
            pe.sem_inc(turned, 2)
            pe.sem_inc(act_ok, 2)
            pe.wait_ge(keep["wl"], WLOADS)
            turn(0, 0)
            steps(pe, body)
            second(N - 1, (N - 1) % NB)


WLOADS = 16 * (3 * NEX + 2)


def build(nc, io, out):
    def dram(name, shape):
        return nc.dram_tensor(name, shape, F32).ap()

    dr = {"h0": dram("h0", (B * LP, HR)), "xs": dram("xs", (XROWS, ROW)), "var_tab": dram("var_tab", (NVAR, 70)),
          "kd": dram("kd", (E, KREV)), "lamd": dram("lamd", (E * NS,)), "c2d": dram("c2d", (E * NS,)),
          "yd": dram("yd", (E, Q * CB))}
    with ExitStack() as ctx:
        def sb(name, shape, dt=F32):
            return ctx.enter_context(nc.sbuf_tensor(name, shape, dt))

        keep = {"ident": sb("ident", [128, 128]), "before": sb("before", [128, 128]), "ones": sb("ones", [128, 128]),
                "wi": sb("wi", [HD + 1, 2, E]), "wo": sb("wo", [128, KO, D]),
                "mu": sb("mu", [CB, Q]), "rs": sb("rs", [CB, Q]),
                "lamc": sb("lamc", [128, NBLK * NG]), "c2c": sb("c2c", [128, NBLK * NG]),
                "texp": sb("texp", [128, Q]), "sexp": sb("sexp", [96, 2]), "own": sb("own", [128, GE]),
                "wl": ctx.enter_context(nc.semaphore("expert_weights_in")),
                "tick": ctx.enter_context(nc.semaphore("tick")), "tick_s": ctx.enter_context(nc.semaphore("tick_s")),
                "tick_p": ctx.enter_context(nc.semaphore("tick_p")), "tick_d": ctx.enter_context(nc.semaphore("tick_d")),
                "gathered": ctx.enter_context(nc.semaphore("gathered")),
                "scattered": ctx.enter_context(nc.semaphore("scattered")),
                "outputs_sent": [ctx.enter_context(nc.semaphore(f"outputs_sent{j}")) for j in range(NB)]}
        with ExitStack() as early:
            def esb(name, shape, dt=F32):
                return early.enter_context(nc.sbuf_tensor(name, shape, dt))

            keep |= {"shift": esb("shift", [128, 128]), "tk": esb("tk", [128, B * 6]), "vr": esb("vr", [128, B * 70]),
                     "tid": esb("tid", [128, B], I32), "vid": esb("vid", [128, B], I32)}
            embed_images(nc, io, dr, keep)
            embed_text(nc, io, dr, keep)
        with nc.sbuf_tensor("xn", [HD + 1, 2, B, HALO + LP], F32) as xn:
            normalise_in(nc, io, dr, keep, xn)
            mix(nc, io, dr, keep, xn)
        late = {"w1": sb("w1e", [HD + 1, 2, NEX * FF]), "w2": sb("w2e", [128, FC, NEX * D]),
                "b2": sb("b2e", [128, NEX * D]), "te": sb("te", [1, NTILE], I32),
                "tb": sb("tb", [1, NTILE], I32)}
        project_route(nc, io, dr, keep, late)
        experts(nc, io, dr, keep, late, out)


_TOK = ["token_has_int", "token_signed_norm", "token_log_norm", "token_is_zero", "token_is_pow2", "token_is_one"]


def kernel(**inputs):
    import numpy as _np
    import concourse.bacc as _bacc
    from concourse import mybir as _mybir
    from concourse.bass_utils import run_bass_kernel_spmd as _run

    nc = _bacc.Bacc("TRN2", target_bir_lowering=False, num_devices=1)
    named = {k: _np.asarray(v) for k, v in inputs.items() if k[7:] not in _TOK}
    named["tok_tab"] = _np.stack([_np.asarray(inputs["L0_txt_" + k]) for k in _TOK], axis=1)
    arrays, io = {}, {}
    for name, a in named.items():
        a = _np.ascontiguousarray(a).reshape(a.shape or (1,))
        arrays[f"in_{name}"] = a
        io[name] = nc.dram_tensor(f"in_{name}", a.shape, _mybir.dt.from_np(a.dtype), kind="ExternalInput").ap()
    out = nc.dram_tensor("out_dram", (B * L, D), F32, kind="ExternalOutput").ap()
    build(nc, io, out)
    r = _run(nc, [arrays], core_ids=[0])
    return r.results[0]["out_dram"].reshape(B, L, D)
```
